# Optimizing a Trainium2 kernel written in Bass

```python
import numpy as np
import jax
import jax.numpy as jnp

def _softmax(x, axis=-1):
    return jax.nn.softmax(x, axis=axis)

def _gelu(x):
    return jax.nn.gelu(x, approximate=True)

def _silu(x):
    return jax.nn.silu(x)

def _sigmoid(x):
    return jax.nn.sigmoid(x)

def _layernorm(x, axis=-1, eps=1e-05):
    m = jnp.mean(x, axis=axis, keepdims=True)
    v = jnp.var(x, axis=axis, keepdims=True)
    return (x - m) / jnp.sqrt(v + eps)

def _scatter_add(tgt, idx, src, axis=0):
    return tgt.at[idx].add(src)

def _segment_sum(src, seg, n):
    return jax.ops.segment_sum(src, seg, n)
kernel_name = 'mk_xattn_ffn_d1_seqx_r4_265d83'

def setup_inputs(seed: int=0):
    np.random.seed(seed)
    _w = jnp.asarray

    def _rec_inputs():
        import jax
        import jax.numpy as jnp
        _rk = jax.random.key(seed)
        x = -0.0002928 + 1 * jax.random.normal(jax.random.fold_in(_rk, 1), (16, 128, 256), jnp.float32)
        _lenS = 128 - jax.random.randint(jax.random.fold_in(_rk, 7), (16,), 0, max(1, 128 // 4) + 1, jnp.int32)
        _lenS2 = 128 - jax.random.randint(jax.random.fold_in(_rk, 8), (16,), 0, max(1, 128 // 4) + 1, jnp.int32)
        _ctx_1024P = jax.random.normal(jax.random.fold_in(_rk, 11), (16, 16, 256), jnp.float32)
        _ctx_1024c = jax.random.dirichlet(jax.random.fold_in(_rk, 511), 0.3 * jnp.ones((16,), jnp.float32), (16, 128))
        _ctx_1024t = jnp.einsum('bsk,bkd->bsd', _ctx_1024c, _ctx_1024P)
        _ctx_1024t = _ctx_1024t * jax.lax.rsqrt(jnp.mean(jnp.square(_ctx_1024t)) + 1e-12) * 0.953939
        ctx_1024 = -1.39393e-06 + 0.999914 * (_ctx_1024t + 0.3 * jax.random.normal(jax.random.fold_in(_rk, 611), (16, 128, 256), jnp.float32))
        return (x, ctx_1024)
    x, ctx_1024 = _rec_inputs()

    def _L0_xattn_setup():
        import jax, jax.numpy as jnp
        import numpy as np
        EMB = 256
        NH = 8
        HD = EMB // NH
        EPS = 1e-06

        def _mlstm_head(q, k, v, ig, fg):
            S, DH = q.shape
            log_fg = jax.nn.log_sigmoid(fg)
            cs = jnp.concatenate([jnp.zeros((1, 1), q.dtype), jnp.cumsum(log_fg, axis=0)], axis=0)
            fg_mat_full = cs - cs.T
            ltr = jnp.tril(jnp.ones((S, S), bool))
            log_fg_matrix = jnp.where(ltr, fg_mat_full[1:, 1:], -jnp.inf)
            log_D = log_fg_matrix + ig.T
            max_log_D = jnp.max(log_D, axis=-1, keepdims=True)
            D = jnp.exp(log_D - max_log_D)
            qk = q @ (k.T / jnp.sqrt(jnp.asarray(DH, q.dtype)))
            C = qk * D
            normalizer = jnp.maximum(jnp.abs(C.sum(-1, keepdims=True)), jnp.exp(-max_log_D))
            return C / (normalizer + EPS) @ v
        key = jax.random.key(seed)
        ks = jax.random.split(key, 6)
        B, S = (2, 512)
        q = jax.random.normal(ks[0], (B, S, EMB), jnp.float32)
        k = jax.random.normal(ks[1], (B, S, EMB), jnp.float32)
        v = jax.random.normal(ks[2], (B, S, EMB), jnp.float32)
        igate_kernel = jax.random.normal(ks[3], (3 * EMB, NH), jnp.float32) * 0.02
        igate_bias = jax.random.normal(ks[4], (NH,), jnp.float32) * 0.1
        fgate_kernel = jax.random.normal(ks[5], (3 * EMB, NH), jnp.float32) * 0.02
        fgate_bias = jnp.linspace(3.0, 6.0, NH).astype(jnp.float32)
        return dict(q=q, k=k, v=v, igate_kernel=igate_kernel, igate_bias=igate_bias, fgate_kernel=fgate_kernel, fgate_bias=fgate_bias)
    _L0_xattn_all = _L0_xattn_setup()
    _L0_xattn_in = {k: v for k, v in _L0_xattn_all.items() if k in ('igate_kernel', 'igate_bias', 'fgate_kernel', 'fgate_bias')}
    del _L0_xattn_all

    def _L0_ffn_setup():
        import jax, jax.numpy as jnp
        import numpy as np
        B, S, D = (4, 512, 256)
        E, F = (8, 1024)
        key = jax.random.key(seed)
        ks = jax.random.split(key, 5)
        x = jax.random.normal(ks[0], (B, S, D), dtype=jnp.float32)
        switch_w = jax.random.normal(ks[1], (D, E), dtype=jnp.float32) * D ** (-0.5)
        switch_b = jnp.zeros((E,), dtype=jnp.float32)
        w1 = jax.random.normal(ks[2], (E, D, F), dtype=jnp.float32) * D ** (-0.5)
        b1 = jnp.zeros((E, F), dtype=jnp.float32)
        w2 = jax.random.normal(ks[3], (E, F, D), dtype=jnp.float32) * F ** (-0.5)
        b2 = jnp.zeros((E, D), dtype=jnp.float32)
        return {'x': x, 'switch_w': switch_w, 'switch_b': switch_b, 'w1': w1, 'b1': b1, 'w2': w2, 'b2': b2}
    _L0_ffn_all = _L0_ffn_setup()
    _L0_ffn_in = {k: v for k, v in _L0_ffn_all.items() if k in ('switch_w', 'switch_b', 'w1', 'b1', 'w2', 'b2')}
    del _L0_ffn_all
    return {'x': x, 'ctx_1024': ctx_1024, 'L0_xattn_igate_kernel': _L0_xattn_in['igate_kernel'], 'L0_xattn_igate_bias': _L0_xattn_in['igate_bias'], 'L0_xattn_fgate_kernel': _L0_xattn_in['fgate_kernel'], 'L0_xattn_fgate_bias': _L0_xattn_in['fgate_bias'], 'L0_ffn_switch_w': _L0_ffn_in['switch_w'], 'L0_ffn_switch_b': _L0_ffn_in['switch_b'], 'L0_ffn_w1': _L0_ffn_in['w1'], 'L0_ffn_b1': _L0_ffn_in['b1'], 'L0_ffn_w2': _L0_ffn_in['w2'], 'L0_ffn_b2': _L0_ffn_in['b2']}

def reference(x, ctx_1024, L0_xattn_igate_kernel, L0_xattn_igate_bias, L0_xattn_fgate_kernel, L0_xattn_fgate_bias, L0_ffn_switch_w, L0_ffn_switch_b, L0_ffn_w1, L0_ffn_b1, L0_ffn_w2, L0_ffn_b2):
    import jax
    import jax.numpy as jnp

    def _L0_xattn_ref(q, k, v, igate_kernel, igate_bias, fgate_kernel, fgate_bias):
        import jax, jax.numpy as jnp
        import numpy as np
        EMB = 256
        NH = 8
        HD = EMB // NH
        EPS = 1e-06

        def _mlstm_head(q, k, v, ig, fg):
            S, DH = q.shape
            log_fg = jax.nn.log_sigmoid(fg)
            cs = jnp.concatenate([jnp.zeros((1, 1), q.dtype), jnp.cumsum(log_fg, axis=0)], axis=0)
            fg_mat_full = cs - cs.T
            ltr = jnp.tril(jnp.ones((S, S), bool))
            log_fg_matrix = jnp.where(ltr, fg_mat_full[1:, 1:], -jnp.inf)
            log_D = log_fg_matrix + ig.T
            max_log_D = jnp.max(log_D, axis=-1, keepdims=True)
            D = jnp.exp(log_D - max_log_D)
            qk = q @ (k.T / jnp.sqrt(jnp.asarray(DH, q.dtype)))
            C = qk * D
            normalizer = jnp.maximum(jnp.abs(C.sum(-1, keepdims=True)), jnp.exp(-max_log_D))
            return C / (normalizer + EPS) @ v
        B, S, H = q.shape
        x = jnp.concatenate([q, k, v], axis=-1)
        ig = x @ igate_kernel + igate_bias
        fg = x @ fgate_kernel + fgate_bias
        qh = q.reshape(B, S, NH, HD).swapaxes(1, 2)
        kh = k.reshape(B, S, NH, HD).swapaxes(1, 2)
        vh = v.reshape(B, S, NH, HD).swapaxes(1, 2)
        igp = ig.swapaxes(1, 2)[..., None]
        fgp = fg.swapaxes(1, 2)[..., None]
        h = jax.vmap(jax.vmap(_mlstm_head))(qh, kh, vh, igp, fgp)
        hf = h.astype(jnp.float32)
        h = (hf * jax.lax.rsqrt(jnp.mean(jnp.square(hf), axis=-1, keepdims=True) + 1e-06)).astype(h.dtype)
        return h.swapaxes(1, 2).reshape(B, S, H)

    def _L0_ffn_ref(x, switch_w, switch_b, w1, b1, w2, b2):
        import jax, jax.numpy as jnp
        import numpy as np
        B, S, D = (4, 512, 256)
        E, F = (8, 1024)
        b, s, d = x.shape
        t = x.reshape(-1, d)
        logits = t @ switch_w + switch_b
        route_prob = jax.nn.softmax(logits, axis=-1)
        route_prob_max = jnp.max(route_prob, axis=-1)
        routes = jnp.argmax(route_prob, axis=-1)
        out = jnp.zeros_like(t)
        n_experts = w1.shape[0]
        for e in range(n_experts):
            h = jax.nn.gelu(t @ w1[e] + b1[e])
            y = h @ w2[e] + b2[e]
            mask = (routes == e)[:, None]
            out = jnp.where(mask, y, out)
        out = out * route_prob_max[:, None]
        return out.reshape(b, s, d)
    x = x + _L0_xattn_ref(_layernorm(x, axis=-1), ctx_1024, ctx_1024, L0_xattn_igate_kernel, L0_xattn_igate_bias, L0_xattn_fgate_kernel, L0_xattn_fgate_bias)
    x = x + _L0_ffn_ref(_layernorm(x, axis=-1), L0_ffn_switch_w, L0_ffn_switch_b, L0_ffn_w1, L0_ffn_b1, L0_ffn_w2, L0_ffn_b2)
    return x

_drawn_inputs = setup_inputs


def setup_inputs(seed=0):
    import zlib

    import numpy as np

    out = dict(_drawn_inputs(seed))
    spreads = {'L0_ffn_switch_b': (0.0, 0.1), 'L0_ffn_b1': (0.0, 0.508), 'L0_ffn_b2': (0.0, 0.353)}
    factors = {'L0_xattn_igate_bias': 64.0}
    for name, (base, spread) in spreads.items():
        noise = np.random.default_rng([zlib.crc32(name.encode()), seed]).standard_normal(out[name].shape)
        drawn = base * np.exp(spread * noise) if base else spread * noise
        out[name] = jnp.asarray(drawn.astype(out[name].dtype))
    for name, factor in factors.items():
        out[name] = (out[name] * factor).astype(out[name].dtype)
    return out
```

```python
from contextlib import ExitStack

import concourse.bass as bass
from concourse import mybir

ALU = mybir.AluOpType
ACT = mybir.ActivationFunctionType
AX_X = mybir.AxisListType.X
F32 = mybir.dt.float32
F16 = mybir.dt.float16
BF16 = mybir.dt.bfloat16
I32 = mybir.dt.int32
U32 = mybir.dt.uint32

P = 128
NH = 8
HD = 32
G = P // HD
LN_EPS = 1e-5
MASKED = -1e30
TOKEN_SCALE = 2048.0
GW = 96
ds = bass.ds


def xattn_ffn_kernel(nc, x, ctx_in, ig_w, ig_b, fg_w, fg_b, sw_w, sw_b, w1, b1, w2, b2, out):
    B, S, D = x.shape
    E, _, F = w1.shape
    N = B * S
    KC = D // P
    FC = F // P
    NT = N // P
    TILES = NT + E - 1
    BH = B * NH
    ROW = D + 4
    MEAN, RSTD, PROB, TOKEN = D, D + 1, D + 2, D + 3
    PAIRS = B // 2
    HALF = KC * F
    W1HI, W2HI, W1LO, W2LO = 0, HALF, 2 * HALF, 3 * HALF
    assert S == P and BH == P and KC == 2 and FC * D == HALF and E == PAIRS and E == NH

    x_f = x
    out_f = out.rearrange("b s d -> (b s) d")
    w1_v = w1.rearrange("e (k p) f -> e p k f", p=P)
    w2_v = w2.rearrange("e (c p) d -> e p c d", p=P)

    transposed_dram = nc.dram_tensor("transposed_dram", (B, P, 2 * D), F32, kind="Internal").ap()
    negmax_dram = nc.dram_tensor("negmax_dram", (3, BH, P), BF16, kind="Internal").ap()
    decay_dram = nc.dram_tensor("decay_dram", (BH, 3, P), BF16, kind="Internal").ap()
    sorted_dram = nc.dram_tensor("sorted_dram", (TILES * P, ROW), F32, kind="Internal").ap()

    with ExitStack() as stack:
        def sb(name, shape, dt=F32):
            return stack.enter_context(nc.sbuf_tensor(name, shape, dt))

        def sem(name):
            return stack.enter_context(nc.semaphore(name))

        psum = stack.enter_context(nc.psum_tensor("psum", [P, 8, 512], F32))

        weights = sb("weights", [P, E + 1, 4 * HALF], F16)
        rows = sb("rows", [P, B, ROW])
        ident = sb("ident", [P, P])
        ident16 = sb("ident16", [P, P], F16)
        identb = sb("identb", [P, P], BF16)
        upto = sb("upto", [P, P])
        before = sb("before", [P, P], BF16)
        ones32 = sb("ones32", [P, P])
        onesb = sb("onesb", [P, P], BF16)
        mask = sb("mask", [P, G, P], BF16)
        gates = sb("gates", [P, 2, BH])
        exp_negmax = sb("exp_negmax", [P, BH])
        logits = sb("logits", [P, B, E])
        gate_bias = sb("gate_bias", [P, 2, NH])
        router_bias = sb("router_bias", [P, E])
        router_w = sb("router_w", [P, KC, GW])
        b1_cols = sb("b1_cols", [P, E * FC])
        square_sums = sb("square_sums", [P, E, 2])
        partial_sums = sb("partial_sums", [P, 2])
        head_norm = sb("head_norm", [P, 2, NH])
        head_rms = sb("head_rms", [P, 2, NH])
        zero_row = sb("zero_row", [P, ROW])
        weight_scale = sb("weight_scale", [P, E, 2])
        eps_col = sb("eps_col", [P, 2])
        exponent = sb("exponent", [P, 2], I32)
        tile_expert = sb("tile_expert", [P, 32], I32)
        stat6 = sb("stat6", [P, 2, 6])
        moments = sb("moments", [P, 2, 2])

        WORDS = 9472
        shared = sb("shared", [P, WORDS])

        class Region:
            def __init__(self, at=0):
                self.at = at

            def __call__(self, shape, dt=F32):
                n = 1
                for d in shape:
                    n *= d
                words = n * (2 if dt in (F16, BF16) else 4) // 4
                v = shared[:, self.at:self.at + words]
                self.at += words
                assert self.at <= WORDS
                if dt is not F32:
                    v = v.bitcast(dt)
                if len(shape) == 2:
                    v = v.rearrange("p (a b) -> p a b", a=shape[0])
                if len(shape) == 3:
                    v = v.rearrange("p (a b c) -> p a b c", a=shape[0], b=shape[1])
                return v

        r = Region()
        q_diag = r([2, KC * G * P])
        k_cols = r([2, KC * P])
        v_tile = r([2, D + HD])
        add_rhs = r([2, KC * G * P], BF16)
        add_lhs = r([2, KC * P], BF16)
        junk = r([HALF], F16)
        squared = junk.bitcast(F32)[:, 0:2 * D]
        stage1_at = r.at
        decay = r([2, KC * G * P])
        heads = r([2, D])
        normed = r([2, D])
        normed_cols = r([2 * KC * P])
        r = Region(stage1_at)
        t_cols = r([2, 2 * D])
        ctx_tile = r([2, D])
        xn_tile = r([2, D])
        gate_w = r([4, GW])
        gate_raw = r([3, KC * 2 * NH])
        b1_rows = r([P])
        r = Region(stage1_at + 4 * D)
        neg_parts = r([3, P], BF16)
        a_parts = r([3, P], BF16)
        magnitude, decayed, log1p, log_forget, cum, a_rows, run_max, rest, cum_max = (r([P]) for _ in range(9))
        r = Region()
        top, total, prob, position, smallest = (r([B]) for _ in range(5))
        diff, chance, key, onehot, place, totals_et, scan, inside, base_et, spare = (r([BH]) for _ in range(10))
        onehot_b = r([BH], BF16)
        zeros128 = r([P])
        expert_no = r([BH])
        tile_edge = r([P])
        tile_no = r([32, E])
        slot_cmp = r([32, E])
        tile_expert_f = r([32])
        counts, run_tiles, run_end, run_start = (r([E]) for _ in range(4))
        position_u = sb("position_u", [P, B], U32)
        r = Region()
        tok32 = r([2, D])
        tok16 = r([2, 2 * D], F16)
        tok_cols = r([2, 2 * KC * P], F16)
        hidden = r([2, FC * P])
        hid16 = r([2, 2 * FC * P], F16)
        y_tile = r([2, D])
        row_ring = r([4, ROW])
        b2_rows = r([E, D])
        gelu_scale = sb("gelu_scale", [P, E])
        hidden_scale = sb("hidden_scale", [P, E])
        y_scale = sb("y_scale", [P, E])
        scale_tmp = sb("scale_tmp", [P, 4, E])
        row_token = sb("row_token", [P, 2], U32)
        b1_partial = sb("b1_partial", [P, E])

        cols_ps = [psum[:, 0, :], psum[:, 1, :]]
        gates_ps = [psum[:, 2, :], psum[:, 3, :]]
        b1_ps = psum[:, 4, :]
        cum_ps, igt_ps, cmt_ps = psum[:, 5, 0:P], psum[:, 6, 0:P], psum[:, 7, 0:P]
        add_ps = [psum[:, 0, :], psum[:, 1, :]]
        score_ps = [psum[:, 2, :], psum[:, 3, :]]
        head_ps = [psum[:, 4, :], psum[:, 5, :]]
        ncols_ps = psum[:, 6, :]
        logit_ps = psum[:, 7, :]
        ROW_SUM = 384
        SUMS = 448
        b1sum_ps = psum[:, 5, 0:E]
        rank_ps, total_ps = psum[:, 0, 0:P], psum[:, 1, 0:P]
        hidden_ps = [[psum[:, 0, :], psum[:, 1, :]], [psum[:, 2, :], psum[:, 3, :]]]
        tokc_ps = [psum[:, 4, 0:256].bitcast(F16), psum[:, 5, 0:256].bitcast(F16)]
        y_ps = [psum[:, 6, 0:D], psum[:, 7, 0:D]]

        consts_in = sem("consts_in")
        pool_step = sem("pool_step")
        ident_ready = sem("ident_ready")
        b1_ready = sem("b1_ready")
        heads_scaled = sem("heads_scaled")
        normed_ready = sem("normed_ready")
        presets_ready = sem("presets_ready")
        x_in = [sem("x_in0"), sem("x_in1")]
        ctx_landed = [sem("ctx_landed0"), sem("ctx_landed1")]
        gate_w_ready = sem("gate_w_ready")
        stats_done = sem("stats_done")
        moments_done = sem("moments_done")
        ln_done = sem("ln_done")
        rstd_ready = sem("rstd_ready")
        eps_ready = sem("eps_ready")
        rms_sums = sem("rms_sums")
        rms_ln_done, rms_ready = sem("rms_ln_done"), sem("rms_ready")
        xn_ready = sem("xn_ready")
        cols_done = sem("cols_done")
        cols_ready = sem("cols_ready")
        cols_stored = [sem("cols_stored0"), sem("cols_stored1")]
        gates_done = sem("gates_done")
        gates_read = sem("gates_read")
        b1_done = sem("b1_done")
        vec2 = sem("vec2")
        act2 = sem("act2")
        magnitude_ready, log_forget_ready = sem("magnitude_ready"), sem("log_forget_ready")
        gates_turned, cum_max_ready = sem("gates_turned"), sem("cum_max_ready")
        cum_max_turned, exp_negmax_ready = sem("cum_max_turned"), sem("exp_negmax_ready")
        neg_ready, a_ready = sem("neg_ready"), sem("a_ready")
        parts_stored = sem("parts_stored")
        scores_in = [sem("scores_in0"), sem("scores_in1")]
        v_in = [sem("v_in0"), sem("v_in1")]
        add_done = sem("add_done")
        decay_ready = sem("decay_ready")
        scores_done = sem("scores_done")
        product_ready = sem("product_ready")
        heads_done = sem("heads_done")
        post = sem("post")
        squares_done = sem("squares_done")
        ncols_done = sem("ncols_done")
        ncols_ready = sem("ncols_ready")
        logits_done = sem("logits_done")
        logits_read = sem("logits_read")
        w1_in, w2_in = sem("w1_in"), sem("w2_in")
        sq_done = sem("sq_done")
        scale_step = sem("scale_step")
        scaled = sem("scaled")
        hi_ready = sem("hi_ready")
        lo_ready = sem("lo_ready")
        rows_cleared = sem("rows_cleared")
        vec4 = sem("vec4")
        diff_ready, chance_ready = sem("diff_ready"), sem("chance_ready")
        onehot_ready, ranks_done = sem("onehot_ready"), sem("ranks_done")
        b1_partial_ready, b1_summed = sem("b1_partial_ready"), sem("b1_summed")
        numbers_ready = sem("numbers_ready")
        route_ready = sem("route_ready")
        rows_sorted = sem("rows_sorted")
        b2_in = sem("b2_in")
        row_in = sem("row_in")
        tok_step = sem("tok_step")
        tok_ready = sem("tok_ready")
        tokc_done = sem("tokc_done")
        tokc_ready = sem("tokc_ready")
        hidden_done = sem("hidden_done")
        gelu_ready = sem("gelu_ready")
        hid_step = sem("hid_step")
        hid_ready = sem("hid_ready")
        y_done = sem("y_done")
        y_step = sem("y_step")
        y_ready = sem("y_ready")
        y_stored = [sem("y_stored0"), sem("y_stored1")]

        waited = [sem("waited_vector"), sem("waited_pool"), sem("waited_sync")]

        block = stack.enter_context(nc.Block())

        def at(first, n):
            return slice(first, first + n) if isinstance(first, int) else ds(first, n)

        def raw(e):
            return weights[:, at(e + 1, 1), :].bitcast(F32).rearrange("p a b -> p (a b)")

        def part(e, first, n):
            return weights[:, at(e, 1), first:first + n].rearrange("p a b -> p (a b)")

        def row(b, first, n):
            return rows[:, at(b, 1), first:first + n].rearrange("p a b -> p (a b)")

        def windows(v, first, step):
            return bass.AP(tensor=v.tensor, offset=v.offset + first, ap=[v.ap[0], [step, 3], [1, HD]])

        def has(n, low, high):
            return not isinstance(n, int) or low <= n < high

        def peeled(eng, body, first, loop_first, loop_last, last):
            for i in range(first, loop_first):
                body(i)
            with eng.Fori(loop_first, loop_last) as i:
                body(i)
            for i in range(loop_last, last):
                body(i)

        SMALL_LOADS = 11
        SCORE_DMAS = G + 3

        @block.sync
        def _(sp):
            def load_x(i, q):
                t = 2 * i + q
                if has(i, 1, PAIRS):
                    sp.wait_ge(x_in[q], 16 * i)
                sp.dma_start(row(t, 0, D), x[at(t, 1)].rearrange("a s d -> (a s) d")).then_inc(x_in[q], 16)

            def load_ctx(i, q):
                t = 2 * i + q
                if has(i, 1, PAIRS):
                    sp.wait_ge(ctx_landed[q], 16 * i)
                    sp.wait_ge(cols_done, t - 1)
                sp.dma_start(ctx_tile[:, q, :],
                             ctx_in[at(t, 1)].rearrange("a s d -> (a s) d")).then_inc(ctx_landed[q], 16)

            def store(i, q):
                t = 2 * i + q
                sp.wait_ge(cols_ready, t + 1)
                sp.dma_start(transposed_dram[at(t, 1)].rearrange("a p c -> (a p) c"),
                             t_cols[:, q, :]).then_inc(cols_stored[q], 16)

            def weight_loads(e):
                if has(e, 1, E):
                    sp.wait_ge(w1_in, 16 * e)
                    sp.wait_ge(w2_in, 16 * e)
                sp.dma_start(raw(e)[:, 0:HALF].rearrange("p (k f) -> p k f", k=KC),
                             w1_v[at(e, 1)].rearrange("a p k f -> p (a k) f")).then_inc(w1_in, 16)
                sp.dma_start(raw(e)[:, HALF:].rearrange("p (c d) -> p c d", c=FC),
                             w2_v[at(e, 1)].rearrange("a p c d -> p (a c) d")).then_inc(w2_in, 16)

            for i in range(2):
                for q in range(2):
                    load_x(i, q)
            for q in range(2):
                load_ctx(0, q)
            for j, w in enumerate((ig_w, fg_w)):
                for m in range(3):
                    sp.dma_start(gate_raw[:, m, :].rearrange("p (k h) -> p k h", k=KC)[:, :, NH * j:NH * (j + 1)],
                                 w.rearrange("(m k p) h -> m p k h", k=KC, p=P)[m]).then_inc(consts_in, 16)
            sp.dma_start(router_w[:, :, 0:E], sw_w.rearrange("(k p) e -> p k e", p=P)).then_inc(consts_in, 16)
            sp.dma_start(b1_rows[0:E * FC, :], b1.rearrange("e (c p) -> (e c) p", p=P)).then_inc(consts_in, 16)
            sp.dma_start(gate_bias[:, 0, :], ig_b.partition_broadcast(P)).then_inc(consts_in, 16)
            sp.dma_start(gate_bias[:, 1, :], fg_b.partition_broadcast(P)).then_inc(consts_in, 16)
            sp.dma_start(router_bias[:], sw_b.partition_broadcast(P)).then_inc(consts_in, 16)

            def pair_of_loads(i):
                for q in range(2):
                    if has(i, 1, PAIRS - 1):
                        load_x(i + 1, q)
                    if has(i, 1, PAIRS):
                        load_ctx(i, q)
                for q in range(2):
                    store(i - 1, q)

            peeled(sp, pair_of_loads, 1, 1, PAIRS - 1, PAIRS + 1)
            weight_loads(0)
            weight_loads(1)

            sp.wait_ge(neg_ready, 1)
            sp.dma_start(negmax_dram.rearrange("m r i -> r m i"), neg_parts).then_inc(parts_stored, 16)
            sp.wait_ge(a_ready, 1)
            sp.dma_start(decay_dram, a_parts).then_inc(parts_stored, 16)
            for q in range(2):
                sp.wait_ge(cols_stored[q], 16 * PAIRS)
            sp.wait_ge(parts_stored, 32)
            sp.wait_ge(presets_ready, 1)

            def score_loads(i, q):
                b = 2 * i + q
                if has(i, 1, PAIRS):
                    sp.wait_ge(scores_done, KC * (b - 1))
                one = transposed_dram[at(b, 1)].rearrange("a p c -> (a p) c")
                for g in range(G):
                    sp.dma_start(q_diag[HD * g:HD * (g + 1), q, :].rearrange("p (k c) -> p k c", k=KC)[
                                     :, :, P * g:P * (g + 1)],
                                 one[HD * g:HD * (g + 1), 0:D].rearrange("p (k s) -> p k s", k=KC)
                                 ).then_inc(scores_in[q], 16)
                sp.dma_start(k_cols[:, q, :], one[:, D:2 * D]).then_inc(scores_in[q], 16)
                sp.dma_start(add_rhs[3 * G:3 * G + 3, q, :].rearrange("m (h i) -> m h i", i=P),
                             negmax_dram[:, at(NH * b, NH), :]).then_inc(scores_in[q], 16)
                sp.dma_start(add_lhs[0:3 * G, q, :].rearrange("r (k i) -> r k i", k=KC),
                             decay_dram[at(NH * b, NH)].rearrange("(k g) m j -> (g m) k j", k=KC)
                             ).then_inc(scores_in[q], 16)

            def v_load(i, q):
                b = 2 * i + q
                if has(i, 1, PAIRS):
                    sp.wait_ge(heads_done, b - 1)
                sp.dma_start(v_tile[:, q, 0:D],
                             ctx_in[at(b, 1)].rearrange("a s d -> (a s) d")).then_inc(v_in[q], 16)

            def attention(i):
                for q in range(2):
                    score_loads(i, q)
                    v_load(i, q)
                if has(i, 0, E - 2):
                    weight_loads(i + 2)

            peeled(sp, attention, 0, 1, PAIRS - 2, PAIRS)

            sp.wait_ge(route_ready, 1)
            sp.dma_start(b2_rows.rearrange("p e d -> p (e d)"),
                         b2.rearrange("e d -> (e d)").partition_broadcast(P)).then_inc(b2_in, 16)
            sp.wait_ge(rows_sorted, 16 * B)
            for s in range(4):
                sp.dma_start(row_ring[:, s, :], sorted_dram[s * P:(s + 1) * P, :]).then_inc(row_in, 16)
                sp.wait_ge(row_in, 16 * (s + 1))
            with sp.Fori(4, TILES) as s:
                sp.wait_ge(row_in, 16 * s)
                sp.sem_inc(waited[2], 1)
                sp.wait_ge(y_ready, s - 3)
                sp.sem_inc(waited[2], 1)
                sp.dma_start(row_ring[:, ds(s % 4, 1), :].rearrange("p a b -> p (a b)"),
                             sorted_dram[ds(s * P, P), :]).then_inc(row_in, 16)
            for q in range(2):
                sp.wait_ge(y_stored[q], 16 * ((TILES + 1 - q) // 2))

        @block.gpsimd
        def _(pool):
            chain = [0]

            def link(ins):
                chain[0] += 1
                ins.then_inc(pool_step, 1)
                pool.wait_ge(pool_step, chain[0])

            nc.gpsimd.memset(eps_col[:, 0:1], LN_EPS)
            nc.gpsimd.memset(eps_col[:, 1:2], 1e-6).then_inc(eps_ready, 1)
            nc.gpsimd.memset(ident[:], 0.0)
            nc.gpsimd.memset(ones32[:], 1.0)
            nc.gpsimd.memset(onesb[:], 1.0)
            link(nc.gpsimd.memset(mask[:], 0.0))
            nc.gpsimd.affine_select(out=ident[:], in_=ident[:], compare_op=ALU.not_equal, fill=1.0, base=0,
                                    pattern=[[-1, P]], channel_multiplier=1).then_inc(ident_ready, 1)
            nc.gpsimd.affine_select(out=upto[:], in_=ones32[:], compare_op=ALU.is_ge, fill=0.0, base=0,
                                    pattern=[[1, P]], channel_multiplier=-1)
            nc.gpsimd.affine_select(out=before[:], in_=onesb[:], compare_op=ALU.is_gt, fill=0.0, base=0,
                                    pattern=[[1, P]], channel_multiplier=-1)
            nc.gpsimd.affine_select(out=mask[:], in_=mask[:], compare_op=ALU.is_ge, fill=MASKED, base=0,
                                    pattern=[[0, G], [1, P]], channel_multiplier=-1)
            pool.wait_ge(ident_ready, 1)
            nc.gpsimd.tensor_copy(ident16[:], ident[:])
            nc.gpsimd.tensor_copy(identb[:], ident[:])
            for b in range(B):
                nc.gpsimd.iota(rows[:, b, TOKEN:TOKEN + 1].bitcast(I32), pattern=[[0, 1]], base=P * b,
                               channel_multiplier=1)
            nc.gpsimd.iota(zero_row[:, TOKEN:TOKEN + 1].bitcast(I32), pattern=[[0, 1]], base=N,
                           channel_multiplier=1)
            link(nc.gpsimd.memset(zero_row[:, 0:TOKEN], 0.0))
            ind = add_rhs[0:3 * G, :, :].rearrange("p q (k g s) -> p (q k) g s", k=KC, g=G)
            link(nc.gpsimd.memset(add_rhs[0:3 * G, :, :], 1.0))
            link(nc.gpsimd.affine_select(out=ind, in_=ind, compare_op=ALU.is_ge, fill=0.0, base=0,
                                         pattern=[[0, 2 * KC], [-3, G], [0, P]], channel_multiplier=1))
            link(nc.gpsimd.affine_select(out=ind, in_=ind, compare_op=ALU.is_ge, fill=0.0, base=2,
                                         pattern=[[0, 2 * KC], [3, G], [0, P]], channel_multiplier=-1))
            nc.gpsimd.memset(add_lhs[0:3 * G + 3, :, :], 1.0)
            nc.gpsimd.memset(v_tile[:, :, D:], 1.0)
            nc.gpsimd.memset(q_diag[:, :, :], 0.0).then_inc(presets_ready, 1)
            for t in range(TILES):
                pool.dma_start(sorted_dram[t * P:(t + 1) * P, :], zero_row[:]).then_inc(rows_cleared, 16)

            with pool.Fori(0, E) as e:
                pool.wait_ge(hi_ready, e + 1)
                nc.gpsimd.tensor_tensor(part(e, W1LO, 2 * HALF), raw(e), part(e, W1HI, 2 * HALF),
                                        ALU.subtract).then_inc(lo_ready, 1)

            pool.wait_ge(heads_done, B)
            nc.gpsimd.iota(expert_no, pattern=[[0, B], [1, E]], base=0, channel_multiplier=0,
                           allow_small_or_imprecise_dtypes=True)
            nc.gpsimd.iota(tile_edge, pattern=[[0, E], [P, B]], base=0, channel_multiplier=0,
                           allow_small_or_imprecise_dtypes=True)
            nc.gpsimd.iota(tile_no, pattern=[[1, 32], [0, E]], base=0, channel_multiplier=0,
                           allow_small_or_imprecise_dtypes=True).then_inc(numbers_ready, 1)

            pool.wait_ge(rows_cleared, 16 * TILES)
            pool.wait_ge(route_ready, 1)
            for b in range(B):
                pool.indirect_dma_start(out=sorted_dram, out_offset=bass.IndirectOffsetOnAxis(
                    ap=position_u[:, b:b + 1], axis=0), in_=rows[:, b, :], in_offset=None,
                    bounds_check=TILES * P - 1).then_inc(rows_sorted, 16)

            last_token = pool.to_reg(N - 1)

            def store(s, q):
                pool.wait_ge(y_ready, s + 1)
                pool.sem_inc(waited[1], 1)
                pool.indirect_dma_start(out=out_f, out_offset=bass.IndirectOffsetOnAxis(
                    ap=row_token[:, q:q + 1], axis=0), in_=y_tile[:, q, :], in_offset=None,
                    bounds_check=last_token, oob_is_err=False).then_inc(y_stored[q], 16)

            with pool.Fori(0, TILES // 2) as i:
                for q in range(2):
                    store(2 * i + q, q)
            store(TILES - 1, 0)

        @block.scalar
        def _(act):
            act.wait_ge(b1_done, 1)
            nc.scalar.activation(b1_cols[:], b1_ps[:, 0:E * FC], ACT.Copy).then_inc(b1_ready, 1)

            def rstd(i):
                last = moments[:, :, 1]
                act.wait_ge(moments_done, i + 1)
                nc.scalar.activation(last, last, ACT.Ln, bias=eps_col[:, 0:1]).then_inc(ln_done, 1)
                act.wait_ge(ln_done, i + 1)
                nc.scalar.activation(last, last, ACT.Exp, scale=-0.5).then_inc(rstd_ready, 1)

            def norm_pair(i):
                if has(i, 0, PAIRS):
                    rstd(i)
                if has(i, 1, PAIRS + 1):
                    columns(i - 1)

            def columns(i):
                for q in range(2):
                    t = 2 * i + q
                    act.wait_ge(cols_done, t + 1)
                    if not (isinstance(i, int) and i == 0):
                        act.wait_ge(gates_done, t - 1)
                        act.wait_ge(cols_stored[q], 16 * i)
                    nc.scalar.activation(t_cols[:, q, :], cols_ps[q], ACT.Copy).then_inc(cols_ready, 1)

            def squares(e):
                act.wait_ge(w1_in, 16 * (e + 1))
                act.wait_ge(w2_in, 16 * (e + 1))
                if has(e, 1, E):
                    act.wait_ge(logits_done, e)
                if has(e, 2, E):
                    act.wait_ge(rms_sums, e - 1)
                for j in range(2):
                    if j == 1:
                        act.wait_ge(sq_done, 2 * e + 1)
                    nc.scalar.activation(junk, raw(e)[:, HALF * j:HALF * (j + 1)], ACT.Square,
                                         accum_out=partial_sums[:, j:j + 1]).then_inc(sq_done, 1)

            act.wait_ge(eps_ready, 1)
            peeled(act, norm_pair, 0, 2, PAIRS, PAIRS + 1)

            act.wait_ge(magnitude_ready, 1)
            nc.scalar.activation(decayed, magnitude, ACT.Exp).then_inc(act2, 1)
            act.wait_ge(act2, 1)
            nc.scalar.activation(log1p, decayed, ACT.Ln, bias=1.0).then_inc(act2, 1)
            squares(0)
            act.wait_ge(cum_max_turned, 1)
            nc.scalar.activation(exp_negmax[:], cmt_ps, ACT.Exp, scale=-1.0).then_inc(exp_negmax_ready, 1)

            def decays(b, q):
                for k in range(KC):
                    act.wait_ge(add_done, KC * b + k + 1)
                    if k == 0 and not (isinstance(b, int) and b < 2):
                        act.wait_ge(heads_done, b - 1)
                    nc.scalar.activation(decay[:, q, G * P * k:G * P * (k + 1)], add_ps[k],
                                         ACT.Exp).then_inc(decay_ready, 1)

            def hi(e, h):
                if h == 0:
                    act.wait_ge(scaled, e + 1)
                    if not (isinstance(e, int) and e == 0):
                        act.wait_ge(lo_ready, e)
                ins = nc.scalar.activation(part(e, W1HI + HALF * h, HALF),
                                           raw(e)[:, HALF * h:HALF * (h + 1)], ACT.Copy)
                if h == 1:
                    ins.then_inc(hi_ready, 1)

            def attention(i):
                if has(i, 0, PAIRS):
                    decays(2 * i, 0)
                if has(i, 3, PAIRS + 3):
                    act.wait_ge(ncols_done, i - 2)
                    nc.scalar.activation(normed_cols, ncols_ps, ACT.Copy).then_inc(ncols_ready, 1)
                if has(i, 1, E + 1):
                    hi(i - 1, 0)
                if has(i, 1, PAIRS + 1):
                    act.wait_ge(heads_scaled, i)
                    nc.scalar.activation(squared, heads.rearrange("p q d -> p (q d)"),
                                         ACT.Square).then_inc(squares_done, 1)
                if has(i, 0, PAIRS):
                    decays(2 * i + 1, 1)
                if has(i, 1, E + 1):
                    hi(i - 1, 1)
                if has(i, 1, PAIRS + 1):
                    act.wait_ge(rms_sums, i)
                    nc.scalar.activation(head_rms[:], head_rms[:], ACT.Ln, scale=1.0 / HD,
                                         bias=eps_col[:, 1:2]).then_inc(rms_ln_done, 1)
                    act.wait_ge(rms_ln_done, i)
                    nc.scalar.activation(head_rms[:], head_rms[:], ACT.Exp, scale=-0.5).then_inc(rms_ready, 1)
                if has(i, 0, E - 1):
                    squares(i + 1)
                if has(i, 1, PAIRS + 1):
                    rstd(i - 1 + PAIRS)

            peeled(act, attention, 0, 3, PAIRS - 1, PAIRS + 3)

            act.wait_ge(diff_ready, 1)
            nc.scalar.activation(chance, diff, ACT.Exp).then_inc(chance_ready, 1)

            def gelu(s, q):
                e = act.value_load(tile_expert[0:1, at(s, 1)], min_val=0, max_val=E - 1)
                for c in range(FC):
                    if c % 4 == 0:
                        act.wait_ge(hidden_done, 2 * s + c // 4 + 1)
                        if c == 0 and not (isinstance(s, int) and s < 2):
                            act.wait_ge(hid_ready, 2 * (s - 1))
                    ins = nc.scalar.activation(
                        hidden[:, q, P * c:P * (c + 1)], hidden_ps[q][c // 4][:, P * (c % 4):P * (c % 4 + 1)],
                        ACT.Gelu_apprx_tanh, bias=b1_cols[:, ds(e * FC + c, 1)], scale=gelu_scale[:, ds(e, 1)])
                    if c % 4 == 3:
                        ins.then_inc(gelu_ready, 1)

            act.wait_ge(route_ready, 1)
            gelu(0, 0)
            gelu(1, 1)
            with act.Fori(1, TILES // 2) as i:
                for q in range(2):
                    gelu(2 * i + q, q)
            gelu(TILES - 1, 0)

        @block.tensor
        def _(pe):
            pe.wait_ge(ident_ready, 1)
            pe.wait_ge(consts_in, 16 * SMALL_LOADS)
            nc.tensor.transpose(b1_ps[:, 0:E * FC], b1_rows[0:E * FC, :],
                                ident[0:E * FC, 0:E * FC]).then_inc(b1_done, 1)
            pe.wait_ge(gate_w_ready, 1)

            def turn(i, q):
                t = 2 * i + q
                pe.wait_ge(xn_ready, t + 1)
                pe.wait_ge(ctx_landed[q], 16 * (i + 1))
                if has(i, 1, PAIRS):
                    pe.wait_ge(cols_ready, t - 1)
                for k in range(KC):
                    nc.tensor.transpose(cols_ps[q][:, P * k:P * (k + 1)], xn_tile[:, q, P * k:P * (k + 1)],
                                        ident[:])
                for k in range(KC):
                    last = nc.tensor.transpose(cols_ps[q][:, D + P * k:D + P * (k + 1)],
                                               ctx_tile[:, q, P * k:P * (k + 1)], ident[:])
                last.then_inc(cols_done, 1)

            def gate(i, q):
                t = 2 * i + q
                pe.wait_ge(cols_ready, t + 1)
                if not (isinstance(t, int) and t < 2):
                    pe.wait_ge(gates_read, t - 1)
                for m in range(2 * KC):
                    last = nc.tensor.matmul(gates_ps[q][:, 0:GW], t_cols[:, q, P * m:P * (m + 1)],
                                            gate_w[:, m, :], start=(m == 0), stop=(m == 2 * KC - 1))
                last.then_inc(gates_done, 1)

            def gates_pair(i):
                turn(i, 0)
                if has(i, 1, PAIRS):
                    gate(i - 1, 1)
                turn(i, 1)
                gate(i, 0)

            peeled(pe, gates_pair, 0, 1, PAIRS, PAIRS)
            gate(PAIRS - 1, 1)

            pe.wait_ge(presets_ready, 1)
            pe.wait_ge(log_forget_ready, 1)
            nc.tensor.matmul(cum_ps, log_forget, upto[:], start=True, stop=True)
            nc.tensor.transpose(igt_ps, gates[:, 0, :], ident[:]).then_inc(gates_turned, 1)
            pe.wait_ge(cum_max_ready, 1)
            nc.tensor.transpose(cmt_ps, cum_max, ident[:]).then_inc(cum_max_turned, 1)

            def sums(e):
                pe.wait_ge(sq_done, 2 * (e + 1))
                return nc.tensor.matmul(logit_ps[:, SUMS:SUMS + 2], ones32[:], partial_sums[:],
                                        start=True, stop=True)

            pe.wait_ge(exp_negmax_ready, 1)
            sums(0).then_inc(logits_done, 1)

            def scores(i, q):
                b = 2 * i + q
                pe.wait_ge(scores_in[q], 16 * SCORE_DMAS * (i + 1))
                for k in range(KC):
                    if not (isinstance(b, int) and b == 0):
                        pe.wait_ge(decay_ready, KC * (b - 1) + k + 1)
                    nc.tensor.matmul(add_ps[k], identb[:], mask[:].rearrange("p g s -> p (g s)"),
                                     start=True, stop=False)
                    nc.tensor.matmul(add_ps[k], add_lhs[0:3 * G + 3, q, P * k:P * (k + 1)],
                                     add_rhs[0:3 * G + 3, q, G * P * k:G * P * (k + 1)],
                                     start=False, stop=True).then_inc(add_done, 1)
                for k in range(KC):
                    if not (isinstance(b, int) and b == 0):
                        pe.wait_ge(product_ready, KC * (b - 1) + k + 1)
                    nc.tensor.matmul(score_ps[k], k_cols[:, q, P * k:P * (k + 1)],
                                     q_diag[:, q, G * P * k:G * P * (k + 1)],
                                     start=True, stop=True).then_inc(scores_done, 1)

            def values(i, q):
                b = 2 * i + q
                pe.wait_ge(product_ready, KC * (b + 1))
                pe.wait_ge(v_in[q], 16 * (i + 1))
                if not (isinstance(b, int) and b < 2):
                    pe.wait_ge(heads_scaled, i)
                for h in range(NH):
                    halfway = (D - HD * h) // 2
                    moving = windows(v_tile[:, q, :], HD * h, halfway)
                    target = windows(head_ps[q], HD * h, (ROW_SUM + 2 * h - HD * h) // 2)
                    last = nc.tensor.matmul(target, decay[:, q, P * h:P * (h + 1)], moving,
                                            start=True, stop=True)
                last.then_inc(heads_done, 1)

            def attention(i):
                if has(i, 3, PAIRS + 3):
                    pe.wait_ge(normed_ready, i - 2)
                    if has(i, 4, PAIRS + 3):
                        pe.wait_ge(ncols_ready, i - 3)
                    for q in range(2):
                        for k in range(KC):
                            last = nc.tensor.transpose(ncols_ps[:, D * q + P * k:D * q + P * (k + 1)],
                                                       normed[:, q, P * k:P * (k + 1)], ident[:])
                    last.then_inc(ncols_done, 1)
                if has(i, 0, PAIRS):
                    scores(i, 0)
                if has(i, 1, PAIRS + 1):
                    values(i - 1, 1)
                if has(i, 0, PAIRS):
                    scores(i, 1)
                    values(i, 0)
                if has(i, 0, E - 1) or has(i, 3, PAIRS + 3):
                    pe.wait_ge(logits_read, i + 1)
                if has(i, 3, PAIRS + 3):
                    pe.wait_ge(ncols_ready, i - 2)
                    for q in range(2):
                        for k in range(KC):
                            last = nc.tensor.matmul(
                                logit_ps[:, GW * q:GW * (q + 1)],
                                normed_cols[:, D * q + P * k:D * q + P * (k + 1)],
                                router_w[:, k, :], start=(k == 0), stop=(k == KC - 1))
                if has(i, 0, E - 1):
                    last = sums(i + 1)
                if has(i, 0, E - 1) or has(i, 3, PAIRS + 3):
                    last.then_inc(logits_done, 1)

            peeled(pe, attention, 0, 4, PAIRS - 1, PAIRS + 3)

            pe.wait_ge(onehot_ready, 1)
            nc.tensor.matmul(rank_ps, before[:], onehot_b, start=True, stop=True)
            nc.tensor.matmul(total_ps, onesb[:], onehot_b, start=True, stop=True).then_inc(ranks_done, 1)
            pe.wait_ge(b1_partial_ready, 1)
            nc.tensor.matmul(b1sum_ps, ones32[:], b1_partial[:], start=True, stop=True).then_inc(b1_summed, 1)
            pe.wait_ge(route_ready, 1)
            pe.wait_ge(lo_ready, E)

            def turn_tokens(s, q):
                pe.wait_ge(tok_ready, s + 1)
                if not (isinstance(s, int) and s < 2):
                    pe.wait_ge(tokc_ready, s - 1)
                for j in range(2):
                    for k in range(KC):
                        last = nc.tensor.transpose(tokc_ps[q][:, P * (KC * j + k):P * (KC * j + k + 1)],
                                                   tok16[:, q, D * j + P * k:D * j + P * (k + 1)], ident16[:])
                last.then_inc(tokc_done, 1)

            def up(s, q):
                e = pe.value_load(tile_expert[0:1, at(s, 1)], min_val=0, max_val=E - 1)
                pe.wait_ge(tokc_ready, s + 1)
                for c in range(FC):
                    if c == 0 and not (isinstance(s, int) and s < 2):
                        pe.wait_ge(gelu_ready, 2 * (s - 1))
                    n = 0
                    for w_at, j in ((W1HI, 0), (W1LO, 0), (W1HI, 1)):
                        for k in range(KC):
                            last = nc.tensor.matmul(
                                hidden_ps[q][c // 4][:, P * (c % 4):P * (c % 4 + 1)],
                                part(e, w_at + F * k + P * c, P),
                                tok_cols[:, q, P * (KC * j + k):P * (KC * j + k + 1)],
                                start=(n == 0), stop=(n == 3 * KC - 1))
                            n += 1
                    if c % 4 == 3:
                        last.then_inc(hidden_done, 1)

            def down(s, q):
                e = pe.value_load(tile_expert[0:1, at(s, 1)], min_val=0, max_val=E - 1)
                if not (isinstance(s, int) and s < 2):
                    pe.wait_ge(y_ready, s - 1)
                n = 0
                for c in range(FC):
                    if c % 4 == 0:
                        pe.wait_ge(hid_ready, 2 * s + c // 4 + 1)
                    for j, w_at in ((0, W2HI), (0, W2LO), (1, W2HI)):
                        last = nc.tensor.matmul(y_ps[q], hid16[:, q, FC * P * j + P * c:FC * P * j + P * (c + 1)],
                                                part(e, w_at + D * c, D), start=(n == 0), stop=(n == 3 * FC - 1))
                        n += 1
                last.then_inc(y_done, 1)

            def ffn(s, q):
                if has(s, 0, TILES):
                    up(s, q)
                if has(s, 0, TILES - 1):
                    turn_tokens(s + 1, 1 - q)
                if has(s, 1, TILES + 1):
                    down(s - 1, 1 - q)

            turn_tokens(0, 0)
            ffn(0, 0)
            ffn(1, 1)
            with pe.Fori(1, TILES // 2) as i:
                for q in range(2):
                    ffn(2 * i + q, q)
            ffn(TILES - 1, 0)
            ffn(TILES, 1)

        @block.vector
        def _(dve):
            steps = {}

            def link(sem_, ins):
                steps[sem_.name] = steps.get(sem_.name, 0) + 1
                ins.then_inc(sem_, 1)
                dve.wait_ge(sem_, steps[sem_.name])

            dve.wait_ge(consts_in, 16 * SMALL_LOADS)
            nc.vector.memset(router_w[:, :, E:], 0.0)
            nc.vector.memset(gate_w[:, :, 2 * NH:], 0.0)
            nc.vector.tensor_copy(gate_w[:, 0:KC, 0:2 * NH], gate_raw[:, 0, :].rearrange("p (k h) -> p k h", k=KC))
            nc.vector.tensor_tensor(gate_w[:, KC:2 * KC, 0:2 * NH],
                                    gate_raw[:, 1, :].rearrange("p (k h) -> p k h", k=KC),
                                    gate_raw[:, 2, :].rearrange("p (k h) -> p k h", k=KC),
                                    ALU.add).then_inc(gate_w_ready, 1)

            def read_gates(i):
                for q in range(2):
                    t = 2 * i + q
                    dve.wait_ge(gates_done, t + 1)
                    nc.vector.tensor_tensor(gates[:, :, at(NH * t, NH)],
                                            gates_ps[q][:, 0:2 * NH].rearrange("p (j h) -> p j h", j=2),
                                            gate_bias[:], ALU.add).then_inc(gates_read, 1)

            def norm_pair(i):
                if has(i, 0, PAIRS):
                    if has(i, 1, PAIRS):
                        dve.wait_ge(moments_done, i)
                    for q in range(2):
                        dve.wait_ge(x_in[q], 16 * (i + 1))
                        dve.sem_inc(waited[0], 1)
                        ins = nc.vector.bn_stats(stat6[:, q, :], row(2 * i + q, 0, D))
                    ins.then_inc(stats_done, 1)
                if has(i, 1, PAIRS + 1):
                    dve.wait_ge(rstd_ready, i)
                    for q in range(2):
                        t = 2 * (i - 1) + q
                        if has(i, 2, PAIRS + 1):
                            dve.wait_ge(cols_done, t - 1)
                        nc.vector.tensor_scalar(xn_tile[:, q, :], row(t, 0, D), moments[:, q, 0:1],
                                                moments[:, q, 1:2], ALU.subtract, ALU.mult).then_inc(xn_ready, 1)
                if has(i, 0, PAIRS):
                    if has(i, 1, PAIRS):
                        dve.wait_ge(xn_ready, 2 * i)
                    dve.wait_ge(stats_done, i + 1)
                    dve.sem_inc(waited[0], 1)
                    for q in range(2):
                        ins = nc.vector.bn_aggr(moments[:, q, :], stat6[:, q, :])
                    ins.then_inc(moments_done, 1)
                if has(i, 2, PAIRS + 2):
                    read_gates(i - 2)

            peeled(dve, norm_pair, 0, 2, PAIRS, PAIRS + 2)

            dve.wait_ge(gates_read, B)
            nc.vector.scalar_tensor_tensor(magnitude, gates[:, 1, :], -1.0, gates[:, 1, :], ALU.mult,
                                           ALU.min).then_inc(magnitude_ready, 1)
            dve.wait_ge(act2, 2)
            nc.vector.scalar_tensor_tensor(log_forget, gates[:, 1, :], 0.0, log1p, ALU.min,
                                           ALU.subtract).then_inc(log_forget_ready, 1)
            dve.wait_ge(gates_turned, 1)
            link(vec2, nc.vector.tensor_copy(cum, cum_ps))
            link(vec2, nc.vector.tensor_tensor(a_rows, igt_ps, cum, ALU.subtract))
            link(vec2, nc.vector.tensor_tensor_scan(run_max, a_rows, a_rows, -3.0e38, ALU.max, ALU.max))
            nc.vector.tensor_tensor(cum_max, cum, run_max, ALU.add).then_inc(cum_max_ready, 1)
            for parts, source, sign, ready in ((neg_parts, run_max, -1.0, neg_ready), (a_parts, a_rows, 1.0, a_ready)):
                link(vec2, nc.vector.tensor_scalar(parts[:, 0, :], source, sign, None, ALU.mult))
                link(vec2, nc.vector.scalar_tensor_tensor(rest, source, sign, parts[:, 0, :],
                                                          ALU.mult, ALU.subtract))
                link(vec2, nc.vector.tensor_copy(parts[:, 1, :], rest))
                nc.vector.tensor_tensor(parts[:, 2, :], rest, parts[:, 1, :], ALU.subtract).then_inc(ready, 1)
                dve.wait_ge(ready, 1)

            POST = 6

            def products(b, q):
                for k in range(KC):
                    dve.wait_ge(decay_ready, KC * b + k + 1)
                    dve.wait_ge(scores_done, KC * b + k + 1)
                    half = decay[:, q, G * P * k:G * P * (k + 1)]
                    nc.vector.scalar_tensor_tensor(half, score_ps[k], HD ** -0.5, half, ALU.mult,
                                                   ALU.mult).then_inc(product_ready, 1)

            def after_heads(j):
                n = [0]

                def chain(ins):
                    n[0] += 1
                    ins.then_inc(post, 1)
                    dve.wait_ge(post, POST * j + n[0])

                two = rows[:, at(2 * j, 2), :]
                by_head = heads.rearrange("p q (h d) -> p (q h) d", h=NH)

                def divide():
                    dve.wait_ge(heads_done, 2 * j + 2)
                    for sign in (-1.0, 1.0):
                        for q in range(2):
                            sums = head_ps[q][:, ROW_SUM:ROW_SUM + 2 * NH:2]
                            other = exp_negmax[:, at(NH * (2 * j + q), NH)] if sign < 0 else head_norm[:, q, :]
                            ins = nc.vector.scalar_tensor_tensor(head_norm[:, q, :], sums, sign, other,
                                                                 ALU.mult, ALU.max)
                        chain(ins)
                    chain(nc.vector.tensor_scalar(head_norm[:], head_norm[:], 1e-6, None, ALU.add))
                    chain(nc.vector.reciprocal(head_norm[:], head_norm[:]))
                    for q in range(2):
                        ins = nc.vector.tensor_tensor(
                            heads[:, q, :].rearrange("p (h d) -> p h d", h=NH),
                            head_ps[q][:, 0:D].rearrange("p (h d) -> p h d", h=NH),
                            head_norm[:, q, :].unsqueeze(2).broadcast_to([P, NH, HD]), ALU.mult)
                    ins.then_inc(heads_scaled, 1)

                def sum_squares():
                    dve.wait_ge(squares_done, j + 1)
                    nc.vector.tensor_reduce(head_rms[:].rearrange("p q h -> p (q h)"),
                                            squared.rearrange("p (h d) -> p h d", d=HD), AX_X,
                                            ALU.add).then_inc(rms_sums, 1)

                def residual():
                    dve.wait_ge(rms_ready, j + 1)
                    chain(nc.vector.tensor_tensor(
                        by_head, by_head,
                        head_rms[:].rearrange("p q h -> p (q h)").unsqueeze(2).broadcast_to([P, 2 * NH, HD]),
                        ALU.mult))
                    chain(nc.vector.tensor_tensor(two[:, :, 0:D], two[:, :, 0:D], heads, ALU.add))
                    dve.sem_inc(waited[0], 1)
                    if not (isinstance(j, int) and j == 0):
                        dve.wait_ge(moments_done, PAIRS + j)
                        dve.sem_inc(waited[0], 1)
                    for q in range(2):
                        ins = nc.vector.bn_stats(stat6[:, q, :], row(2 * j + q, 0, D))
                    ins.then_inc(stats_done, 1)
                    if not (isinstance(j, int) and j == 0):
                        dve.wait_ge(normed_ready, j)
                    dve.wait_ge(stats_done, PAIRS + j + 1)
                    dve.sem_inc(waited[0], 1)
                    for q in range(2):
                        ins = nc.vector.bn_aggr(moments[:, q, :], stat6[:, q, :])
                    ins.then_inc(moments_done, 1)

                return divide, sum_squares, residual

            def norm_x1(j):
                dve.wait_ge(rstd_ready, PAIRS + j + 1)
                if not (isinstance(j, int) and j == 0):
                    dve.wait_ge(ncols_done, j)
                nc.vector.tensor_copy(rows[:, at(2 * j, 2), MEAN:MEAN + 2], moments[:])
                for q in range(2):
                    ins = nc.vector.tensor_scalar(normed[:, q, :], row(2 * j + q, 0, D), moments[:, q, 0:1],
                                                  moments[:, q, 1:2], ALU.subtract, ALU.mult)
                ins.then_inc(normed_ready, 1)

            def attention(i):
                if has(i, 0, PAIRS):
                    products(2 * i, 0)
                nothing = lambda: None
                divide = sum_squares = residual = nothing
                if has(i, 1, PAIRS + 1):
                    divide, sum_squares, residual = after_heads(i - 1)
                divide()
                if has(i, 0, E) or has(i, 4, PAIRS + 4):
                    dve.wait_ge(logits_done, i + 1)
                if has(i, 4, PAIRS + 4):
                    ins = nc.vector.tensor_tensor(
                        logits[:, at(2 * (i - 4), 2), :],
                        logit_ps[:, 0:2 * GW].rearrange("p (q e) -> p q e", q=2)[:, :, 0:E],
                        router_bias[:].unsqueeze(1).broadcast_to([P, 2, E]), ALU.add)
                if has(i, 0, E):
                    nc.vector.tensor_copy(square_sums[:, at(i, 1), :].rearrange("p a j -> p (a j)"),
                                          logit_ps[:, SUMS:SUMS + 2])
                    ins = nc.vector.tensor_scalar(exponent[:], logit_ps[:, SUMS:SUMS + 2].bitcast(I32), 24, None,
                                                  ALU.logical_shift_right)
                if has(i, 0, E) or has(i, 4, PAIRS + 4):
                    ins.then_inc(logits_read, 1)
                if has(i, 0, E):
                    dve.wait_ge(logits_read, i + 1)
                    scale = weight_scale[:, at(i, 1), :].rearrange("p a j -> p (a j)")
                    nc.vector.tensor_scalar(scale.bitcast(I32), exponent[:], -float(1 << 23), float(204 << 23),
                                            ALU.mult, ALU.add).then_inc(scale_step, 1)
                if has(i, 0, PAIRS):
                    products(2 * i + 1, 1)
                if has(i, 0, E):
                    dve.wait_ge(scale_step, i + 1)
                    for j in range(2):
                        words = raw(i)[:, HALF * j:HALF * (j + 1)]
                        ins = nc.vector.tensor_scalar(words, words, scale[:, j:j + 1], None, ALU.mult)
                    ins.then_inc(scaled, 1)
                sum_squares()
                if has(i, 2, PAIRS + 2):
                    norm_x1(i - 2)
                residual()

            peeled(dve, attention, 0, 4, PAIRS - 1, PAIRS + 4)

            dve.wait_ge(logits_read, PAIRS + 4)
            by_tile = lambda v: v.rearrange("p (b e) -> p b e", e=E)
            wide = lambda v: v.unsqueeze(2).broadcast_to([P, B, E])
            link(vec4, nc.vector.tensor_reduce(top, logits[:], AX_X, ALU.max))
            nc.vector.tensor_tensor(by_tile(diff), logits[:], wide(top), ALU.subtract).then_inc(diff_ready, 1)
            dve.wait_ge(diff_ready, 1)
            dve.wait_ge(numbers_ready, 1)
            link(vec4, nc.vector.tensor_scalar(key, diff, 0.0, float(E), ALU.is_lt, ALU.mult))
            link(vec4, nc.vector.tensor_tensor(key, key, expert_no, ALU.add))
            link(vec4, nc.vector.tensor_reduce(smallest, by_tile(key), AX_X, ALU.min))
            link(vec4, nc.vector.tensor_tensor(by_tile(onehot), by_tile(expert_no), wide(smallest), ALU.is_equal))
            nc.vector.tensor_copy(onehot_b, onehot).then_inc(onehot_ready, 1)
            dve.wait_ge(chance_ready, 1)
            link(vec4, nc.vector.tensor_reduce(total, by_tile(chance), AX_X, ALU.add))
            link(vec4, nc.vector.reciprocal(rows[:, :, PROB], total))
            link(vec4, nc.vector.tensor_tensor(spare[:, 0:E * FC], b1_cols[:], b1_cols[:], ALU.mult))
            nc.vector.tensor_reduce(b1_partial[:], spare[:, 0:E * FC].rearrange("p (e c) -> p e c", e=E), AX_X,
                                    ALU.add).then_inc(b1_partial_ready, 1)
            dve.wait_ge(b1_summed, 1)
            bound, bits, inverse = scale_tmp[:, 0, :], scale_tmp[:, 1, :].bitcast(I32), scale_tmp[:, 2, :]
            link(vec4, nc.vector.tensor_scalar(bound, square_sums[:, :, 0], 256.0, None, ALU.mult))
            link(vec4, nc.vector.tensor_tensor(bound, b1sum_ps, bound, ALU.add))
            link(vec4, nc.vector.tensor_scalar(bound, bound, 2.0, None, ALU.mult))
            link(vec4, nc.vector.tensor_scalar(bits, bound.bitcast(I32), 24, None, ALU.logical_shift_right))
            link(vec4, nc.vector.tensor_scalar(hidden_scale[:].bitcast(I32), bits, -float(1 << 23), float(204 << 23),
                                               ALU.mult, ALU.add))
            link(vec4, nc.vector.reciprocal(inverse, weight_scale[:, :, 0]))
            link(vec4, nc.vector.tensor_scalar(gelu_scale[:], inverse, 1.0 / TOKEN_SCALE, None, ALU.mult))
            link(vec4, nc.vector.reciprocal(inverse, hidden_scale[:]))
            link(vec4, nc.vector.reciprocal(bound, weight_scale[:, :, 1]))
            link(vec4, nc.vector.tensor_tensor(y_scale[:], inverse, bound, ALU.mult))
            by_expert = lambda v: v.rearrange("p (e b) -> p e b", e=E)
            wide_e = lambda v: v.unsqueeze(2).broadcast_to([P, E, B])
            dve.wait_ge(ranks_done, 1)
            nc.vector.memset(zeros128, 0.0)
            link(vec4, nc.vector.tensor_copy(by_expert(totals_et), by_tile(total_ps).rearrange("p b e -> p e b")))
            link(vec4, nc.vector.tensor_tensor_scan(scan, totals_et, zeros128, 0.0, ALU.add, ALU.add))
            link(vec4, nc.vector.tensor_tensor(inside, scan, totals_et, ALU.subtract))
            link(vec4, nc.vector.tensor_tensor(counts, by_expert(scan)[:, :, B - 1], by_expert(inside)[:, :, 0],
                                               ALU.subtract))
            link(vec4, nc.vector.tensor_tensor(by_expert(spare), by_expert(tile_edge), wide_e(counts), ALU.is_lt))
            link(vec4, nc.vector.tensor_reduce(run_tiles, by_expert(spare), AX_X, ALU.add))
            link(vec4, nc.vector.tensor_tensor_scan(run_end, run_tiles, zeros128[:, 0:E], 0.0, ALU.add, ALU.add))
            link(vec4, nc.vector.tensor_tensor(run_start, run_end, run_tiles, ALU.subtract))
            link(vec4, nc.vector.tensor_scalar(run_start, run_start, float(P), None, ALU.mult))
            link(vec4, nc.vector.tensor_tensor(run_start, run_start, by_expert(inside)[:, :, 0], ALU.subtract))
            link(vec4, nc.vector.tensor_tensor(by_expert(base_et), by_expert(inside), wide_e(run_start), ALU.add))
            link(vec4, nc.vector.tensor_tensor(by_tile(place), by_tile(rank_ps),
                                               by_expert(base_et).rearrange("p e b -> p b e"), ALU.add))
            link(vec4, nc.vector.tensor_tensor(place, place, onehot, ALU.mult))
            link(vec4, nc.vector.tensor_reduce(position, by_tile(place), AX_X, ALU.add))
            nc.vector.tensor_copy(position_u[:], position)
            link(vec4, nc.vector.tensor_tensor(slot_cmp, run_end.unsqueeze(1).broadcast_to([P, 32, E]), tile_no,
                                               ALU.is_le))
            link(vec4, nc.vector.tensor_reduce(tile_expert_f, slot_cmp, AX_X, ALU.add))
            nc.vector.tensor_scalar(tile_expert[:], tile_expert_f, float(E - 1), None,
                                    ALU.min).then_inc(route_ready, 1)
            dve.wait_ge(route_ready, 1)

            def ring(s, first, n):
                return row_ring[:, at(s % 4, 1), first:first + n].rearrange("p a b -> p (a b)")

            def tokens(s, q):
                dve.wait_ge(row_in, 16 * (s + 1))
                nc.vector.tensor_scalar(tok32[:, q, :], ring(s, 0, D), ring(s, MEAN, 1), ring(s, RSTD, 1),
                                        ALU.subtract, ALU.mult).then_inc(tok_step, 1)
                dve.wait_ge(tok_step, 2 * s + 1)
                if not (isinstance(s, int) and s < 2):
                    dve.wait_ge(tokc_done, s - 1)
                nc.vector.tensor_scalar(tok16[:, q, 0:D], tok32[:, q, :], TOKEN_SCALE, None,
                                        ALU.mult).then_inc(tok_step, 1)
                dve.wait_ge(tok_step, 2 * s + 2)
                nc.vector.scalar_tensor_tensor(tok16[:, q, D:2 * D], tok32[:, q, :], TOKEN_SCALE, tok16[:, q, 0:D],
                                               ALU.mult, ALU.subtract).then_inc(tok_ready, 1)

            def token_cols(s, q):
                dve.wait_ge(tokc_done, s + 1)
                if not (isinstance(s, int) and s < 2):
                    dve.wait_ge(hidden_done, 2 * (s - 1))
                nc.vector.tensor_copy(tok_cols[:, q, :], tokc_ps[q]).then_inc(tokc_ready, 1)

            def split_hidden(s, q, e):
                for h in range(2):
                    dve.wait_ge(gelu_ready, 2 * s + h + 1)
                    if h == 0 and not (isinstance(s, int) and s < 2):
                        dve.wait_ge(y_done, s - 1)
                    a, b = FC * P // 2 * h, FC * P // 2 * (h + 1)
                    nc.vector.tensor_scalar(hid16[:, q, a:b], hidden[:, q, a:b], hidden_scale[:, ds(e, 1)], None,
                                            ALU.mult).then_inc(hid_step, 1)
                    dve.wait_ge(hid_step, 2 * s + h + 1)
                    nc.vector.scalar_tensor_tensor(hid16[:, q, FC * P + a:FC * P + b], hidden[:, q, a:b],
                                                   hidden_scale[:, ds(e, 1)], hid16[:, q, a:b],
                                                   ALU.mult, ALU.subtract).then_inc(hid_ready, 1)

            def finish(s, q, e):
                dve.wait_ge(y_done, s + 1)
                if not (isinstance(s, int) and s < 2):
                    dve.wait_ge(y_stored[q], 16 * (s // 2))
                nc.vector.scalar_tensor_tensor(y_tile[:, q, :], y_ps[q], y_scale[:, ds(e, 1)],
                                               b2_rows[:, ds(e, 1), :].rearrange("p a d -> p (a d)"),
                                               ALU.mult, ALU.add).then_inc(y_step, 1)
                nc.vector.tensor_copy(row_token[:, q:q + 1], ring(s, TOKEN, 1).bitcast(U32))
                dve.wait_ge(y_step, s + 1)
                nc.vector.scalar_tensor_tensor(y_tile[:, q, :], y_tile[:, q, :], ring(s, PROB, 1), ring(s, 0, D),
                                               ALU.mult, ALU.add).then_inc(y_ready, 1)

            def ffn(s, q):
                if has(s, 1, TILES + 1):
                    e = dve.value_load(tile_expert[0:1, at(s - 1, 1)], min_val=0, max_val=E - 1)
                    split_hidden(s - 1, 1 - q, e)
                if has(s, 2, TILES + 2):
                    e = dve.value_load(tile_expert[0:1, at(s - 2, 1)], min_val=0, max_val=E - 1)
                    finish(s - 2, q, e)
                if has(s, 0, TILES - 1):
                    token_cols(s + 1, 1 - q)
                if has(s, 0, TILES - 2):
                    tokens(s + 2, q)

            tokens(0, 0)
            tokens(1, 1)
            token_cols(0, 0)
            dve.wait_ge(b2_in, 16)
            ffn(0, 0)
            ffn(1, 1)
            with dve.Fori(1, (TILES - 2) // 2) as i:
                for q in range(2):
                    ffn(2 * i + q, q)
            for s in range(2 * ((TILES - 2) // 2), TILES + 2):
                ffn(s, s % 2)


_INS = ['x', 'ctx_1024', 'L0_xattn_igate_kernel', 'L0_xattn_igate_bias', 'L0_xattn_fgate_kernel',
        'L0_xattn_fgate_bias', 'L0_ffn_switch_w', 'L0_ffn_switch_b', 'L0_ffn_w1', 'L0_ffn_b1', 'L0_ffn_w2',
        'L0_ffn_b2']
_OUTS = [((16, 128, 256), 'float32')]


def kernel(**inputs):
    import numpy as _np
    import concourse.bacc as _bacc
    from concourse import mybir as _mybir
    from concourse.bass_utils import run_bass_kernel_spmd as _run

    nc = _bacc.Bacc("TRN2", target_bir_lowering=False, num_devices=1)
    arrays, args = {}, []
    for name in _INS:
        a = _np.ascontiguousarray(inputs[name])
        arrays[f"in_{name}_dram"] = a
        args.append(nc.dram_tensor(f"in_{name}_dram", a.shape, _mybir.dt.from_np(a.dtype), kind="ExternalInput").ap())
    for i, (shape, dtype) in enumerate(_OUTS):
        dt = _mybir.dt.from_np(_np.dtype(dtype))
        args.append(nc.dram_tensor(f"out_{i}_dram", shape, dt, kind="ExternalOutput").ap())
    xattn_ffn_kernel(nc, *args)
    r = _run(nc, [arrays], core_ids=[0])
    got = tuple(r.results[0][f"out_{i}_dram"] for i in range(len(_OUTS)))
    return got[0]
```

```python
from contextlib import ExitStack

import concourse.bass as bass
from concourse import mybir

ALU = mybir.AluOpType
ACT = mybir.ActivationFunctionType
AX_X = mybir.AxisListType.X
F32 = mybir.dt.float32
F16 = mybir.dt.float16
BF16 = mybir.dt.bfloat16
I32 = mybir.dt.int32
U32 = mybir.dt.uint32

P = 128
NH = 8
HD = 32
G = P // HD
LN_EPS = 1e-5
MASKED = -1e30
TOKEN_SCALE = 2048.0
GW = 96
ds = bass.ds


def xattn_ffn_kernel(nc, x, ctx_in, ig_w, ig_b, fg_w, fg_b, sw_w, sw_b, w1, b1, w2, b2, out):
    B, S, D = x.shape
    E, _, F = w1.shape
    N = B * S
    KC = D // P
    FC = F // P
    NT = N // P
    TILES = NT + E - 1
    BH = B * NH
    TP = 24
    NOWHERE = 2 * N
    PAIRS = B // 2
    HALF = KC * F
    W1HI, W2HI, W1LO, W2LO = 0, HALF, 2 * HALF, 3 * HALF
    assert S == P and BH == P and KC == 2 and FC * D == HALF and E == PAIRS and E == NH

    x_f = x
    out_f = out.rearrange("b s d -> (b s) d")
    w1_v = w1.rearrange("e (k p) f -> e p k f", p=P)
    w2_v = w2.rearrange("e (c p) d -> e p c d", p=P)

    transposed_dram = nc.dram_tensor("transposed_dram", (B, P, 2 * D), F32, kind="Internal").ap()
    negmax_dram = nc.dram_tensor("negmax_dram", (3, BH, P), BF16, kind="Internal").ap()
    decay_dram = nc.dram_tensor("decay_dram", (BH, 3, P), BF16, kind="Internal").ap()
    normed_dram = nc.dram_tensor("normed_dram", (N, D), F32, kind="Internal").ap()

    with ExitStack() as stack:
        def sb(name, shape, dt=F32):
            return stack.enter_context(nc.sbuf_tensor(name, shape, dt))

        def sem(name):
            return stack.enter_context(nc.semaphore(name))

        psum = stack.enter_context(nc.psum_tensor("psum", [P, 8, 512], F32))

        weights = sb("weights", [P, E + 1, 4 * HALF], F16)
        rows = sb("rows", [P, B, D])
        ident = sb("ident", [P, P])
        ident16 = sb("ident16", [P, P], F16)
        identb = sb("identb", [P, P], BF16)
        upto = sb("upto", [P, P])
        before = sb("before", [P, P], BF16)
        ones32 = sb("ones32", [P, P])
        onesb = sb("onesb", [P, P], BF16)
        mask = sb("mask", [P, G, P], BF16)
        gates = sb("gates", [P, 2, BH])
        exp_negmax = sb("exp_negmax", [P, BH])
        logits = sb("logits", [P, B, E])
        gate_bias = sb("gate_bias", [P, 2, NH])
        router_bias = sb("router_bias", [P, E])
        router_w = sb("router_w", [P, KC, GW])
        b1_cols = sb("b1_cols", [P, E * FC])
        square_sums = sb("square_sums", [P, E, 2])
        partial_sums = sb("partial_sums", [P, 2])
        head_norm = sb("head_norm", [P, 2, NH])
        head_rms = sb("head_rms", [P, 2, NH])
        weight_scale = sb("weight_scale", [P, E, 2])
        eps_col = sb("eps_col", [P, 2])
        exponent = sb("exponent", [P, 2], I32)
        tile_expert = sb("tile_expert", [P, 32], I32)
        stat6 = sb("stat6", [P, 2, 6])
        moments = sb("moments", [P, 2, 2])

        WORDS = 9536
        shared = sb("shared", [P, WORDS])

        class Region:
            def __init__(self, at=0):
                self.at = at

            def __call__(self, shape, dt=F32):
                n = 1
                for d in shape:
                    n *= d
                words = n * (2 if dt in (F16, BF16) else 4) // 4
                v = shared[:, self.at:self.at + words]
                self.at += words
                assert self.at <= WORDS
                if dt is not F32:
                    v = v.bitcast(dt)
                if len(shape) == 2:
                    v = v.rearrange("p (a b) -> p a b", a=shape[0])
                if len(shape) == 3:
                    v = v.rearrange("p (a b c) -> p a b c", a=shape[0], b=shape[1])
                return v

        r = Region()
        q_diag = r([2, KC * G * P])
        k_cols = r([2, KC * P])
        v_tile = r([2, D + HD])
        add_rhs = r([2, KC * G * P], BF16)
        add_lhs = r([2, KC * P], BF16)
        junk = r([HALF], F16)
        stage1_at = r.at
        decay = r([2, KC * G * P])
        heads = r([2, D])
        normed = r([2, D])
        normed_cols = r([2 * KC * P])
        squared = r([2 * D])
        r = Region(stage1_at)
        t_cols = r([2, 2 * D])
        xn_tile = r([2, D])
        gate_w = r([4, GW])
        gate_raw = r([3, KC * 2 * NH])
        b1_rows = r([P])
        r = Region(stage1_at + 4 * D)
        neg_parts = r([3, P], BF16)
        a_parts = r([3, P], BF16)
        magnitude, decayed, log1p, log_forget, cum, a_rows, run_max, rest, cum_max = (r([P]) for _ in range(9))
        r = Region()
        top, total, prob, position, smallest = (r([B]) for _ in range(5))
        diff, chance, key, onehot, place, totals_et, scan, inside, base_et, spare = (r([BH]) for _ in range(10))
        onehot_b = r([BH], BF16)
        zeros128 = r([P])
        expert_no = r([BH])
        tile_edge = r([P])
        tile_no = r([32, E])
        slot_cmp = r([32, E])
        tile_expert_f = r([32])
        counts, run_tiles, run_end, run_start = (r([E]) for _ in range(4))
        tile_f, place_f = r([B]), r([B])
        position_i = r([B], I32)
        place_no, slot_no = r([P]), r([TP])
        values = r([B, 4], F16)
        in_tile = r([B, TP], F16)
        at_place = r([B, P], F16)
        spread = shared[:, r.at:r.at + B * 4 * TP // 2].bitcast(F16).rearrange("p (b v s) -> p b v s", b=B, v=4)
        r.at += B * 4 * TP // 2
        chosen = r([4 * TP])
        target_f = r([TP])
        gather_u = sb("gather_u", [P, TP], U32)
        scatter_u = sb("scatter_u", [P, TP], U32)
        probs = sb("probs", [P, TP])
        gather_now = sb("gather_now", [P, 4], U32)
        scatter_now = sb("scatter_now", [P, 4], U32)
        r = Region()
        tok16 = r([2, 2 * D], F16)
        tok_cols = r([2, 2 * KC * P], F16)
        hidden = r([2, FC * P])
        hid16 = r([2, 2 * FC * P], F16)
        y_tile = r([2, D])
        row_ring = r([4, D])
        b2_rows = r([E, D])
        gelu_scale = sb("gelu_scale", [P, E])
        hidden_scale = sb("hidden_scale", [P, E])
        y_scale = sb("y_scale", [P, E])
        scale_tmp = sb("scale_tmp", [P, 4, E])
        b1_partial = sb("b1_partial", [P, E])

        cols_ps = [psum[:, 0, :], psum[:, 1, :]]
        gates_ps = [psum[:, 2, :], psum[:, 3, :]]
        b1_ps = psum[:, 4, :]
        cum_ps, igt_ps, cmt_ps = psum[:, 5, 0:P], psum[:, 6, 0:P], psum[:, 7, 0:P]
        add_ps = [psum[:, 0, :], psum[:, 1, :]]
        score_ps = [psum[:, 2, :], psum[:, 3, :]]
        head_ps = [psum[:, 4, :], psum[:, 5, :]]
        ncols_ps = psum[:, 6, :]
        logit_ps = psum[:, 7, :]
        ROW_SUM = 384
        SUMS = 448
        b1sum_ps = psum[:, 5, 0:E]
        rank_ps, total_ps = psum[:, 0, 0:P], psum[:, 1, 0:P]
        chosen_ps = psum[:, 2, 0:4 * TP]
        hidden_ps = [[psum[:, 0, :], psum[:, 1, :]], [psum[:, 2, :], psum[:, 3, :]]]
        tokc_ps = [psum[:, 4, 0:256].bitcast(F16), psum[:, 5, 0:256].bitcast(F16)]
        y_ps = [psum[:, 6, :], psum[:, 7, :]]

        gate_w_in = sem("gate_w_in")
        consts_in = sem("consts_in")
        pool_step = sem("pool_step")
        ident_ready = sem("ident_ready")
        b1_ready = sem("b1_ready")
        heads_scaled = sem("heads_scaled")
        normed_ready = sem("normed_ready")
        presets_ready = sem("presets_ready")
        x_in = [sem("x_in0"), sem("x_in1")]
        ctx_landed = [sem("ctx_landed0"), sem("ctx_landed1")]
        gate_w_ready = sem("gate_w_ready")
        stats_done = sem("stats_done")
        moments_done = sem("moments_done")
        ln_done = sem("ln_done")
        rstd_ready = sem("rstd_ready")
        eps_ready = sem("eps_ready")
        rms_sums = sem("rms_sums")
        rms_ln_done, rms_ready = sem("rms_ln_done"), sem("rms_ready")
        xn_ready = sem("xn_ready")
        cols_done = sem("cols_done")
        cols_ready = sem("cols_ready")
        cols_stored = [sem("cols_stored0"), sem("cols_stored1")]
        gates_done = sem("gates_done")
        gates_read = sem("gates_read")
        b1_done = sem("b1_done")
        vec2 = sem("vec2")
        act2 = sem("act2")
        magnitude_ready, log_forget_ready = sem("magnitude_ready"), sem("log_forget_ready")
        gates_turned, cum_max_ready = sem("gates_turned"), sem("cum_max_ready")
        cum_max_turned, exp_negmax_ready = sem("cum_max_turned"), sem("exp_negmax_ready")
        neg_ready, a_ready = sem("neg_ready"), sem("a_ready")
        parts_stored = sem("parts_stored")
        scores_in = [sem("scores_in0"), sem("scores_in1")]
        v_in = [sem("v_in0"), sem("v_in1")]
        add_done = sem("add_done")
        decay_ready = sem("decay_ready")
        scores_done = sem("scores_done")
        product_ready = sem("product_ready")
        heads_done = sem("heads_done")
        heads_normed = sem("heads_normed")
        x1_ready = sem("x1_ready")
        post = sem("post")
        ncols_done = sem("ncols_done")
        ncols_ready = sem("ncols_ready")
        logits_done = sem("logits_done")
        logits_read = sem("logits_read")
        w1_in, w2_in = sem("w1_in"), sem("w2_in")
        sq_done = sem("sq_done")
        scale_ready = sem("scale_ready")
        scaled = sem("scaled")
        hi_ready = sem("hi_ready")
        lo_ready = sem("lo_ready")
        vec4 = sem("vec4")
        diff_ready, chance_ready = sem("diff_ready"), sem("chance_ready")
        onehot_ready, ranks_done = sem("onehot_ready"), sem("ranks_done")
        b1_partial_ready, b1_summed = sem("b1_partial_ready"), sem("b1_summed")
        numbers_ready = sem("numbers_ready")
        in_tile_ready, spread_ready = sem("in_tile_ready"), sem("spread_ready")
        at_place_ready, chosen_done = sem("at_place_ready"), sem("chosen_done")
        route_ready = sem("route_ready")
        scales_ready = sem("scales_ready")
        x1_stored = sem("x1_stored")
        normed_stored = sem("normed_stored")
        b2_in = sem("b2_in")
        row_in = [sem(f"row_in{u}") for u in range(4)]
        tok_step = sem("tok_step")
        tok_ready = sem("tok_ready")
        tokc_done = sem("tokc_done")
        tokc_ready = sem("tokc_ready")
        hidden_done = [sem("hidden_done0"), sem("hidden_done1")]
        gelu_ready = [sem("gelu_ready0"), sem("gelu_ready1")]
        hid_step = [sem("hid_step0"), sem("hid_step1")]
        hid_ready = [sem("hid_ready0"), sem("hid_ready1")]
        down_done = [sem("down_done0"), sem("down_done1")]
        y_step = [sem("y_step0"), sem("y_step1")]
        y_ready = sem("y_ready")
        y_stored = [sem("y_stored0"), sem("y_stored1")]

        waited = [sem("waited_vector"), sem("waited_pool"), sem("waited_sync")]

        block = stack.enter_context(nc.Block())

        def at(first, n):
            return slice(first, first + n) if isinstance(first, int) else ds(first, n)

        def raw(e):
            return weights[:, at(e + 1, 1), :].bitcast(F32).rearrange("p a b -> p (a b)")

        def part(e, first, n):
            return weights[:, at(e, 1), first:first + n].rearrange("p a b -> p (a b)")

        def ctx_tile(m, q):
            return raw(E - 1)[:, D * (2 * m + q):D * (2 * m + q + 1)]

        def row(b, first, n):
            return rows[:, at(b, 1), first:first + n].rearrange("p a b -> p (a b)")

        def windows(v, first, step):
            return bass.AP(tensor=v.tensor, offset=v.offset + first, ap=[v.ap[0], [step, 3], [1, HD]])

        def has(n, low, high):
            return not isinstance(n, int) or low <= n < high

        def peeled(eng, body, first, loop_first, loop_last, last):
            for i in range(first, loop_first):
                body(i)
            with eng.Fori(loop_first, loop_last) as i:
                body(i)
            for i in range(loop_last, last):
                body(i)

        def in_twos(eng, body, first, stop, last):
            twos = (stop - first) // 2
            for i in range(first):
                body(i, i % 2)
            with eng.Fori(first // 2, first // 2 + twos) as j:
                for m in range(2):
                    body(2 * j + m, m)
            for i in range(first + 2 * twos, last):
                body(i, i % 2)

        def in_fours(eng, body, first, stop, last):
            fours = (stop - first) // 4
            for s in range(first):
                body(s, s % 4)
            with eng.Fori(first // 4, first // 4 + fours) as i:
                for u in range(4):
                    body(4 * i + u, u)
            for s in range(first + 4 * fours, last):
                body(s, s % 4)

        class TileExperts:
            def __init__(self, eng):
                self.eng = eng
                self.regs = [eng.alloc_register(f"expert{u}") for u in range(4)]

            def load(self, s, u):
                self.eng.reg_load(self.regs[u % 4], tile_expert[0:1, at(s, 1)])
                return self.of(u)

            def of(self, u):
                return self.eng.snap(self.regs[u % 4], min_val=0, max_val=E - 1)

        GATE_LOADS, SMALL_LOADS = 4, 3
        SCORE_DMAS = G + 3

        @block.sync
        def _(sp):
            def load(landed, source, i, q, target):
                if has(i, 1, PAIRS):
                    sp.wait_ge(landed[q], 16 * i)
                    sp.sem_inc(waited[2], 1)
                sp.dma_start(target, source[at(2 * i + q, 1)].rearrange("a s d -> (a s) d")).then_inc(landed[q], 16)

            def loads(i, m):
                for q in range(2):
                    if has(i, 0, PAIRS - 1):
                        load(x_in, x, i + 1, q, row(2 * (i + 1) + q, 0, D))
                    if has(i, 2, PAIRS):
                        sp.wait_ge(cols_done, 2 * i + q - 3)
                        sp.sem_inc(waited[2], 1)
                    load(ctx_landed, ctx_in, i, q, ctx_tile(m, q))
                if isinstance(i, int) and i < 2:
                    weight_load(i, 0)
                    weight_load(i, 1)

            def weight_load(e, j):
                landed, source, n = ((w1_in, w1_v, KC), (w2_in, w2_v, FC))[j]
                if e > 0:
                    sp.wait_ge(landed, 16 * e)
                sp.dma_start(raw(e)[:, HALF * j:HALF * (j + 1)].rearrange("p (n d) -> p n d", n=n),
                             source[e]).then_inc(landed, 16)

            for q in range(2):
                load(x_in, x, 0, q, row(q, 0, D))
            in_twos(sp, loads, 2, PAIRS - 1, PAIRS)

            def qk_loads(i, q):
                b = 2 * i + q
                if has(i, 1, PAIRS):
                    sp.wait_ge(scores_done, KC * (b - 1))
                one = transposed_dram[at(b, 1)].rearrange("a p c -> (a p) c")
                for g in range(G):
                    sp.dma_start(q_diag[HD * g:HD * (g + 1), q, :].rearrange("p (k c) -> p k c", k=KC)[
                                     :, :, P * g:P * (g + 1)],
                                 one[HD * g:HD * (g + 1), 0:D].rearrange("p (k s) -> p k s", k=KC)
                                 ).then_inc(scores_in[q], 16)
                sp.dma_start(k_cols[:, q, :], one[:, D:2 * D]).then_inc(scores_in[q], 16)

            def exponent_loads(i, q):
                b = 2 * i + q
                sp.dma_start(add_rhs[3 * G:3 * G + 3, q, :].rearrange("m (h i) -> m h i", i=P),
                             negmax_dram[:, at(NH * b, NH), :]).then_inc(scores_in[q], 16)
                sp.dma_start(add_lhs[0:3 * G, q, :].rearrange("r (k i) -> r k i", k=KC),
                             decay_dram[at(NH * b, NH)].rearrange("(k g) m j -> (g m) k j", k=KC)
                             ).then_inc(scores_in[q], 16)

            def v_load(i, q):
                b = 2 * i + q
                if has(i, 1, PAIRS):
                    sp.wait_ge(heads_done, b - 1)
                sp.dma_start(v_tile[:, q, 0:D],
                             ctx_in[at(b, 1)].rearrange("a s d -> (a s) d")).then_inc(v_in[q], 16)

            def attention(i):
                early = isinstance(i, int) and i + 3 < E
                if early:
                    weight_load(i + 3, 0)
                if has(i, 1, PAIRS):
                    qk_loads(i, 0)
                    exponent_loads(i, 0)
                if has(i, 2, PAIRS + 1):
                    v_load(i - 1, 1)
                if early:
                    weight_load(i + 3, 1)
                if has(i, 1, PAIRS):
                    qk_loads(i, 1)
                    exponent_loads(i, 1)
                    v_load(i, 0)
                if has(i, 3, PAIRS + 3):
                    x1_store(i - 3)
                if has(i, 4, PAIRS + 4):
                    normed_store(i - 4)

            def x1_store(j):
                if has(j, 1, PAIRS):
                    sp.wait_ge(x1_stored, 16 * j)
                    sp.sem_inc(waited[2], 1)
                sp.wait_ge(x1_ready, j + 1)
                sp.sem_inc(waited[2], 1)
                sp.dma_start(out[at(2 * j, 2)].rearrange("b s d -> s b d"),
                             rows[:, at(2 * j, 2), :]).then_inc(x1_stored, 16)

            def normed_store(j):
                if has(j, 1, PAIRS):
                    sp.wait_ge(normed_stored, 16 * j)
                    sp.sem_inc(waited[2], 1)
                sp.wait_ge(normed_ready, j + 1)
                sp.sem_inc(waited[2], 1)
                sp.dma_start(normed_dram.rearrange("(b s) d -> b s d", s=P)[at(2 * j, 2)].rearrange("b s d -> s b d"),
                             normed).then_inc(normed_stored, 16)

            sp.wait_ge(presets_ready, 1)
            for q in range(2):
                v_load(0, q)
            for q in range(2):
                sp.wait_ge(cols_stored[q], 16 * PAIRS)
            qk_loads(0, 0)
            qk_loads(0, 1)
            weight_load(2, 0)
            weight_load(2, 1)
            sp.wait_ge(neg_ready, 1)
            sp.dma_start(negmax_dram.rearrange("m r i -> r m i"), neg_parts).then_inc(parts_stored, 16)
            sp.wait_ge(a_ready, 1)
            sp.dma_start(decay_dram, a_parts).then_inc(parts_stored, 16)
            sp.wait_ge(parts_stored, 32)
            for q in range(2):
                exponent_loads(0, q)
            attention(0)
            peeled(sp, attention, 1, 5, PAIRS, PAIRS + 4)

            sp.wait_ge(row_in[0], 16)
            sp.dma_start(b2_rows.rearrange("p e d -> p (e d)"),
                         b2.rearrange("e d -> (e d)").partition_broadcast(P)).then_inc(b2_in, 16)
            for q in range(2):
                sp.wait_ge(y_stored[q], 16 * ((TILES + 1 - q) // 2))

        @block.gpsimd
        def _(pool):
            chain = [0]

            def link(ins):
                chain[0] += 1
                ins.then_inc(pool_step, 1)
                pool.wait_ge(pool_step, chain[0])

            nc.gpsimd.memset(eps_col[:, 0:1], LN_EPS)
            nc.gpsimd.memset(eps_col[:, 1:2], 1e-6).then_inc(eps_ready, 1)
            nc.gpsimd.memset(ident[:], 0.0)
            nc.gpsimd.memset(ones32[:], 1.0)
            nc.gpsimd.memset(onesb[:], 1.0)
            link(nc.gpsimd.memset(mask[:], 0.0))
            nc.gpsimd.affine_select(out=ident[:], in_=ident[:], compare_op=ALU.not_equal, fill=1.0, base=0,
                                    pattern=[[-1, P]], channel_multiplier=1).then_inc(ident_ready, 1)
            nc.gpsimd.affine_select(out=upto[:], in_=ones32[:], compare_op=ALU.is_ge, fill=0.0, base=0,
                                    pattern=[[1, P]], channel_multiplier=-1)
            nc.gpsimd.affine_select(out=before[:], in_=onesb[:], compare_op=ALU.is_gt, fill=0.0, base=0,
                                    pattern=[[1, P]], channel_multiplier=-1)
            nc.gpsimd.affine_select(out=mask[:], in_=mask[:], compare_op=ALU.is_ge, fill=MASKED, base=0,
                                    pattern=[[0, G], [1, P]], channel_multiplier=-1)
            pool.wait_ge(ident_ready, 1)
            nc.gpsimd.tensor_copy(ident16[:], ident[:])
            nc.gpsimd.tensor_copy(identb[:], ident[:])
            ind = add_rhs[0:3 * G, :, :].rearrange("p q (k g s) -> p (q k) g s", k=KC, g=G)
            link(nc.gpsimd.memset(add_rhs[0:3 * G, :, :], 1.0))
            link(nc.gpsimd.affine_select(out=ind, in_=ind, compare_op=ALU.is_ge, fill=0.0, base=0,
                                         pattern=[[0, 2 * KC], [-3, G], [0, P]], channel_multiplier=1))
            link(nc.gpsimd.affine_select(out=ind, in_=ind, compare_op=ALU.is_ge, fill=0.0, base=2,
                                         pattern=[[0, 2 * KC], [3, G], [0, P]], channel_multiplier=-1))
            nc.gpsimd.memset(add_lhs[0:3 * G + 3, :, :], 1.0)
            nc.gpsimd.memset(v_tile[:, :, D:], 1.0)
            nc.gpsimd.memset(q_diag[:, :, :], 0.0).then_inc(presets_ready, 1)

            def lo(e, h):
                pool.wait_ge(hi_ready, 2 * e + h + 1)
                if not (isinstance(e, int) and e == 0):
                    pool.wait_ge(lo_ready, 2 * e)
                nc.gpsimd.tensor_tensor(part(e, W1LO + HALF * h, HALF), raw(e)[:, HALF * h:HALF * (h + 1)],
                                        part(e, W1HI + HALF * h, HALF), ALU.subtract).then_inc(lo_ready, 1)

            def residual(j):
                by_head = heads.rearrange("p q (h d) -> p (q h) d", h=NH)
                pool.wait_ge(rms_ready, j + 1)
                nc.gpsimd.tensor_tensor(
                    by_head, by_head,
                    head_rms[:].rearrange("p q h -> p (q h)").unsqueeze(2).broadcast_to([P, 2 * NH, HD]),
                    ALU.mult).then_inc(heads_normed, 1)
                pool.wait_ge(heads_normed, j + 1)
                pool.sem_inc(waited[1], 1)
                two = rows[:, at(2 * j, 2), :]
                nc.gpsimd.tensor_tensor(two, two, heads, ALU.add).then_inc(x1_ready, 1)

            def attention(i):
                if has(i, 2, PAIRS + 2):
                    residual(i - 2)
                if has(i, 1, E + 1):
                    for h in range(2):
                        lo(i - 1, h)

            peeled(pool, attention, 1, 2, PAIRS, PAIRS + 2)

            pool.wait_ge(heads_done, B)
            nc.gpsimd.iota(expert_no, pattern=[[0, B], [1, E]], base=0, channel_multiplier=0,
                           allow_small_or_imprecise_dtypes=True)
            nc.gpsimd.iota(tile_edge, pattern=[[0, E], [P, B]], base=0, channel_multiplier=0,
                           allow_small_or_imprecise_dtypes=True)
            nc.gpsimd.iota(tile_no, pattern=[[1, 32], [0, E]], base=0, channel_multiplier=0,
                           allow_small_or_imprecise_dtypes=True)
            nc.gpsimd.iota(place_no, pattern=[[1, P]], base=0, channel_multiplier=0,
                           allow_small_or_imprecise_dtypes=True)
            nc.gpsimd.iota(slot_no, pattern=[[1, TP]], base=0, channel_multiplier=0,
                           allow_small_or_imprecise_dtypes=True)
            nc.gpsimd.iota(values[:, :, 0], pattern=[[P, B]], base=1, channel_multiplier=1,
                           allow_small_or_imprecise_dtypes=True).then_inc(numbers_ready, 1)

            pool.wait_ge(numbers_ready, 1)
            pool.wait_ge(in_tile_ready, 1)
            nc.gpsimd.tensor_tensor(spread, in_tile.unsqueeze(2).broadcast_to([P, B, 4, TP]),
                                    values.unsqueeze(3).broadcast_to([P, B, 4, TP]),
                                    ALU.mult).then_inc(spread_ready, 1)

            last_token = pool.to_reg(N - 1)

            def gather(s, u, index):
                pool.indirect_dma_start(out=row_ring[:, u, :], out_offset=None, in_=normed_dram,
                                        in_offset=bass.IndirectOffsetOnAxis(ap=index, axis=0),
                                        bounds_check=last_token, oob_is_err=False).then_inc(row_in[u], 16)

            def move_rows(s, u):
                if has(s, 0, TILES - 4):
                    pool.wait_ge(tok_ready, s + 1)
                    pool.sem_inc(waited[1], 1)
                    gather(s + 4, u, gather_now[:, u:u + 1])
                if has(s, 4, TILES + 4):
                    pool.wait_ge(y_ready, s - 3)
                    pool.sem_inc(waited[1], 1)
                    pool.indirect_dma_start(out=out_f, out_offset=bass.IndirectOffsetOnAxis(
                        ap=scatter_now[:, u:u + 1], axis=0), in_=y_tile[:, u % 2, :], in_offset=None,
                        bounds_check=last_token, oob_is_err=False,
                        compute_op=ALU.add).then_inc(y_stored[u % 2], 16)

            pool.wait_ge(normed_stored, 16 * PAIRS)
            pool.wait_ge(x1_stored, 16 * PAIRS)
            pool.wait_ge(route_ready, 1)
            for s in range(4):
                gather(s, s, gather_u[:, s:s + 1])
            in_fours(pool, move_rows, 4, TILES - 4, TILES + 4)

        @block.scalar
        def _(act):
            act.preload_act_table_set("natural_log_exp_and_others")
            for j, (w, bias) in enumerate(((ig_w, ig_b), (fg_w, fg_b))):
                act.dma_start(gate_raw.rearrange("p m (k h) -> p (m k) h", k=KC)[:, :, NH * j:NH * (j + 1)],
                              w.rearrange("(c p) h -> p c h", p=P)).then_inc(gate_w_in, 16)
                act.dma_start(gate_bias[:, j, :], bias.partition_broadcast(P)).then_inc(gate_w_in, 16)

            def rstd(i):
                last = moments[:, :, 1]
                act.wait_ge(moments_done, i + 1)
                nc.scalar.activation(last, last, ACT.Ln, bias=eps_col[:, 0:1]).then_inc(ln_done, 1)
                act.wait_ge(ln_done, i + 1)
                nc.scalar.activation(last, last, ACT.Exp, scale=-0.5).then_inc(rstd_ready, 1)

            def norm_pair(i):
                if has(i, 0, PAIRS):
                    rstd(i)
                if has(i, 1, PAIRS + 1):
                    columns(i - 1)

            def columns(i):
                for q in range(2):
                    t = 2 * i + q
                    act.wait_ge(cols_done, t + 1)
                    if not (isinstance(i, int) and i == 0):
                        act.wait_ge(gates_done, t - 1)
                        act.wait_ge(cols_stored[q], 16 * i)
                    nc.scalar.activation(t_cols[:, q, :], cols_ps[q], ACT.Copy).then_inc(cols_ready, 1)
                    act.wait_ge(cols_ready, t + 1)
                    act.dma_start(transposed_dram[at(t, 1)].rearrange("a p c -> (a p) c"),
                                  t_cols[:, q, :]).then_inc(cols_stored[q], 16)

            def squares(e, j):
                act.wait_ge((w1_in, w2_in)[j], 16 * (e + 1))
                if j == 0 and has(e, 1, E):
                    act.wait_ge(logits_done, e)
                if j == 1 or not (isinstance(e, int) and e == 0):
                    act.wait_ge(sq_done, 2 * e + j)
                nc.scalar.activation(junk, raw(e)[:, HALF * j:HALF * (j + 1)], ACT.Square,
                                     accum_out=partial_sums[:, j:j + 1]).then_inc(sq_done, 1)

            act.wait_ge(eps_ready, 1)
            norm_pair(0)
            act.dma_start(router_w[:, :, 0:E], sw_w.rearrange("(k p) e -> p k e", p=P)).then_inc(consts_in, 16)
            act.dma_start(b1_rows[0:E * FC, :], b1.rearrange("e (c p) -> (e c) p", p=P)).then_inc(consts_in, 16)
            act.dma_start(router_bias[:], sw_b.partition_broadcast(P)).then_inc(consts_in, 16)
            peeled(act, norm_pair, 1, 2, PAIRS, PAIRS + 1)
            act.wait_ge(b1_done, 1)
            nc.scalar.activation(b1_cols[:], b1_ps[:, 0:E * FC], ACT.Copy).then_inc(b1_ready, 1)

            squares(0, 0)
            squares(0, 1)
            act.wait_ge(magnitude_ready, 1)
            nc.scalar.activation(decayed, magnitude, ACT.Exp).then_inc(act2, 1)
            act.wait_ge(act2, 1)
            nc.scalar.activation(log1p, decayed, ACT.Ln, bias=1.0).then_inc(act2, 1)
            act.wait_ge(cum_max_turned, 1)
            nc.scalar.activation(exp_negmax[:], cmt_ps, ACT.Exp, scale=-1.0).then_inc(exp_negmax_ready, 1)

            def decays(b, q):
                for k in range(KC):
                    act.wait_ge(add_done, KC * b + k + 1)
                    if k == 0 and not (isinstance(b, int) and b < 2):
                        act.wait_ge(heads_done, b - 1)
                    nc.scalar.activation(decay[:, q, G * P * k:G * P * (k + 1)], add_ps[k],
                                         ACT.Exp).then_inc(decay_ready, 1)

            def hi(e, h):
                act.wait_ge(scaled, 2 * e + h + 1)
                if h == 0 and not (isinstance(e, int) and e == 0):
                    act.wait_ge(lo_ready, 2 * e - 1)
                nc.scalar.activation(part(e, W1HI + HALF * h, HALF), raw(e)[:, HALF * h:HALF * (h + 1)],
                                     ACT.Copy).then_inc(hi_ready, 1)

            def attention(i):
                if has(i, 0, PAIRS):
                    decays(2 * i, 0)
                if has(i, 1, E + 1):
                    hi(i - 1, 0)
                if has(i, 4, PAIRS + 4):
                    act.wait_ge(ncols_done, i - 3)
                    if has(i, 5, PAIRS + 4):
                        act.wait_ge(logits_done, i)
                    nc.scalar.activation(normed_cols, ncols_ps, ACT.Copy).then_inc(ncols_ready, 1)
                if has(i, 0, E - 1):
                    squares(i + 1, 0)
                if has(i, 0, PAIRS):
                    decays(2 * i + 1, 1)
                if has(i, 1, E + 1):
                    hi(i - 1, 1)
                if has(i, 0, E - 1):
                    squares(i + 1, 1)
                if has(i, 1, PAIRS + 1):
                    act.wait_ge(rms_sums, i)
                    nc.scalar.activation(head_rms[:], head_rms[:], ACT.Ln, scale=1.0 / HD,
                                         bias=eps_col[:, 1:2]).then_inc(rms_ln_done, 1)
                    act.wait_ge(rms_ln_done, i)
                    nc.scalar.activation(head_rms[:], head_rms[:], ACT.Exp, scale=-0.5).then_inc(rms_ready, 1)
                if has(i, 2, PAIRS + 2):
                    rstd(i - 2 + PAIRS)

            peeled(act, attention, 0, 5, PAIRS - 1, PAIRS + 4)

            act.wait_ge(diff_ready, 1)
            nc.scalar.activation(chance, diff, ACT.Exp).then_inc(chance_ready, 1)

            experts = TileExperts(act)

            def gelu(s, q):
                e = experts.load(s, q)
                for c in range(FC):
                    if c % 4 == 0:
                        act.wait_ge(hidden_done[c // 4], s + 1)
                        if not (isinstance(s, int) and s < 2):
                            act.wait_ge(hid_ready[c // 4], s - 1)
                    ins = nc.scalar.activation(
                        hidden[:, q, P * c:P * (c + 1)], hidden_ps[q][c // 4][:, P * (c % 4):P * (c % 4 + 1)],
                        ACT.Gelu_apprx_tanh, bias=b1_cols[:, ds(e * FC + c, 1)], scale=gelu_scale[:, ds(e, 1)])
                    if c % 4 == 3:
                        ins.then_inc(gelu_ready[c // 4], 1)

            act.wait_ge(scales_ready, 1)
            in_fours(act, lambda s, u: gelu(s, u % 2), 4, TILES, TILES)

        @block.tensor
        def _(pe):
            pe.wait_ge(ident_ready, 1)

            def turn(i, m, q):
                t = 2 * i + q
                pe.wait_ge(xn_ready, t + 1)
                pe.wait_ge(ctx_landed[q], 16 * (i + 1))
                if has(i, 1, PAIRS):
                    pe.wait_ge(cols_ready, t - 1)
                for k in range(KC):
                    nc.tensor.transpose(cols_ps[q][:, P * k:P * (k + 1)], xn_tile[:, q, P * k:P * (k + 1)],
                                        ident[:])
                for k in range(KC):
                    last = nc.tensor.transpose(cols_ps[q][:, D + P * k:D + P * (k + 1)],
                                               ctx_tile(m, q)[:, P * k:P * (k + 1)], ident[:])
                last.then_inc(cols_done, 1)

            def gate(i, q):
                t = 2 * i + q
                pe.wait_ge(cols_ready, t + 1)
                if not (isinstance(t, int) and t < 2):
                    pe.wait_ge(gates_read, t - 1)
                for m in range(2 * KC):
                    last = nc.tensor.matmul(gates_ps[q][:, 0:GW], t_cols[:, q, P * m:P * (m + 1)],
                                            gate_w[:, m, :], start=(m == 0), stop=(m == 2 * KC - 1))
                last.then_inc(gates_done, 1)

            def gates_pair(i, m):
                turn(i, m, 0)
                if has(i, 1, PAIRS):
                    gate(i - 1, 1)
                turn(i, m, 1)
                if has(i, 0, 1) and isinstance(i, int):
                    pe.wait_ge(gate_w_ready, 1)
                gate(i, 0)

            in_twos(pe, gates_pair, 2, PAIRS, PAIRS)
            gate(PAIRS - 1, 1)
            pe.wait_ge(consts_in, 16 * SMALL_LOADS)
            nc.tensor.transpose(b1_ps[:, 0:E * FC], b1_rows[0:E * FC, :],
                                ident[0:E * FC, 0:E * FC]).then_inc(b1_done, 1)

            pe.wait_ge(presets_ready, 1)
            pe.wait_ge(log_forget_ready, 1)
            nc.tensor.matmul(cum_ps, log_forget, upto[:], start=True, stop=True)
            nc.tensor.transpose(igt_ps, gates[:, 0, :], ident[:]).then_inc(gates_turned, 1)
            pe.wait_ge(cum_max_ready, 1)
            nc.tensor.transpose(cmt_ps, cum_max, ident[:]).then_inc(cum_max_turned, 1)

            def sums(e):
                pe.wait_ge(sq_done, 2 * (e + 1))
                return nc.tensor.matmul(logit_ps[:, SUMS:SUMS + 2], ones32[:], partial_sums[:],
                                        start=True, stop=True)

            def scores(i, q):
                b = 2 * i + q
                pe.wait_ge(scores_in[q], 16 * SCORE_DMAS * (i + 1))
                for k in range(KC):
                    if not (isinstance(b, int) and b == 0):
                        pe.wait_ge(decay_ready, KC * (b - 1) + k + 1)
                    nc.tensor.matmul(add_ps[k], identb[:], mask[:].rearrange("p g s -> p (g s)"),
                                     start=True, stop=False)
                    nc.tensor.matmul(add_ps[k], add_lhs[0:3 * G + 3, q, P * k:P * (k + 1)],
                                     add_rhs[0:3 * G + 3, q, G * P * k:G * P * (k + 1)],
                                     start=False, stop=True).then_inc(add_done, 1)
                for k in range(KC):
                    if not (isinstance(b, int) and b == 0):
                        pe.wait_ge(product_ready, KC * (b - 1) + k + 1)
                    nc.tensor.matmul(score_ps[k], k_cols[:, q, P * k:P * (k + 1)],
                                     q_diag[:, q, G * P * k:G * P * (k + 1)],
                                     start=True, stop=True).then_inc(scores_done, 1)

            def values(i, q):
                b = 2 * i + q
                pe.wait_ge(product_ready, KC * (b + 1))
                pe.wait_ge(v_in[q], 16 * (i + 1))
                if not (isinstance(b, int) and b < 2):
                    pe.wait_ge(heads_scaled, i)
                for h in range(NH):
                    halfway = (D - HD * h) // 2
                    moving = windows(v_tile[:, q, :], HD * h, halfway)
                    target = windows(head_ps[q], HD * h, (ROW_SUM + 2 * h - HD * h) // 2)
                    last = nc.tensor.matmul(target, decay[:, q, P * h:P * (h + 1)], moving,
                                            start=True, stop=True)
                last.then_inc(heads_done, 1)

            def attention(i):
                if has(i, 0, E) or has(i, 5, PAIRS + 5):
                    if has(i, 1, PAIRS + 5):
                        pe.wait_ge(logits_read, i)
                    else:
                        pe.wait_ge(exp_negmax_ready, 1)
                if has(i, 5, PAIRS + 5):
                    pe.wait_ge(ncols_ready, i - 4)
                    for q in range(2):
                        for k in range(KC):
                            last = nc.tensor.matmul(
                                logit_ps[:, GW * q:GW * (q + 1)],
                                normed_cols[:, D * q + P * k:D * q + P * (k + 1)],
                                router_w[:, k, :], start=(k == 0), stop=(k == KC - 1))
                if has(i, 0, E):
                    last = sums(i)
                if has(i, 0, E) or has(i, 5, PAIRS + 5):
                    last.then_inc(logits_done, 1)
                if has(i, 4, PAIRS + 4):
                    pe.wait_ge(normed_ready, i - 3)
                    if has(i, 5, PAIRS + 4):
                        pe.wait_ge(ncols_ready, i - 4)
                    for q in range(2):
                        for k in range(KC):
                            last = nc.tensor.transpose(ncols_ps[:, D * q + P * k:D * q + P * (k + 1)],
                                                       normed[:, q, P * k:P * (k + 1)], ident[:])
                    last.then_inc(ncols_done, 1)
                if has(i, 0, PAIRS):
                    scores(i, 0)
                if has(i, 1, PAIRS + 1):
                    values(i - 1, 1)
                if has(i, 0, PAIRS):
                    scores(i, 1)
                    values(i, 0)

            peeled(pe, attention, 0, 5, PAIRS, PAIRS + 5)

            pe.wait_ge(onehot_ready, 1)
            nc.tensor.matmul(rank_ps, before[:], onehot_b, start=True, stop=True)
            nc.tensor.matmul(total_ps, onesb[:], onehot_b, start=True, stop=True).then_inc(ranks_done, 1)
            pe.wait_ge(b1_partial_ready, 1)
            nc.tensor.matmul(b1sum_ps, ones32[:], b1_partial[:], start=True, stop=True).then_inc(b1_summed, 1)
            pe.wait_ge(spread_ready, 1)
            for h in range(2):
                pe.wait_ge(at_place_ready, h + 1)
                for b in range(B // 2 * h, B // 2 * (h + 1)):
                    last = nc.tensor.matmul(chosen_ps, at_place[:, b, :], spread[:, b, :, :].rearrange("p v s -> p (v s)"),
                                            start=(b == 0), stop=(b == B - 1))
            last.then_inc(chosen_done, 1)
            pe.wait_ge(route_ready, 1)
            pe.wait_ge(lo_ready, 2 * E)

            def turn_tokens(s, q):
                pe.wait_ge(tok_ready, s + 1)
                if not (isinstance(s, int) and s < 2):
                    pe.wait_ge(tokc_ready, s - 1)
                for j in range(2):
                    for k in range(KC):
                        last = nc.tensor.transpose(tokc_ps[q][:, P * (KC * j + k):P * (KC * j + k + 1)],
                                                   tok16[:, q, D * j + P * k:D * j + P * (k + 1)], ident16[:])
                last.then_inc(tokc_done, 1)

            def up(s, q, e, c):
                if c == 0:
                    pe.wait_ge(tokc_ready, s + 1)
                    if not (isinstance(s, int) and s < 2):
                        pe.wait_ge(gelu_ready[1], s - 1)
                n = 0
                for w_at, parts in ((W1HI, (0, 1)), (W1LO, (0,))):
                    for k, j in [(k, j) for k in range(KC) for j in parts]:
                        last = nc.tensor.matmul(
                            hidden_ps[q][c // 4][:, P * (c % 4):P * (c % 4 + 1)],
                            part(e, w_at + F * k + P * c, P),
                            tok_cols[:, q, P * (KC * j + k):P * (KC * j + k + 1)],
                            start=(n == 0), stop=(n == 3 * KC - 1))
                        n += 1
                if c % 4 == 3:
                    last.then_inc(hidden_done[c // 4], 1)

            def down(s, q, e, c):
                if c == 0 and not (isinstance(s, int) and s < 2):
                    pe.wait_ge(y_ready, s - 1)
                if c % 4 == 0:
                    pe.wait_ge(hid_ready[c // 4], s + 1)
                both = weights[:, at(e, 1), :].rearrange("p a (m n) -> p (a m) n", m=4)
                for j, out_, w in ((0, y_ps[q], both[:, 1::2, D * c:D * (c + 1)]),
                                   (1, y_ps[q][:, 0:D], both[:, 1, D * c:D * (c + 1)]))[::-1 if c == FC - 1 else 1]:
                    last = nc.tensor.matmul(out_, hid16[:, q, FC * P * j + P * c:FC * P * j + P * (c + 1)], w,
                                            start=(c == 0 and j == 0), stop=(c == FC - 1 and j == 0))
                if c % 4 == 3:
                    last.then_inc(down_done[c // 4], 1)

            experts = TileExperts(pe)

            def ffn(s, u):
                q = u % 2
                if has(s, 0, TILES):
                    e_up = experts.load(s, u)
                if has(s, 2, TILES + 2):
                    e_down = experts.of(u - 2)
                for c in range(FC):
                    if has(s, 0, TILES):
                        up(s, q, e_up, c)
                    if c == FC // 2 and has(s, 0, TILES - 1):
                        turn_tokens(s + 1, 1 - q)
                    if has(s, 2, TILES + 2):
                        down(s - 2, q, e_down, c)

            turn_tokens(0, 0)
            in_fours(pe, ffn, 4, TILES, TILES + 2)

        @block.vector
        def _(dve):
            steps = {}

            def link(sem_, ins):
                steps[sem_.name] = steps.get(sem_.name, 0) + 1
                ins.then_inc(sem_, 1)
                dve.wait_ge(sem_, steps[sem_.name])

            nc.vector.memset(router_w[:, :, E:], 0.0)
            nc.vector.memset(gate_w[:, :, 2 * NH:], 0.0)

            def gate_weights():
                dve.wait_ge(gate_w_in, 16 * GATE_LOADS)
                nc.vector.tensor_copy(gate_w[:, 0:KC, 0:2 * NH],
                                      gate_raw[:, 0, :].rearrange("p (k h) -> p k h", k=KC))
                nc.vector.tensor_tensor(gate_w[:, KC:2 * KC, 0:2 * NH],
                                        gate_raw[:, 1, :].rearrange("p (k h) -> p k h", k=KC),
                                        gate_raw[:, 2, :].rearrange("p (k h) -> p k h", k=KC),
                                        ALU.add).then_inc(gate_w_ready, 1)

            def read_gates(i):
                for q in range(2):
                    t = 2 * i + q
                    dve.wait_ge(gates_done, t + 1)
                    nc.vector.tensor_tensor(gates[:, :, at(NH * t, NH)],
                                            gates_ps[q][:, 0:2 * NH].rearrange("p (j h) -> p j h", j=2),
                                            gate_bias[:], ALU.add).then_inc(gates_read, 1)

            def norm_pair(i):
                if has(i, 1, PAIRS + 1):
                    dve.wait_ge(rstd_ready, i)
                    for q in range(2):
                        t = 2 * (i - 1) + q
                        if has(i, 2, PAIRS + 1):
                            dve.wait_ge(cols_done, t - 1)
                        nc.vector.tensor_scalar(xn_tile[:, q, :], row(t, 0, D), moments[:, q, 0:1],
                                                moments[:, q, 1:2], ALU.subtract, ALU.mult).then_inc(xn_ready, 1)
                if has(i, 0, PAIRS):
                    if has(i, 1, PAIRS):
                        dve.wait_ge(moments_done, i)
                    for q in range(2):
                        dve.wait_ge(x_in[q], 16 * (i + 1))
                        dve.sem_inc(waited[0], 1)
                        ins = nc.vector.bn_stats(stat6[:, q, :], row(2 * i + q, 0, D))
                    ins.then_inc(stats_done, 1)
                    if has(i, 1, PAIRS):
                        dve.wait_ge(xn_ready, 2 * i)
                    dve.wait_ge(stats_done, i + 1)
                    dve.sem_inc(waited[0], 1)
                    for q in range(2):
                        ins = nc.vector.bn_aggr(moments[:, q, :], stat6[:, q, :])
                    ins.then_inc(moments_done, 1)
                if has(i, 2, PAIRS + 2):
                    read_gates(i - 2)

            norm_pair(0)
            norm_pair(1)
            gate_weights()
            peeled(dve, norm_pair, 2, 2, PAIRS, PAIRS + 2)

            dve.wait_ge(gates_read, B)
            nc.vector.scalar_tensor_tensor(magnitude, gates[:, 1, :], -1.0, gates[:, 1, :], ALU.mult,
                                           ALU.min).then_inc(magnitude_ready, 1)
            dve.wait_ge(act2, 2)
            nc.vector.scalar_tensor_tensor(log_forget, gates[:, 1, :], 0.0, log1p, ALU.min,
                                           ALU.subtract).then_inc(log_forget_ready, 1)
            dve.wait_ge(gates_turned, 1)
            link(vec2, nc.vector.tensor_copy(cum, cum_ps))
            link(vec2, nc.vector.tensor_tensor(a_rows, igt_ps, cum, ALU.subtract))
            link(vec2, nc.vector.tensor_tensor_scan(run_max, a_rows, a_rows, -3.0e38, ALU.max, ALU.max))
            nc.vector.tensor_tensor(cum_max, cum, run_max, ALU.add).then_inc(cum_max_ready, 1)
            for parts, source, sign, ready in ((neg_parts, run_max, -1.0, neg_ready), (a_parts, a_rows, 1.0, a_ready)):
                link(vec2, nc.vector.tensor_scalar(parts[:, 0, :], source, sign, None, ALU.mult))
                link(vec2, nc.vector.scalar_tensor_tensor(rest, source, sign, parts[:, 0, :],
                                                          ALU.mult, ALU.subtract))
                link(vec2, nc.vector.tensor_copy(parts[:, 1, :], rest))
                nc.vector.tensor_tensor(parts[:, 2, :], rest, parts[:, 1, :], ALU.subtract).then_inc(ready, 1)
                dve.wait_ge(ready, 1)

            dve.wait_ge(consts_in, 16 * SMALL_LOADS)
            POST = 5

            def products(b, q):
                for k in range(KC):
                    dve.wait_ge(decay_ready, KC * b + k + 1)
                    dve.wait_ge(scores_done, KC * b + k + 1)
                    half = decay[:, q, G * P * k:G * P * (k + 1)]
                    nc.vector.scalar_tensor_tensor(half, score_ps[k], HD ** -0.5, half, ALU.mult,
                                                   ALU.mult).then_inc(product_ready, 1)

            def after_heads(j):
                n = [0]

                def chain(ins):
                    n[0] += 1
                    ins.then_inc(post, 1)
                    dve.wait_ge(post, POST * j + n[0])


                def divide():
                    dve.wait_ge(heads_done, 2 * j + 2)
                    for sign in (-1.0, 1.0):
                        for q in range(2):
                            sums = head_ps[q][:, ROW_SUM:ROW_SUM + 2 * NH:2]
                            other = exp_negmax[:, at(NH * (2 * j + q), NH)] if sign < 0 else head_norm[:, q, :]
                            ins = nc.vector.scalar_tensor_tensor(head_norm[:, q, :], sums, sign, other,
                                                                 ALU.mult, ALU.max)
                        chain(ins)
                    chain(nc.vector.tensor_scalar(head_norm[:], head_norm[:], 1e-6, None, ALU.add))
                    chain(nc.vector.reciprocal(head_norm[:], head_norm[:]))
                    if not (isinstance(j, int) and j == 0):
                        dve.wait_ge(x1_ready, j)
                    for q in range(2):
                        ins = nc.vector.tensor_tensor(
                            heads[:, q, :].rearrange("p (h d) -> p h d", h=NH),
                            head_ps[q][:, 0:D].rearrange("p (h d) -> p h d", h=NH),
                            head_norm[:, q, :].unsqueeze(2).broadcast_to([P, NH, HD]), ALU.mult)
                    ins.then_inc(heads_scaled, 1)

                def sum_squares():
                    dve.wait_ge(heads_scaled, j + 1)
                    both = heads.rearrange("p q d -> p (q d)")
                    chain(nc.vector.tensor_tensor(squared, both, both, ALU.mult))
                    nc.vector.tensor_reduce(head_rms[:].rearrange("p q h -> p (q h)"),
                                            squared.rearrange("p (h d) -> p h d", d=HD), AX_X,
                                            ALU.add).then_inc(rms_sums, 1)

                return divide, sum_squares

            def stats_x1(j):
                if not (isinstance(j, int) and j == 0):
                    dve.wait_ge(moments_done, PAIRS + j)
                    dve.wait_ge(normed_ready, j)
                dve.wait_ge(x1_ready, j + 1)
                dve.sem_inc(waited[0], 1)
                for q in range(2):
                    ins = nc.vector.bn_stats(stat6[:, q, :], row(2 * j + q, 0, D))
                ins.then_inc(stats_done, 1)
                dve.wait_ge(stats_done, PAIRS + j + 1)
                dve.sem_inc(waited[0], 1)
                for q in range(2):
                    ins = nc.vector.bn_aggr(moments[:, q, :], stat6[:, q, :])
                ins.then_inc(moments_done, 1)

            def norm_x1(j):
                dve.wait_ge(rstd_ready, PAIRS + j + 1)
                if not (isinstance(j, int) and j == 0):
                    dve.wait_ge(ncols_done, j)
                    dve.wait_ge(normed_stored, 16 * j)
                for q in range(2):
                    ins = nc.vector.tensor_scalar(normed[:, q, :], row(2 * j + q, 0, D), moments[:, q, 0:1],
                                                  moments[:, q, 1:2], ALU.subtract, ALU.mult)
                ins.then_inc(normed_ready, 1)

            def attention(i):
                if has(i, 0, PAIRS):
                    products(2 * i, 0)
                divide = sum_squares = lambda: None
                if has(i, 1, PAIRS + 1):
                    divide, sum_squares = after_heads(i - 1)
                if has(i, 3, PAIRS + 3):
                    norm_x1(i - 3)
                if has(i, 2, PAIRS + 2):
                    stats_x1(i - 2)
                if has(i, 0, E) or has(i, 5, PAIRS + 5):
                    dve.wait_ge(logits_done, i + 1)
                if has(i, 5, PAIRS + 5):
                    ins = nc.vector.tensor_tensor(
                        logits[:, at(2 * (i - 5), 2), :],
                        logit_ps[:, 0:2 * GW].rearrange("p (q e) -> p q e", q=2)[:, :, 0:E],
                        router_bias[:].unsqueeze(1).broadcast_to([P, 2, E]), ALU.add)
                if has(i, 0, E):
                    nc.vector.tensor_copy(square_sums[:, at(i, 1), :].rearrange("p a j -> p (a j)"),
                                          logit_ps[:, SUMS:SUMS + 2])
                    ins = nc.vector.tensor_scalar(exponent[:], logit_ps[:, SUMS:SUMS + 2].bitcast(I32), 24, None,
                                                  ALU.logical_shift_right)
                if has(i, 0, E) or has(i, 5, PAIRS + 5):
                    ins.then_inc(logits_read, 1)
                if has(i, 0, E):
                    dve.wait_ge(logits_read, i + 1)
                    scale = weight_scale[:, at(i, 1), :].rearrange("p a j -> p (a j)")
                    nc.vector.tensor_scalar(scale.bitcast(I32), exponent[:], -float(1 << 23), float(204 << 23),
                                            ALU.mult, ALU.add).then_inc(scale_ready, 1)
                divide()
                if has(i, 0, PAIRS):
                    products(2 * i + 1, 1)
                sum_squares()
                if has(i, 0, E):
                    dve.wait_ge(scale_ready, i + 1)
                    for j in range(2):
                        words = raw(i)[:, HALF * j:HALF * (j + 1)]
                        nc.vector.tensor_scalar(words, words, scale[:, j:j + 1], None, ALU.mult).then_inc(scaled, 1)

            peeled(dve, attention, 0, 5, PAIRS, PAIRS + 5)

            dve.wait_ge(logits_read, PAIRS + 5)
            by_tile = lambda v: v.rearrange("p (b e) -> p b e", e=E)
            wide = lambda v: v.unsqueeze(2).broadcast_to([P, B, E])
            link(vec4, nc.vector.tensor_reduce(top, logits[:], AX_X, ALU.max))
            nc.vector.tensor_tensor(by_tile(diff), logits[:], wide(top), ALU.subtract).then_inc(diff_ready, 1)
            dve.wait_ge(diff_ready, 1)
            dve.wait_ge(numbers_ready, 1)
            link(vec4, nc.vector.tensor_scalar(key, diff, 0.0, float(E), ALU.is_lt, ALU.mult))
            link(vec4, nc.vector.tensor_tensor(key, key, expert_no, ALU.add))
            link(vec4, nc.vector.tensor_reduce(smallest, by_tile(key), AX_X, ALU.min))
            link(vec4, nc.vector.tensor_tensor(by_tile(onehot), by_tile(expert_no), wide(smallest), ALU.is_equal))
            nc.vector.tensor_copy(onehot_b, onehot).then_inc(onehot_ready, 1)
            dve.wait_ge(chance_ready, 1)
            link(vec4, nc.vector.tensor_reduce(total, by_tile(chance), AX_X, ALU.add))
            link(vec4, nc.vector.reciprocal(prob, total))
            link(vec4, nc.vector.tensor_copy(values[:, :, 1], prob))
            link(vec4, nc.vector.tensor_tensor(prob, prob, values[:, :, 1], ALU.subtract))
            link(vec4, nc.vector.tensor_copy(values[:, :, 2], prob))
            nc.vector.tensor_tensor(values[:, :, 3], prob, values[:, :, 2], ALU.subtract)
            dve.wait_ge(b1_ready, 1)
            link(vec4, nc.vector.tensor_tensor(spare[:, 0:E * FC], b1_cols[:], b1_cols[:], ALU.mult))
            nc.vector.tensor_reduce(b1_partial[:], spare[:, 0:E * FC].rearrange("p (e c) -> p e c", e=E), AX_X,
                                    ALU.add).then_inc(b1_partial_ready, 1)
            def scales():
                dve.wait_ge(b1_summed, 1)
                bound, bits, inverse = scale_tmp[:, 0, :], scale_tmp[:, 1, :].bitcast(I32), scale_tmp[:, 2, :]
                link(vec4, nc.vector.tensor_scalar(bound, square_sums[:, :, 0], 256.0, None, ALU.mult))
                link(vec4, nc.vector.tensor_tensor(bound, b1sum_ps, bound, ALU.add))
                link(vec4, nc.vector.tensor_scalar(bound, bound, 2.0, None, ALU.mult))
                link(vec4, nc.vector.tensor_scalar(bits, bound.bitcast(I32), 24, None, ALU.logical_shift_right))
                link(vec4, nc.vector.tensor_scalar(hidden_scale[:].bitcast(I32), bits, -float(1 << 23), float(204 << 23),
                                                   ALU.mult, ALU.add))
                link(vec4, nc.vector.reciprocal(inverse, weight_scale[:, :, 0]))
                link(vec4, nc.vector.tensor_scalar(gelu_scale[:], inverse, 1.0 / TOKEN_SCALE, None, ALU.mult))
                link(vec4, nc.vector.reciprocal(inverse, hidden_scale[:]))
                link(vec4, nc.vector.reciprocal(bound, weight_scale[:, :, 1]))
                nc.vector.tensor_tensor(y_scale[:], inverse, bound, ALU.mult).then_inc(scales_ready, 1)
            by_expert = lambda v: v.rearrange("p (e b) -> p e b", e=E)
            wide_e = lambda v: v.unsqueeze(2).broadcast_to([P, E, B])
            dve.wait_ge(ranks_done, 1)
            nc.vector.memset(zeros128, 0.0)
            link(vec4, nc.vector.tensor_copy(by_expert(totals_et), by_tile(total_ps).rearrange("p b e -> p e b")))
            link(vec4, nc.vector.tensor_tensor_scan(scan, totals_et, zeros128, 0.0, ALU.add, ALU.add))
            link(vec4, nc.vector.tensor_tensor(inside, scan, totals_et, ALU.subtract))
            link(vec4, nc.vector.tensor_tensor(counts, by_expert(scan)[:, :, B - 1], by_expert(inside)[:, :, 0],
                                               ALU.subtract))
            link(vec4, nc.vector.tensor_tensor(by_expert(spare), by_expert(tile_edge), wide_e(counts), ALU.is_lt))
            link(vec4, nc.vector.tensor_reduce(run_tiles, by_expert(spare), AX_X, ALU.add))
            link(vec4, nc.vector.tensor_tensor_scan(run_end, run_tiles, zeros128[:, 0:E], 0.0, ALU.add, ALU.add))
            link(vec4, nc.vector.tensor_tensor(run_start, run_end, run_tiles, ALU.subtract))
            link(vec4, nc.vector.tensor_scalar(run_start, run_start, float(P), None, ALU.mult))
            link(vec4, nc.vector.tensor_tensor(run_start, run_start, by_expert(inside)[:, :, 0], ALU.subtract))
            link(vec4, nc.vector.tensor_tensor(by_expert(base_et), by_expert(inside), wide_e(run_start), ALU.add))
            link(vec4, nc.vector.tensor_tensor(by_tile(place), by_tile(rank_ps),
                                               by_expert(base_et).rearrange("p e b -> p b e"), ALU.add))
            link(vec4, nc.vector.tensor_tensor(place, place, onehot, ALU.mult))
            link(vec4, nc.vector.tensor_reduce(position, by_tile(place), AX_X, ALU.add))
            link(vec4, nc.vector.tensor_copy(position_i, position))
            link(vec4, nc.vector.tensor_scalar(position_i, position_i, P.bit_length() - 1, None,
                                               ALU.logical_shift_right))
            link(vec4, nc.vector.tensor_copy(tile_f, position_i))
            nc.vector.tensor_tensor(in_tile, slot_no.unsqueeze(1).broadcast_to([P, B, TP]),
                                    tile_f.unsqueeze(2).broadcast_to([P, B, TP]),
                                    ALU.is_equal).then_inc(in_tile_ready, 1)
            link(vec4, nc.vector.scalar_tensor_tensor(place_f, tile_f, -float(P), position, ALU.mult, ALU.add))
            for h in range(2):
                half = slice(B // 2 * h, B // 2 * (h + 1))
                nc.vector.tensor_tensor(at_place[:, half, :], place_no.unsqueeze(1).broadcast_to([P, B // 2, P]),
                                        place_f[:, half].unsqueeze(2).broadcast_to([P, B // 2, P]),
                                        ALU.is_equal).then_inc(at_place_ready, 1)
            link(vec4, nc.vector.tensor_tensor(slot_cmp, run_end.unsqueeze(1).broadcast_to([P, 32, E]), tile_no,
                                               ALU.is_le))
            link(vec4, nc.vector.tensor_reduce(tile_expert_f, slot_cmp, AX_X, ALU.add))
            nc.vector.tensor_scalar(tile_expert[:], tile_expert_f, float(E - 1), None, ALU.min)
            dve.wait_ge(chosen_done, 1)
            link(vec4, nc.vector.tensor_copy(chosen, chosen_ps))
            number = chosen[:, 0:TP]
            nc.vector.tensor_scalar(gather_u[:], number, -1.0, 0.0, ALU.add, ALU.max).then_inc(route_ready, 1)
            link(vec4, nc.vector.tensor_scalar(target_f, number, 0.5, float(NOWHERE), ALU.is_lt, ALU.mult))
            link(vec4, nc.vector.scalar_tensor_tensor(target_f, number, -1.0, target_f, ALU.add, ALU.add))
            nc.vector.tensor_copy(scatter_u[:], target_f)
            link(vec4, nc.vector.tensor_reduce(probs[:], chosen[:, TP:].rearrange("p (v s) -> p s v", v=3), AX_X,
                                               ALU.add))
            scales()
            dve.wait_ge(route_ready, 1)
            dve.wait_ge(scales_ready, 1)

            def tokens(s, u):
                q = u % 2
                dve.wait_ge(row_in[u], 4 * (s - u) + 16)
                if not (isinstance(s, int) and s < 2):
                    dve.wait_ge(tokc_done, s - 1)
                nc.vector.tensor_scalar(tok16[:, q, 0:D], row_ring[:, u, :], TOKEN_SCALE, None,
                                        ALU.mult).then_inc(tok_step, 1)
                if has(s, 0, TILES - 4):
                    nc.vector.tensor_copy(gather_now[:, u:u + 1], gather_u[:, at(s + 4, 1)])
                dve.wait_ge(tok_step, s + 1)
                nc.vector.scalar_tensor_tensor(tok16[:, q, D:2 * D], row_ring[:, u, :], TOKEN_SCALE,
                                               tok16[:, q, 0:D], ALU.mult, ALU.subtract).then_inc(tok_ready, 1)

            def token_cols(s, q):
                dve.wait_ge(tokc_done, s + 1)
                if not (isinstance(s, int) and s < 2):
                    dve.wait_ge(hidden_done[1], s - 1)
                nc.vector.tensor_copy(tok_cols[:, q, :], tokc_ps[q]).then_inc(tokc_ready, 1)

            def split_hidden(s, q, e, h):
                dve.wait_ge(gelu_ready[h], s + 1)
                if not (isinstance(s, int) and s < 2):
                    dve.wait_ge(down_done[h], s - 1)
                a, b = FC * P // 2 * h, FC * P // 2 * (h + 1)
                nc.vector.tensor_scalar(hid16[:, q, a:b], hidden[:, q, a:b], hidden_scale[:, ds(e, 1)], None,
                                        ALU.mult).then_inc(hid_step[h], 1)
                dve.wait_ge(hid_step[h], s + 1)
                nc.vector.scalar_tensor_tensor(hid16[:, q, FC * P + a:FC * P + b], hidden[:, q, a:b],
                                               hidden_scale[:, ds(e, 1)], hid16[:, q, a:b],
                                               ALU.mult, ALU.subtract).then_inc(hid_ready[h], 1)

            def finish(s, u, e):
                q = u % 2
                dve.wait_ge(down_done[1], s + 1)
                if not (isinstance(s, int) and s < 2):
                    dve.wait_ge(y_stored[q], 16 * (s // 2))
                nc.vector.scalar_tensor_tensor(y_tile[:, q, :], y_ps[q][:, D:], y_scale[:, ds(e, 1)],
                                               b2_rows[:, ds(e, 1), :].rearrange("p a d -> p (a d)"),
                                               ALU.mult, ALU.add).then_inc(y_step[0], 1)
                nc.vector.tensor_copy(scatter_now[:, u:u + 1], scatter_u[:, at(s, 1)])
                dve.wait_ge(y_step[0], s + 1)
                nc.vector.scalar_tensor_tensor(y_tile[:, q, :], y_ps[q][:, 0:D], y_scale[:, ds(e, 1)],
                                               y_tile[:, q, :], ALU.mult, ALU.add).then_inc(y_step[1], 1)
                dve.wait_ge(y_step[1], s + 1)
                nc.vector.tensor_scalar(y_tile[:, q, :], y_tile[:, q, :], probs[:, at(s, 1)], None,
                                        ALU.mult).then_inc(y_ready, 1)

            experts = TileExperts(dve)

            def ffn(s, u):
                q = u % 2
                if has(s, 3, TILES + 3):
                    finish(s - 3, (u - 3) % 4, experts.of(u - 3))
                if has(s, 1, TILES + 1):
                    split_hidden(s - 1, 1 - q, experts.of(u - 1), 1)
                if has(s, 0, TILES - 2):
                    tokens(s + 2, (u + 2) % 4)
                if has(s, 0, TILES - 1):
                    token_cols(s + 1, 1 - q)
                if has(s, 0, TILES):
                    split_hidden(s, q, experts.load(s, u), 0)

            tokens(0, 0)
            tokens(1, 1)
            token_cols(0, 0)
            dve.wait_ge(b2_in, 16)
            in_fours(dve, ffn, 4, TILES - 6, TILES + 3)


_INS = ['x', 'ctx_1024', 'L0_xattn_igate_kernel', 'L0_xattn_igate_bias', 'L0_xattn_fgate_kernel',
        'L0_xattn_fgate_bias', 'L0_ffn_switch_w', 'L0_ffn_switch_b', 'L0_ffn_w1', 'L0_ffn_b1', 'L0_ffn_w2',
        'L0_ffn_b2']
_OUTS = [((16, 128, 256), 'float32')]


def kernel(**inputs):
    import numpy as _np
    import concourse.bacc as _bacc
    from concourse import mybir as _mybir
    from concourse.bass_utils import run_bass_kernel_spmd as _run

    nc = _bacc.Bacc("TRN2", target_bir_lowering=False, num_devices=1)
    arrays, args = {}, []
    for name in _INS:
        a = _np.ascontiguousarray(inputs[name])
        arrays[f"in_{name}_dram"] = a
        args.append(nc.dram_tensor(f"in_{name}_dram", a.shape, _mybir.dt.from_np(a.dtype), kind="ExternalInput").ap())
    for i, (shape, dtype) in enumerate(_OUTS):
        dt = _mybir.dt.from_np(_np.dtype(dtype))
        args.append(nc.dram_tensor(f"out_{i}_dram", shape, dt, kind="ExternalOutput").ap())
    xattn_ffn_kernel(nc, *args)
    r = _run(nc, [arrays], core_ids=[0])
    got = tuple(r.results[0][f"out_{i}_dram"] for i in range(len(_OUTS)))
    return got[0]
```

```python
from contextlib import ExitStack

import concourse.bass as bass
from concourse import mybir

ALU = mybir.AluOpType
ACT = mybir.ActivationFunctionType
AX_X = mybir.AxisListType.X
F32 = mybir.dt.float32
F16 = mybir.dt.float16
BF16 = mybir.dt.bfloat16
I32 = mybir.dt.int32
U32 = mybir.dt.uint32

P = 128
NH = 8
HD = 32
G = P // HD
LN_EPS = 1e-5
MASKED = -1e30
TOKEN_SCALE = 2048.0
GW = 96
ds = bass.ds


def xattn_ffn_kernel(nc, x, ctx_in, ig_w, ig_b, fg_w, fg_b, sw_w, sw_b, w1, b1, w2, b2, out):
    B, S, D = x.shape
    E, _, F = w1.shape
    N = B * S
    KC = D // P
    FC = F // P
    NT = N // P
    TILES = NT + E - 1
    BH = B * NH
    TP = TILES + 1
    NOWHERE = 2 * N
    PAIRS = B // 2
    HALF = KC * F
    W1HI, W1LO = 0, 2 * HALF
    assert TP % 2 == 0
    assert S == P and BH == P and KC == 2 and FC * D == HALF and E == PAIRS and E == NH

    out_f = out.rearrange("b s d -> (b s) d")
    w1_v = w1.rearrange("e (k p) f -> e p k f", p=P)
    w2_v = w2.rearrange("e (c p) d -> e p c d", p=P)

    transposed_dram = nc.dram_tensor("transposed_dram", (B, P, 2 * D), F32, kind="Internal").ap()
    negmax_dram = nc.dram_tensor("negmax_dram", (3, BH, P), BF16, kind="Internal").ap()
    decay_dram = nc.dram_tensor("decay_dram", (BH, 3, P), BF16, kind="Internal").ap()
    normed_dram = nc.dram_tensor("normed_dram", (N, D), F32, kind="Internal").ap()

    with ExitStack() as stack:
        def sb(name, shape, dt=F32):
            return stack.enter_context(nc.sbuf_tensor(name, shape, dt))

        def sem(name):
            return stack.enter_context(nc.semaphore(name))

        psum = stack.enter_context(nc.psum_tensor("psum", [P, 8, 512], F32))

        weights = sb("weights", [P, E + 1, 4 * HALF], F16)
        rows = sb("rows", [P, B, D])
        ident = sb("ident", [P, P])
        ident16 = sb("ident16", [P, P], F16)
        identb = sb("identb", [P, P], BF16)
        upto = sb("upto", [P, P])
        before = sb("before", [P, P], BF16)
        ones32 = sb("ones32", [P, P])
        onesb = sb("onesb", [P, P], BF16)
        mask = sb("mask", [P, G, P], BF16)
        gates = sb("gates", [P, 2, BH])
        exp_negmax = sb("exp_negmax", [P, BH])
        logits = sb("logits", [P, B, E])
        gate_bias = sb("gate_bias", [P, 2, NH])
        router_bias = sb("router_bias", [P, E])
        router_w = sb("router_w", [P, KC, GW])
        b1_cols = sb("b1_cols", [P, E * FC])
        square_sums = sb("square_sums", [P, E, 2])
        partial_sums = sb("partial_sums", [P, 2])
        head_norm = sb("head_norm", [P, 2, NH])
        head_rms = sb("head_rms", [P, 2, NH])
        weight_scale = sb("weight_scale", [P, E, 2])
        eps_col = sb("eps_col", [P, 2])
        exponent = sb("exponent", [P, 2], I32)
        tile_expert = sb("tile_expert", [P, 32], I32)
        stat6 = sb("stat6", [P, 2, 6])
        moments = sb("moments", [P, 2, 2])

        WORDS = 9536
        shared = sb("shared", [P, WORDS])

        class Region:
            def __init__(self, at=0):
                self.at = at

            def __call__(self, shape, dt=F32):
                n = 1
                for d in shape:
                    n *= d
                words = n * (2 if dt in (F16, BF16) else 4) // 4
                v = shared[:, self.at:self.at + words]
                self.at += words
                assert self.at <= WORDS
                if dt is not F32:
                    v = v.bitcast(dt)
                if len(shape) == 2:
                    v = v.rearrange("p (a b) -> p a b", a=shape[0])
                if len(shape) == 3:
                    v = v.rearrange("p (a b c) -> p a b c", a=shape[0], b=shape[1])
                return v

        r = Region()
        q_diag = r([2, KC * G * P])
        k_cols = r([2, KC * P])
        v_tile = r([2, D + HD])
        add_rhs = r([2, KC * G * P], BF16)
        add_lhs = r([2, KC * P], BF16)
        junk = r([HALF], F16)
        stage1_at = r.at
        decay = r([2, KC * G * P])
        heads = r([2, D])
        normed = r([2, D])
        normed_cols = r([2 * KC * P])
        squared = r([2 * D])
        r = Region(stage1_at)
        t_cols = r([4, 2 * D])
        xn_tile = r([2, D])
        gate_w = r([4, GW])
        gate_raw = r([3, KC * 2 * NH])
        b1_rows = r([P])
        r = Region(stage1_at + 8 * D)
        neg_parts = r([3, P], BF16)
        a_parts = r([3, P], BF16)
        magnitude, decayed, log1p, log_forget, cum, a_rows, run_max, rest, cum_max = (r([P]) for _ in range(9))
        r = Region()
        top, total, prob, position, smallest = (r([B]) for _ in range(5))
        diff, chance, key, onehot, place, totals_et, scan, inside, base_et, spare = (r([BH]) for _ in range(10))
        onehot_b = r([BH], BF16)
        zeros128 = r([P])
        expert_no = r([BH])
        tile_edge = r([P])
        tile_no = r([32, E])
        slot_cmp = r([32, E])
        tile_expert_f = r([32])
        counts, run_tiles, run_end, run_start = (r([E]) for _ in range(4))
        tile_f = r([B])
        tile16, place16 = r([B], F16), r([B], F16)
        position_i = r([B], I32)
        place_no, slot_no = r([P], F16), r([TP], F16)
        values = r([B, 4], F16)
        in_tile = r([B, TP], F16)
        at_place = r([B, P], F16)
        spread = shared[:, r.at:r.at + B * 4 * TP // 2].bitcast(F16).rearrange("p (b v s) -> p b v s", b=B, v=4)
        r.at += B * 4 * TP // 2
        chosen = r([4 * TP])
        target_f = r([TP])
        gather_u = sb("gather_u", [P, TP], U32)
        scatter_u = sb("scatter_u", [P, TP], U32)
        probs = sb("probs", [P, TP])
        gather_now = sb("gather_now", [P, 4], U32)
        scatter_now = sb("scatter_now", [P, 4], U32)
        r = Region()
        tok16 = r([2, 2 * D], F16)
        tok_cols = r([2, 2 * KC * P], F16)
        hidden = r([2, FC * P])
        hid16 = r([2, 2 * FC * P], F16)
        y_tile = r([2, D])
        row_ring = r([4, D])
        b2_rows = r([E, D])
        gelu_scale = sb("gelu_scale", [P, E])
        hidden_scale = sb("hidden_scale", [P, E])
        y_scale = sb("y_scale", [P, E])
        scale_tmp = sb("scale_tmp", [P, 3, E])
        b1_partial = sb("b1_partial", [P, E])
        b1_sums = sb("b1_sums", [P, E])

        cols_ps = [psum[:, 0, :], psum[:, 1, :]]
        gates_ps = [psum[:, 2, :], psum[:, 3, :]]
        b1_ps = psum[:, 4, :]
        cum_ps, igt_ps, cmt_ps = psum[:, 5, 0:P], psum[:, 6, 0:P], psum[:, 7, 0:P]
        add_ps = [psum[:, 0, :], psum[:, 1, :]]
        score_ps = [psum[:, 2, :], psum[:, 3, :]]
        head_ps = [psum[:, 4, :], psum[:, 5, :]]
        ncols_ps = psum[:, 6, :]
        logit_ps = psum[:, 7, :]
        ROW_SUM = 384
        SUMS = 448
        b1sum_ps = psum[:, 3, 0:E]
        rank_ps, total_ps = psum[:, 0, 0:P], psum[:, 1, 0:P]
        chosen_ps = psum[:, 2, 0:4 * TP]
        hidden_ps = [[psum[:, 0, :], psum[:, 1, :]], [psum[:, 2, :], psum[:, 3, :]]]
        tokc_ps = [psum[:, 4, 0:256].bitcast(F16), psum[:, 5, 0:256].bitcast(F16)]
        y_ps = [psum[:, 6, :], psum[:, 7, :]]

        gate_w_in = sem("gate_w_in")
        consts_in = sem("consts_in")
        pool_step = sem("pool_step")
        ident_ready = sem("ident_ready")
        b1_ready = sem("b1_ready")
        heads_scaled = sem("heads_scaled")
        normed_ready = sem("normed_ready")
        presets_ready = sem("presets_ready")
        x_in = [sem("x_in0"), sem("x_in1")]
        ctx_landed = [sem("ctx_landed0"), sem("ctx_landed1")]
        gate_w_ready = sem("gate_w_ready")
        stats_done = sem("stats_done")
        moments_done = sem("moments_done")
        ln_done = sem("ln_done")
        rstd_ready = sem("rstd_ready")
        eps_ready = sem("eps_ready")
        rms_sums = sem("rms_sums")
        rms_ln_done, rms_ready = sem("rms_ln_done"), sem("rms_ready")
        xn_ready = sem("xn_ready")
        cols_done = sem("cols_done")
        cols_ready = sem("cols_ready")
        cols_stored = [sem(f"cols_stored{n}") for n in range(4)]
        gates_done = sem("gates_done")
        gates_read = sem("gates_read")
        b1_done = sem("b1_done")
        vec2 = sem("vec2")
        act2 = sem("act2")
        magnitude_ready, log_forget_ready = sem("magnitude_ready"), sem("log_forget_ready")
        gates_turned, cum_max_ready = sem("gates_turned"), sem("cum_max_ready")
        cum_max_turned, exp_negmax_ready = sem("cum_max_turned"), sem("exp_negmax_ready")
        neg_ready, a_ready = sem("neg_ready"), sem("a_ready")
        parts_stored = sem("parts_stored")
        scores_in = [sem("scores_in0"), sem("scores_in1")]
        v_in = [sem("v_in0"), sem("v_in1")]
        add_done = sem("add_done")
        decay_ready = sem("decay_ready")
        scores_done = sem("scores_done")
        product_ready = sem("product_ready")
        heads_done = sem("heads_done")
        heads_normed = sem("heads_normed")
        x1_ready = sem("x1_ready")
        post = sem("post")
        ncols_done = sem("ncols_done")
        ncols_ready = sem("ncols_ready")
        logits_done = sem("logits_done")
        logits_read = sem("logits_read")
        w1_in, w2_in = sem("w1_in"), sem("w2_in")
        sq_done = sem("sq_done")
        scale_ready = sem("scale_ready")
        scaled = sem("scaled")
        hi_ready = sem("hi_ready")
        lo_ready = sem("lo_ready")
        vec4 = sem("vec4")
        diff_ready, chance_ready = sem("diff_ready"), sem("chance_ready")
        onehot_ready, ranks_done = sem("onehot_ready"), sem("ranks_done")
        b1_partial_ready, b1_summed = sem("b1_partial_ready"), sem("b1_summed")
        b1_sums_ready = sem("b1_sums_ready")
        numbers_ready = sem("numbers_ready")
        in_tile_ready, spread_ready = sem("in_tile_ready"), sem("spread_ready")
        at_place_ready, chosen_done = sem("at_place_ready"), sem("chosen_done")
        route_ready = sem("route_ready")
        scales_ready = sem("scales_ready")
        x1_stored = sem("x1_stored")
        normed_stored = sem("normed_stored")
        b2_in = sem("b2_in")
        row_in = [sem(f"row_in{u}") for u in range(4)]
        tok_step = sem("tok_step")
        tok_ready = sem("tok_ready")
        tokc_done = sem("tokc_done")
        tokc_ready = sem("tokc_ready")
        hidden_done = [sem("hidden_done0"), sem("hidden_done1")]
        gelu_ready = [sem("gelu_ready0"), sem("gelu_ready1")]
        hid_step = [sem("hid_step0"), sem("hid_step1")]
        hid_ready = [sem("hid_ready0"), sem("hid_ready1")]
        down_done = [sem("down_done0"), sem("down_done1")]
        y_step = [sem("y_step0"), sem("y_step1")]
        y_ready = sem("y_ready")
        y_stored = [sem("y_stored0"), sem("y_stored1")]

        waited = [sem("waited_vector"), sem("waited_pool"), sem("waited_sync")]

        block = stack.enter_context(nc.Block())

        def at(first, n):
            return slice(first, first + n) if isinstance(first, int) else ds(first, n)

        def raw(e):
            return weights[:, at(e + 1, 1), :].bitcast(F32).rearrange("p a b -> p (a b)")

        def part(e, first, n):
            return weights[:, at(e, 1), first:first + n].rearrange("p a b -> p (a b)")

        def ctx_tile(m, q):
            return raw(E - 1)[:, D * (2 * m + q):D * (2 * m + q + 1)]

        def row(b, first, n):
            return rows[:, at(b, 1), first:first + n].rearrange("p a b -> p (a b)")

        def windows(v, first, step):
            return bass.AP(tensor=v.tensor, offset=v.offset + first, ap=[v.ap[0], [step, 3], [1, HD]])

        def has(n, low, high):
            return not isinstance(n, int) or low <= n < high

        def peeled(eng, body, first, loop_first, loop_last, last):
            for i in range(first, loop_first):
                body(i)
            with eng.Fori(loop_first, loop_last) as i:
                body(i)
            for i in range(loop_last, last):
                body(i)

        def in_twos(eng, body, first, stop, last):
            twos = (stop - first) // 2
            for i in range(first):
                body(i, i % 2)
            with eng.Fori(first // 2, first // 2 + twos) as j:
                for m in range(2):
                    body(2 * j + m, m)
            for i in range(first + 2 * twos, last):
                body(i, i % 2)

        def in_fours(eng, body, first, stop, last):
            fours = (stop - first) // 4
            for s in range(first):
                body(s, s % 4)
            with eng.Fori(first // 4, first // 4 + fours) as i:
                for u in range(4):
                    body(4 * i + u, u)
            for s in range(first + 4 * fours, last):
                body(s, s % 4)

        def normed_of(j):
            return squared.rearrange("p (q d) -> p q d", q=2) if isinstance(j, int) and j == PAIRS - 2 else normed

        class TileExperts:
            def __init__(self, eng):
                self.eng = eng
                self.regs = [eng.alloc_register(f"expert{u}") for u in range(4)]

            def load(self, s, u):
                self.eng.reg_load(self.regs[u % 4], tile_expert[0:1, at(s, 1)])
                return self.of(u)

            def of(self, u):
                return self.eng.snap(self.regs[u % 4], min_val=0, max_val=E - 1)

        GATE_LOADS, SMALL_LOADS = 4, 3
        SCORE_DMAS = G + 3

        @block.sync
        def _(sp):
            def load(landed, source, i, q, target):
                if has(i, 1, PAIRS):
                    sp.wait_ge(landed[q], 16 * i)
                    sp.sem_inc(waited[2], 1)
                sp.dma_start(target, source[at(2 * i + q, 1)].rearrange("a s d -> (a s) d")).then_inc(landed[q], 16)

            def loads(i, m):
                for q in range(2):
                    if has(i, 0, PAIRS - 1):
                        load(x_in, x, i + 1, q, row(2 * (i + 1) + q, 0, D))
                    if has(i, 2, PAIRS):
                        sp.wait_ge(cols_done, 2 * i + q - 3)
                        sp.sem_inc(waited[2], 1)
                    load(ctx_landed, ctx_in, i, q, ctx_tile(m, q))
                if isinstance(i, int) and i == 0:
                    weight_load(0, 0)

            def weight_load(e, j):
                landed, source, n = ((w1_in, w1_v, KC), (w2_in, w2_v, FC))[j]
                if has(e, 1, E):
                    sp.wait_ge(landed, 16 * e)
                    sp.sem_inc(waited[2], 1)
                sp.dma_start(raw(e)[:, HALF * j:HALF * (j + 1)].rearrange("p (n d) -> p n d", n=n),
                             source[at(e, 1)].rearrange("a p n d -> (a p) n d")).then_inc(landed, 16)

            for q in range(2):
                load(x_in, x, 0, q, row(q, 0, D))
            in_twos(sp, loads, 2, PAIRS - 1, PAIRS)

            def qk_loads(i, q):
                b = 2 * i + q
                if has(i, 1, PAIRS):
                    sp.wait_ge(scores_done, KC * (b - 1))
                one = transposed_dram[at(b, 1)].rearrange("a p c -> (a p) c")
                for g in range(G):
                    sp.dma_start(q_diag[HD * g:HD * (g + 1), q, :].rearrange("p (k c) -> p k c", k=KC)[
                                     :, :, P * g:P * (g + 1)],
                                 one[HD * g:HD * (g + 1), 0:D].rearrange("p (k s) -> p k s", k=KC)
                                 ).then_inc(scores_in[q], 16)
                sp.dma_start(k_cols[:, q, :], one[:, D:2 * D]).then_inc(scores_in[q], 16)

            def exponent_loads(i, q):
                b = 2 * i + q
                sp.dma_start(add_rhs[3 * G:3 * G + 3, q, :].rearrange("m (h i) -> m h i", i=P),
                             negmax_dram[:, at(NH * b, NH), :]).then_inc(scores_in[q], 16)
                sp.dma_start(add_lhs[0:3 * G, q, :].rearrange("r (k i) -> r k i", k=KC),
                             decay_dram[at(NH * b, NH)].rearrange("(k g) m j -> (g m) k j", k=KC)
                             ).then_inc(scores_in[q], 16)

            def v_load(i, q):
                b = 2 * i + q
                if has(i, 1, PAIRS):
                    sp.wait_ge(heads_done, b - 1)
                sp.dma_start(v_tile[:, q, 0:D],
                             ctx_in[at(b, 1)].rearrange("a s d -> (a s) d")).then_inc(v_in[q], 16)

            def attention(i):
                if has(i, 1, PAIRS):
                    qk_loads(i, 0)
                    exponent_loads(i, 0)
                if has(i, 2, PAIRS + 1):
                    v_load(i - 1, 1)
                if has(i, 4, PAIRS + 4):
                    normed_store(i - 4)
                if has(i, 1, E - 1):
                    weight_load(i + 1, 0)
                if has(i, 1, PAIRS):
                    qk_loads(i, 1)
                    exponent_loads(i, 1)
                    v_load(i, 0)
                if has(i, 1, E - 1):
                    weight_load(i + 1, 1)

            def normed_store(j):
                if has(j, 1, PAIRS):
                    sp.wait_ge(normed_stored, 16 * j)
                    sp.sem_inc(waited[2], 1)
                sp.wait_ge(normed_ready, j + 1)
                sp.sem_inc(waited[2], 1)
                sp.dma_start(normed_dram.rearrange("(b s) d -> b s d", s=P)[at(2 * j, 2)].rearrange("b s d -> s b d"),
                             normed_of(j)).then_inc(normed_stored, 16)

            sp.wait_ge(presets_ready, 1)
            for q in range(2):
                v_load(0, q)
            weight_load(0, 1)
            for stored in cols_stored:
                sp.wait_ge(stored, 16 * PAIRS // 2)
            qk_loads(0, 0)
            sp.wait_ge(neg_ready, 1)
            sp.dma_start(negmax_dram.rearrange("m r i -> r m i"), neg_parts).then_inc(parts_stored, 16)
            sp.wait_ge(a_ready, 1)
            sp.dma_start(decay_dram, a_parts).then_inc(parts_stored, 16)
            qk_loads(0, 1)
            sp.wait_ge(parts_stored, 32)
            for q in range(2):
                exponent_loads(0, q)
            for j in range(2):
                weight_load(1, j)
            peeled(sp, attention, 1, 5, PAIRS - 1, PAIRS + 4)

            sp.wait_ge(x1_ready, PAIRS)
            sp.dma_start(out.rearrange("b s d -> s b d"), rows[:, :, :]).then_inc(x1_stored, 16)

            sp.wait_ge(row_in[3], 16)
            sp.dma_start(b2_rows.rearrange("p e d -> p (e d)"),
                         b2.rearrange("e d -> (e d)").partition_broadcast(P)).then_inc(b2_in, 16)
            for q in range(2):
                sp.wait_ge(y_stored[q], 16 * ((TILES + 1 - q) // 2))

        @block.gpsimd
        def _(pool):
            chain = [0]

            def link(ins):
                chain[0] += 1
                ins.then_inc(pool_step, 1)
                pool.wait_ge(pool_step, chain[0])

            nc.gpsimd.memset(eps_col[:, 0:1], LN_EPS)
            nc.gpsimd.memset(eps_col[:, 1:2], 1e-6).then_inc(eps_ready, 1)
            nc.gpsimd.memset(ident[:], 0.0)
            nc.gpsimd.memset(ones32[:], 1.0)
            nc.gpsimd.memset(onesb[:], 1.0)
            link(nc.gpsimd.memset(mask[:], 0.0))
            nc.gpsimd.affine_select(out=ident[:], in_=ident[:], compare_op=ALU.not_equal, fill=1.0, base=0,
                                    pattern=[[-1, P]], channel_multiplier=1).then_inc(ident_ready, 1)
            nc.gpsimd.affine_select(out=upto[:], in_=ones32[:], compare_op=ALU.is_ge, fill=0.0, base=0,
                                    pattern=[[1, P]], channel_multiplier=-1)
            nc.gpsimd.affine_select(out=before[:], in_=onesb[:], compare_op=ALU.is_gt, fill=0.0, base=0,
                                    pattern=[[1, P]], channel_multiplier=-1)
            nc.gpsimd.affine_select(out=mask[:], in_=mask[:], compare_op=ALU.is_ge, fill=MASKED, base=0,
                                    pattern=[[0, G], [1, P]], channel_multiplier=-1)
            pool.wait_ge(ident_ready, 1)
            nc.gpsimd.tensor_copy(ident16[:], ident[:])
            nc.gpsimd.tensor_copy(identb[:], ident[:])
            ind = add_rhs[0:3 * G, :, :].rearrange("p q (k g s) -> p (q k) g s", k=KC, g=G)
            link(nc.gpsimd.memset(add_rhs[0:3 * G, :, :], 1.0))
            link(nc.gpsimd.affine_select(out=ind, in_=ind, compare_op=ALU.is_ge, fill=0.0, base=0,
                                         pattern=[[0, 2 * KC], [-3, G], [0, P]], channel_multiplier=1))
            link(nc.gpsimd.affine_select(out=ind, in_=ind, compare_op=ALU.is_ge, fill=0.0, base=2,
                                         pattern=[[0, 2 * KC], [3, G], [0, P]], channel_multiplier=-1))
            nc.gpsimd.memset(add_lhs[0:3 * G + 3, :, :], 1.0)
            nc.gpsimd.memset(v_tile[:, :, D:], 1.0)
            nc.gpsimd.memset(q_diag[:, :, :], 0.0).then_inc(presets_ready, 1)

            def lo(e, h):
                pool.wait_ge(hi_ready, 2 * e + h + 1)
                if not (isinstance(e, int) and e == 0):
                    pool.wait_ge(lo_ready, 2 * e)
                nc.gpsimd.tensor_tensor(part(e, W1LO + HALF * h, HALF), raw(e)[:, HALF * h:HALF * (h + 1)],
                                        part(e, W1HI + HALF * h, HALF), ALU.subtract).then_inc(lo_ready, 1)

            def residual(j):
                by_head = heads.rearrange("p q (h d) -> p (q h) d", h=NH)
                pool.wait_ge(rms_ready, j + 1)
                nc.gpsimd.tensor_tensor(
                    by_head, by_head,
                    head_rms[:].rearrange("p q h -> p (q h)").unsqueeze(2).broadcast_to([P, 2 * NH, HD]),
                    ALU.mult).then_inc(heads_normed, 1)
                pool.wait_ge(heads_normed, j + 1)
                pool.sem_inc(waited[1], 1)
                two = rows[:, at(2 * j, 2), :]
                nc.gpsimd.tensor_tensor(two, two, heads, ALU.add).then_inc(x1_ready, 1)

            def attention(i):
                if has(i, 2, PAIRS):
                    residual(i - 2)
                lo(i - 1, 0)
                if has(i, 1, PAIRS - 1):
                    lo(i - 1, 1)

            peeled(pool, attention, 1, 2, PAIRS - 1, PAIRS)
            residual(PAIRS - 2)
            residual(PAIRS - 1)

            pool.wait_ge(heads_done, B)
            nc.gpsimd.iota(expert_no, pattern=[[0, B], [1, E]], base=0, channel_multiplier=0,
                           allow_small_or_imprecise_dtypes=True)
            nc.gpsimd.iota(tile_edge, pattern=[[0, E], [P, B]], base=0, channel_multiplier=0,
                           allow_small_or_imprecise_dtypes=True)
            nc.gpsimd.iota(tile_no, pattern=[[1, 32], [0, E]], base=0, channel_multiplier=0,
                           allow_small_or_imprecise_dtypes=True)
            nc.gpsimd.iota(place_no, pattern=[[1, P]], base=0, channel_multiplier=0,
                           allow_small_or_imprecise_dtypes=True)
            nc.gpsimd.iota(slot_no, pattern=[[1, TP]], base=0, channel_multiplier=0,
                           allow_small_or_imprecise_dtypes=True)
            nc.gpsimd.iota(values[:, :, 0], pattern=[[P, B]], base=1, channel_multiplier=1,
                           allow_small_or_imprecise_dtypes=True).then_inc(numbers_ready, 1)

            lo(E - 2, 1)
            lo(E - 1, 0)
            lo(E - 1, 1)

            pool.wait_ge(numbers_ready, 1)
            pool.wait_ge(in_tile_ready, 1)
            nc.gpsimd.tensor_tensor(spread, in_tile.unsqueeze(2).broadcast_to([P, B, 4, TP]),
                                    values.unsqueeze(3).broadcast_to([P, B, 4, TP]),
                                    ALU.mult).then_inc(spread_ready, 1)

            last_token = pool.to_reg(N - 1)

            def gather(s, u, index):
                pool.indirect_dma_start(out=row_ring[:, u, :], out_offset=None, in_=normed_dram,
                                        in_offset=bass.IndirectOffsetOnAxis(ap=index, axis=0),
                                        bounds_check=last_token, oob_is_err=False).then_inc(row_in[u], 16)

            def move_rows(s, u):
                if has(s, 0, TILES - 4):
                    pool.wait_ge(tok_ready, s + 1)
                    pool.sem_inc(waited[1], 1)
                    gather(s + 4, u, gather_now[:, u:u + 1])
                if has(s, 4, TILES + 4):
                    pool.wait_ge(y_ready, s - 3)
                    pool.sem_inc(waited[1], 1)
                    pool.indirect_dma_start(out=out_f, out_offset=bass.IndirectOffsetOnAxis(
                        ap=scatter_now[:, u:u + 1], axis=0), in_=y_tile[:, u % 2, :], in_offset=None,
                        bounds_check=last_token, oob_is_err=False,
                        compute_op=ALU.add).then_inc(y_stored[u % 2], 16)

            pool.wait_ge(normed_stored, 16 * PAIRS)
            pool.wait_ge(x1_stored, 16)
            pool.wait_ge(route_ready, 1)
            for s in range(4):
                gather(s, s, gather_u[:, s:s + 1])
            in_fours(pool, move_rows, 4, TILES - 4, TILES + 4)

        @block.scalar
        def _(act):
            act.preload_act_table_set("natural_log_exp_and_others")
            for j, (w, bias) in enumerate(((ig_w, ig_b), (fg_w, fg_b))):
                act.dma_start(gate_raw.rearrange("p m (k h) -> p (m k) h", k=KC)[:, :, NH * j:NH * (j + 1)],
                              w.rearrange("(c p) h -> p c h", p=P)).then_inc(gate_w_in, 16)
                act.dma_start(gate_bias[:, j, :], bias.partition_broadcast(P)).then_inc(gate_w_in, 16)

            def rstd(i):
                last = moments[:, :, 1]
                act.wait_ge(moments_done, i + 1)
                nc.scalar.activation(last, last, ACT.Ln, bias=eps_col[:, 0:1]).then_inc(ln_done, 1)
                act.wait_ge(ln_done, i + 1)
                nc.scalar.activation(last, last, ACT.Exp, scale=-0.5).then_inc(rstd_ready, 1)

            def norm_pair(i, m):
                if has(i, 1, PAIRS + 1):
                    columns(i - 1, 1 - m, 0)
                if has(i, 0, PAIRS):
                    rstd(i)
                if isinstance(i, int) and i == 0:
                    act.dma_start(router_w[:, :, 0:E], sw_w.rearrange("(k p) e -> p k e", p=P)).then_inc(consts_in, 16)
                    act.dma_start(b1_rows[0:E * FC, :], b1.rearrange("e (c p) -> (e c) p", p=P)).then_inc(consts_in, 16)
                    act.dma_start(router_bias[:], sw_b.partition_broadcast(P)).then_inc(consts_in, 16)
                if has(i, 1, PAIRS + 1):
                    columns(i - 1, 1 - m, 1)

            def columns(i, m, q):
                t = 2 * i + q
                n = 2 * m + q
                act.wait_ge(cols_done, t + 1)
                if not (isinstance(i, int) and i < 2):
                    act.wait_ge(gates_done, t - 3)
                    act.wait_ge(cols_stored[n], 8 * (i - m))
                nc.scalar.activation(t_cols[:, n, :], cols_ps[q], ACT.Copy).then_inc(cols_ready, 1)
                act.wait_ge(cols_ready, t + 1)
                act.dma_start(transposed_dram[at(t, 1)].rearrange("a p c -> (a p) c"),
                              t_cols[:, n, :]).then_inc(cols_stored[n], 16)

            def squares(e, j):
                act.wait_ge((w1_in, w2_in)[j], 16 * (e + 1))
                if j == 0 and has(e, 1, E):
                    act.wait_ge(logits_done, e)
                if j == 1 or not (isinstance(e, int) and e == 0):
                    act.wait_ge(sq_done, 2 * e + j)
                nc.scalar.activation(junk, raw(e)[:, HALF * j:HALF * (j + 1)], ACT.Square,
                                     accum_out=partial_sums[:, j:j + 1]).then_inc(sq_done, 1)

            act.wait_ge(eps_ready, 1)
            in_twos(act, norm_pair, 4, PAIRS, PAIRS + 1)
            act.wait_ge(b1_done, 1)
            nc.scalar.activation(b1_cols[:], b1_ps[:, 0:E * FC], ACT.Copy).then_inc(b1_ready, 1)

            act.wait_ge(magnitude_ready, 1)
            nc.scalar.activation(decayed, magnitude, ACT.Exp).then_inc(act2, 1)
            act.wait_ge(act2, 1)
            nc.scalar.activation(log1p, decayed, ACT.Ln, bias=1.0).then_inc(act2, 1)
            squares(0, 0)
            act.wait_ge(cum_max_turned, 1)
            nc.scalar.activation(exp_negmax[:], cmt_ps, ACT.Exp, scale=-1.0).then_inc(exp_negmax_ready, 1)
            squares(0, 1)

            def decays(b, q):
                for k in range(KC):
                    act.wait_ge(add_done, KC * b + k + 1)
                    if k == 0 and not (isinstance(b, int) and b < 2):
                        act.wait_ge(heads_done, b - 1)
                    nc.scalar.activation(decay[:, q, G * P * k:G * P * (k + 1)], add_ps[k],
                                         ACT.Exp).then_inc(decay_ready, 1)

            def hi(e, h):
                act.wait_ge(scaled, 2 * e + h + 1)
                if h == 0 and not (isinstance(e, int) and e == 0):
                    act.wait_ge(lo_ready, 2 * e - 1)
                nc.scalar.activation(part(e, W1HI + HALF * h, HALF), raw(e)[:, HALF * h:HALF * (h + 1)],
                                     ACT.Copy).then_inc(hi_ready, 1)

            def x1_cols(j):
                act.wait_ge(ncols_done, j + 1)
                if not (isinstance(j, int) and j == 0):
                    act.wait_ge(logits_done, j + 5)
                nc.scalar.activation(normed_cols, ncols_ps, ACT.Copy).then_inc(ncols_ready, 1)

            def rms(j):
                act.wait_ge(rms_sums, j + 1)
                nc.scalar.activation(head_rms[:], head_rms[:], ACT.Ln, scale=1.0 / HD,
                                     bias=eps_col[:, 1:2]).then_inc(rms_ln_done, 1)
                act.wait_ge(rms_ln_done, j + 1)
                nc.scalar.activation(head_rms[:], head_rms[:], ACT.Exp, scale=-0.5).then_inc(rms_ready, 1)

            def attention(i):
                decays(2 * i, 0)
                if has(i, 1, PAIRS):
                    hi(i - 1, 0)
                if has(i, 4, PAIRS):
                    x1_cols(i - 4)
                if has(i, 0, E - 1):
                    squares(i + 1, 0)
                decays(2 * i + 1, 1)
                if has(i, 1, PAIRS):
                    hi(i - 1, 1)
                if has(i, 0, E - 1):
                    squares(i + 1, 1)
                if has(i, 1, PAIRS):
                    rms(i - 1)
                if has(i, 2, PAIRS):
                    rstd(i - 2 + PAIRS)

            peeled(act, attention, 0, 5, PAIRS - 1, PAIRS)

            x1_cols(PAIRS - 4)
            hi(E - 1, 0)
            rms(PAIRS - 1)
            x1_cols(PAIRS - 3)
            rstd(2 * PAIRS - 2)
            x1_cols(PAIRS - 2)
            rstd(2 * PAIRS - 1)
            x1_cols(PAIRS - 1)

            act.wait_ge(diff_ready, 1)
            nc.scalar.activation(chance, diff, ACT.Exp).then_inc(chance_ready, 1)
            hi(E - 1, 1)
            act.preload_act_table_set("gelu_apprx_tanh_and_others")

            experts = TileExperts(act)

            def gelu(s, q):
                e = experts.load(s, q)
                for c in range(FC):
                    if c % 4 == 0:
                        act.wait_ge(hidden_done[c // 4], s + 1)
                        if not (isinstance(s, int) and s < 2):
                            act.wait_ge(hid_ready[c // 4], s - 1)
                    ins = nc.scalar.activation(
                        hidden[:, q, P * c:P * (c + 1)], hidden_ps[q][c // 4][:, P * (c % 4):P * (c % 4 + 1)],
                        ACT.Gelu_apprx_tanh, bias=b1_cols[:, ds(e * FC + c, 1)], scale=gelu_scale[:, ds(e, 1)])
                    if c % 4 == 3:
                        ins.then_inc(gelu_ready[c // 4], 1)

            act.wait_ge(scales_ready, 1)
            act.wait_ge(route_ready, 1)
            in_fours(act, lambda s, u: gelu(s, u % 2), 4, TILES, TILES)

        @block.tensor
        def _(pe):
            pe.wait_ge(ident_ready, 1)

            def turn(i, m, q):
                t = 2 * i + q
                pe.wait_ge(xn_ready, t + 1)
                pe.wait_ge(ctx_landed[q], 16 * (i + 1))
                if has(i, 1, PAIRS):
                    pe.wait_ge(cols_ready, t - 1)
                for k in range(KC):
                    nc.tensor.transpose(cols_ps[q][:, P * k:P * (k + 1)], xn_tile[:, q, P * k:P * (k + 1)],
                                        ident[:])
                for k in range(KC):
                    last = nc.tensor.transpose(cols_ps[q][:, D + P * k:D + P * (k + 1)],
                                               ctx_tile(m, q)[:, P * k:P * (k + 1)], ident[:])
                last.then_inc(cols_done, 1)

            def gate(i, m, q):
                t = 2 * i + q
                pe.wait_ge(cols_ready, t + 1)
                if not (isinstance(t, int) and t < 2):
                    pe.wait_ge(gates_read, t - 1)
                for k in range(2 * KC):
                    last = nc.tensor.matmul(gates_ps[q][:, 0:GW], t_cols[:, 2 * m + q, P * k:P * (k + 1)],
                                            gate_w[:, k, :], start=(k == 0), stop=(k == 2 * KC - 1))
                last.then_inc(gates_done, 1)

            def gates_pair(i, m):
                turn(i, m, 0)
                if has(i, 1, PAIRS):
                    gate(i - 1, 1 - m, 1)
                turn(i, m, 1)
                if has(i, 0, 1) and isinstance(i, int):
                    pe.wait_ge(gate_w_ready, 1)
                gate(i, m, 0)

            in_twos(pe, gates_pair, 2, PAIRS, PAIRS)
            gate(PAIRS - 1, 1, 1)
            pe.wait_ge(consts_in, 16 * SMALL_LOADS)
            nc.tensor.transpose(b1_ps[:, 0:E * FC], b1_rows[0:E * FC, :],
                                ident[0:E * FC, 0:E * FC]).then_inc(b1_done, 1)

            pe.wait_ge(presets_ready, 1)
            pe.wait_ge(log_forget_ready, 1)
            nc.tensor.matmul(cum_ps, log_forget, upto[:], start=True, stop=True)
            nc.tensor.transpose(igt_ps, gates[:, 0, :], ident[:]).then_inc(gates_turned, 1)
            pe.wait_ge(cum_max_ready, 1)
            nc.tensor.transpose(cmt_ps, cum_max, ident[:]).then_inc(cum_max_turned, 1)
            pe.wait_ge(b1_partial_ready, 1)
            nc.tensor.matmul(b1sum_ps, ones32[:], b1_partial[:], start=True, stop=True).then_inc(b1_summed, 1)
            pe.wait_ge(b1_sums_ready, 1)

            def sums(e):
                pe.wait_ge(sq_done, 2 * (e + 1))
                return nc.tensor.matmul(logit_ps[:, SUMS:SUMS + 2], ones32[:], partial_sums[:],
                                        start=True, stop=True)

            def scores(i, q):
                b = 2 * i + q
                pe.wait_ge(scores_in[q], 16 * SCORE_DMAS * (i + 1))
                for k in range(KC):
                    if not (isinstance(b, int) and b == 0):
                        pe.wait_ge(decay_ready, KC * (b - 1) + k + 1)
                    nc.tensor.matmul(add_ps[k], identb[:], mask[:].rearrange("p g s -> p (g s)"),
                                     start=True, stop=False)
                    nc.tensor.matmul(add_ps[k], add_lhs[0:3 * G + 3, q, P * k:P * (k + 1)],
                                     add_rhs[0:3 * G + 3, q, G * P * k:G * P * (k + 1)],
                                     start=False, stop=True).then_inc(add_done, 1)
                for k in range(KC):
                    if not (isinstance(b, int) and b == 0):
                        pe.wait_ge(product_ready, KC * (b - 1) + k + 1)
                    nc.tensor.matmul(score_ps[k], k_cols[:, q, P * k:P * (k + 1)],
                                     q_diag[:, q, G * P * k:G * P * (k + 1)],
                                     start=True, stop=True).then_inc(scores_done, 1)

            def values(i, q):
                b = 2 * i + q
                pe.wait_ge(product_ready, KC * (b + 1))
                pe.wait_ge(v_in[q], 16 * (i + 1))
                if not (isinstance(b, int) and b < 2):
                    pe.wait_ge(heads_scaled, i)
                for h in range(NH):
                    halfway = (D - HD * h) // 2
                    moving = windows(v_tile[:, q, :], HD * h, halfway)
                    target = windows(head_ps[q], HD * h, (ROW_SUM + 2 * h - HD * h) // 2)
                    last = nc.tensor.matmul(target, decay[:, q, P * h:P * (h + 1)], moving,
                                            start=True, stop=True)
                last.then_inc(heads_done, 1)

            def route(j):
                pe.wait_ge(ncols_ready, j + 1)
                for q in range(2):
                    for k in range(KC):
                        last = nc.tensor.matmul(
                            logit_ps[:, GW * q:GW * (q + 1)],
                            normed_cols[:, D * q + P * k:D * q + P * (k + 1)],
                            router_w[:, k, :], start=(k == 0), stop=(k == KC - 1))
                return last

            def turn_x1(j):
                pe.wait_ge(normed_ready, j + 1)
                if not (isinstance(j, int) and j == 0):
                    pe.wait_ge(ncols_ready, j)
                for q in range(2):
                    for k in range(KC):
                        last = nc.tensor.transpose(ncols_ps[:, D * q + P * k:D * q + P * (k + 1)],
                                                   normed_of(j)[:, q, P * k:P * (k + 1)], ident[:])
                last.then_inc(ncols_done, 1)

            def attention(i):
                scores(i, 0)
                if has(i, 1, PAIRS):
                    pe.wait_ge(logits_read, i)
                else:
                    pe.wait_ge(exp_negmax_ready, 1)
                if has(i, 5, PAIRS):
                    route(i - 5)
                sums(i).then_inc(logits_done, 1)
                if has(i, 4, PAIRS):
                    turn_x1(i - 4)
                if has(i, 1, PAIRS):
                    values(i - 1, 1)
                scores(i, 1)
                values(i, 0)

            peeled(pe, attention, 0, 5, PAIRS, PAIRS)

            values(PAIRS - 1, 1)
            for j in range(PAIRS - 5, PAIRS):
                pe.wait_ge(logits_read, j + 5)
                route(j).then_inc(logits_done, 1)
                if j + 1 < PAIRS:
                    turn_x1(j + 1)

            pe.wait_ge(onehot_ready, 1)
            nc.tensor.matmul(rank_ps, before[:], onehot_b, start=True, stop=True)
            nc.tensor.matmul(total_ps, onesb[:], onehot_b, start=True, stop=True).then_inc(ranks_done, 1)
            pe.wait_ge(spread_ready, 1)
            for h in range(2):
                pe.wait_ge(at_place_ready, h + 1)
                for b in range(B // 2 * h, B // 2 * (h + 1)):
                    last = nc.tensor.matmul(chosen_ps, at_place[:, b, :], spread[:, b, :, :].rearrange("p v s -> p (v s)"),
                                            start=(b == 0), stop=(b == B - 1))
            last.then_inc(chosen_done, 1)
            pe.wait_ge(route_ready, 1)
            pe.wait_ge(lo_ready, 2 * E)

            def turn_tokens(s, q):
                pe.wait_ge(tok_ready, s + 1)
                if not (isinstance(s, int) and s < 2):
                    pe.wait_ge(tokc_ready, s - 1)
                for j in range(2):
                    for k in range(KC):
                        last = nc.tensor.transpose(tokc_ps[q][:, P * (KC * j + k):P * (KC * j + k + 1)],
                                                   tok16[:, q, D * j + P * k:D * j + P * (k + 1)], ident16[:])
                last.then_inc(tokc_done, 1)

            def up(s, q, e, c):
                if c == 0:
                    pe.wait_ge(tokc_ready, s + 1)
                    if not (isinstance(s, int) and s < 2):
                        pe.wait_ge(gelu_ready[1], s - 1)
                n = 0
                for w_at, parts in ((W1HI, (0, 1)), (W1LO, (0,))):
                    for k, j in [(k, j) for k in range(KC) for j in parts]:
                        last = nc.tensor.matmul(
                            hidden_ps[q][c // 4][:, P * (c % 4):P * (c % 4 + 1)],
                            part(e, w_at + F * k + P * c, P),
                            tok_cols[:, q, P * (KC * j + k):P * (KC * j + k + 1)],
                            start=(n == 0), stop=(n == 3 * KC - 1))
                        n += 1
                if c % 4 == 3:
                    last.then_inc(hidden_done[c // 4], 1)

            def down(s, q, e, c):
                if c == 0 and not (isinstance(s, int) and s < 2):
                    pe.wait_ge(y_ready, s - 1)
                if c % 4 == 0:
                    pe.wait_ge(hid_ready[c // 4], s + 1)
                both = weights[:, at(e, 1), :].rearrange("p a (m n) -> p (a m) n", m=4)
                for j, out_, w in ((0, y_ps[q], both[:, 1::2, D * c:D * (c + 1)]),
                                   (1, y_ps[q][:, 0:D], both[:, 1, D * c:D * (c + 1)]))[::-1 if c == FC - 1 else 1]:
                    last = nc.tensor.matmul(out_, hid16[:, q, FC * P * j + P * c:FC * P * j + P * (c + 1)], w,
                                            start=(c == 0 and j == 0), stop=(c == FC - 1 and j == 0))
                if c % 4 == 3:
                    last.then_inc(down_done[c // 4], 1)

            experts = TileExperts(pe)

            def ffn(s, u):
                q = u % 2
                if has(s, 0, TILES):
                    e_up = experts.of(u)
                if has(s, 2, TILES + 2):
                    e_down = experts.of(u - 2)
                for c in range(FC):
                    if has(s, 0, TILES):
                        up(s, q, e_up, c)
                    if c == FC // 2 and has(s, 0, TILES - 1):
                        turn_tokens(s + 1, 1 - q)
                        experts.load(s + 1, u + 1)
                    if has(s, 2, TILES + 2):
                        down(s - 2, q, e_down, c)

            turn_tokens(0, 0)
            experts.load(0, 0)
            in_fours(pe, ffn, 4, TILES - 1, TILES + 2)

        @block.vector
        def _(dve):
            steps = {}

            def link(sem_, ins):
                steps[sem_.name] = steps.get(sem_.name, 0) + 1
                ins.then_inc(sem_, 1)
                dve.wait_ge(sem_, steps[sem_.name])

            nc.vector.memset(router_w[:, :, E:], 0.0)
            nc.vector.memset(gate_w[:, :, 2 * NH:], 0.0)

            def gate_weights():
                dve.wait_ge(gate_w_in, 16 * GATE_LOADS)
                nc.vector.tensor_copy(gate_w[:, 0:KC, 0:2 * NH],
                                      gate_raw[:, 0, :].rearrange("p (k h) -> p k h", k=KC))
                nc.vector.tensor_tensor(gate_w[:, KC:2 * KC, 0:2 * NH],
                                        gate_raw[:, 1, :].rearrange("p (k h) -> p k h", k=KC),
                                        gate_raw[:, 2, :].rearrange("p (k h) -> p k h", k=KC),
                                        ALU.add).then_inc(gate_w_ready, 1)

            def read_gates(i):
                for q in range(2):
                    t = 2 * i + q
                    dve.wait_ge(gates_done, t + 1)
                    nc.vector.tensor_tensor(gates[:, :, at(NH * t, NH)],
                                            gates_ps[q][:, 0:2 * NH].rearrange("p (j h) -> p j h", j=2),
                                            gate_bias[:], ALU.add).then_inc(gates_read, 1)

            def norm_pair(i):
                if has(i, 1, PAIRS + 1):
                    dve.wait_ge(rstd_ready, i)
                    for q in range(2):
                        t = 2 * (i - 1) + q
                        if has(i, 2, PAIRS + 1):
                            dve.wait_ge(cols_done, t - 1)
                        nc.vector.tensor_scalar(xn_tile[:, q, :], row(t, 0, D), moments[:, q, 0:1],
                                                moments[:, q, 1:2], ALU.subtract, ALU.mult).then_inc(xn_ready, 1)
                if has(i, 0, PAIRS):
                    if has(i, 1, PAIRS):
                        dve.wait_ge(moments_done, i)
                    for q in range(2):
                        dve.wait_ge(x_in[q], 16 * (i + 1))
                        dve.sem_inc(waited[0], 1)
                        ins = nc.vector.bn_stats(stat6[:, q, :], row(2 * i + q, 0, D))
                    ins.then_inc(stats_done, 1)
                    if has(i, 1, PAIRS):
                        dve.wait_ge(xn_ready, 2 * i)
                    dve.wait_ge(stats_done, i + 1)
                    dve.sem_inc(waited[0], 1)
                    for q in range(2):
                        ins = nc.vector.bn_aggr(moments[:, q, :], stat6[:, q, :])
                    ins.then_inc(moments_done, 1)
                if has(i, 2, PAIRS + 2):
                    read_gates(i - 2)

            norm_pair(0)
            norm_pair(1)
            gate_weights()
            peeled(dve, norm_pair, 2, 2, PAIRS, PAIRS + 2)

            dve.wait_ge(gates_read, B)
            nc.vector.scalar_tensor_tensor(magnitude, gates[:, 1, :], -1.0, gates[:, 1, :], ALU.mult,
                                           ALU.min).then_inc(magnitude_ready, 1)
            dve.wait_ge(act2, 2)
            nc.vector.scalar_tensor_tensor(log_forget, gates[:, 1, :], 0.0, log1p, ALU.min,
                                           ALU.subtract).then_inc(log_forget_ready, 1)
            dve.wait_ge(gates_turned, 1)
            link(vec2, nc.vector.tensor_copy(cum, cum_ps))
            link(vec2, nc.vector.tensor_tensor(a_rows, igt_ps, cum, ALU.subtract))
            link(vec2, nc.vector.tensor_tensor_scan(run_max, a_rows, a_rows, -3.0e38, ALU.max, ALU.max))
            nc.vector.tensor_tensor(cum_max, cum, run_max, ALU.add).then_inc(cum_max_ready, 1)
            for parts, source, sign, ready in ((neg_parts, run_max, -1.0, neg_ready), (a_parts, a_rows, 1.0, a_ready)):
                link(vec2, nc.vector.tensor_scalar(parts[:, 0, :], source, sign, None, ALU.mult))
                link(vec2, nc.vector.scalar_tensor_tensor(rest, source, sign, parts[:, 0, :],
                                                          ALU.mult, ALU.subtract))
                link(vec2, nc.vector.tensor_copy(parts[:, 1, :], rest))
                nc.vector.tensor_tensor(parts[:, 2, :], rest, parts[:, 1, :], ALU.subtract).then_inc(ready, 1)
                dve.wait_ge(ready, 1)

            dve.wait_ge(b1_ready, 1)
            link(vec2, nc.vector.tensor_tensor(rest[:, 0:E * FC], b1_cols[:], b1_cols[:], ALU.mult))
            nc.vector.tensor_reduce(b1_partial[:], rest[:, 0:E * FC].rearrange("p (e c) -> p e c", e=E), AX_X,
                                    ALU.add).then_inc(b1_partial_ready, 1)
            dve.wait_ge(b1_summed, 1)
            nc.vector.tensor_copy(b1_sums[:], b1sum_ps).then_inc(b1_sums_ready, 1)
            dve.wait_ge(consts_in, 16 * SMALL_LOADS)
            POST = 5

            def products(b, q):
                for k in range(KC):
                    dve.wait_ge(decay_ready, KC * b + k + 1)
                    dve.wait_ge(scores_done, KC * b + k + 1)
                    half = decay[:, q, G * P * k:G * P * (k + 1)]
                    nc.vector.scalar_tensor_tensor(half, score_ps[k], HD ** -0.5, half, ALU.mult,
                                                   ALU.mult).then_inc(product_ready, 1)

            def after_heads(j):
                n = [0]

                def chain(ins):
                    n[0] += 1
                    ins.then_inc(post, 1)
                    dve.wait_ge(post, POST * j + n[0])


                def divide():
                    dve.wait_ge(heads_done, 2 * j + 2)
                    for sign in (-1.0, 1.0):
                        for q in range(2):
                            sums = head_ps[q][:, ROW_SUM:ROW_SUM + 2 * NH:2]
                            other = exp_negmax[:, at(NH * (2 * j + q), NH)] if sign < 0 else head_norm[:, q, :]
                            ins = nc.vector.scalar_tensor_tensor(head_norm[:, q, :], sums, sign, other,
                                                                 ALU.mult, ALU.max)
                        chain(ins)
                    chain(nc.vector.tensor_scalar(head_norm[:], head_norm[:], 1e-6, None, ALU.add))
                    chain(nc.vector.reciprocal(head_norm[:], head_norm[:]))
                    if not (isinstance(j, int) and j == 0):
                        dve.wait_ge(x1_ready, j)
                    for q in range(2):
                        ins = nc.vector.tensor_tensor(
                            heads[:, q, :].rearrange("p (h d) -> p h d", h=NH),
                            head_ps[q][:, 0:D].rearrange("p (h d) -> p h d", h=NH),
                            head_norm[:, q, :].unsqueeze(2).broadcast_to([P, NH, HD]), ALU.mult)
                    ins.then_inc(heads_scaled, 1)

                def sum_squares():
                    dve.wait_ge(heads_scaled, j + 1)
                    both = heads.rearrange("p q d -> p (q d)")
                    chain(nc.vector.tensor_tensor(squared, both, both, ALU.mult))
                    nc.vector.tensor_reduce(head_rms[:].rearrange("p q h -> p (q h)"),
                                            squared.rearrange("p (h d) -> p h d", d=HD), AX_X,
                                            ALU.add).then_inc(rms_sums, 1)

                return divide, sum_squares

            def stats_x1(j):
                if not (isinstance(j, int) and j == 0):
                    dve.wait_ge(moments_done, PAIRS + j)
                    dve.wait_ge(normed_ready, j)
                dve.wait_ge(x1_ready, j + 1)
                dve.sem_inc(waited[0], 1)
                for q in range(2):
                    ins = nc.vector.bn_stats(stat6[:, q, :], row(2 * j + q, 0, D))
                ins.then_inc(stats_done, 1)
                dve.wait_ge(stats_done, PAIRS + j + 1)
                dve.sem_inc(waited[0], 1)
                for q in range(2):
                    ins = nc.vector.bn_aggr(moments[:, q, :], stat6[:, q, :])
                ins.then_inc(moments_done, 1)

            def norm_x1(j):
                dve.wait_ge(rstd_ready, PAIRS + j + 1)
                if not (isinstance(j, int) and j == 0):
                    before_it = j - 1 if isinstance(j, int) and j == PAIRS - 1 else j
                    dve.wait_ge(ncols_done, before_it)
                    dve.wait_ge(normed_stored, 16 * before_it)
                for q in range(2):
                    ins = nc.vector.tensor_scalar(normed_of(j)[:, q, :], row(2 * j + q, 0, D), moments[:, q, 0:1],
                                                  moments[:, q, 1:2], ALU.subtract, ALU.mult)
                ins.then_inc(normed_ready, 1)

            def take_logits(j):
                return nc.vector.tensor_tensor(
                    logits[:, at(2 * j, 2), :],
                    logit_ps[:, 0:2 * GW].rearrange("p (q e) -> p q e", q=2)[:, :, 0:E],
                    router_bias[:].unsqueeze(1).broadcast_to([P, 2, E]), ALU.add)

            def late_logits(j):
                dve.wait_ge(logits_done, j + 6)
                take_logits(j).then_inc(logits_read, 1)

            def scale_weights(e, j):
                words = raw(e)[:, HALF * j:HALF * (j + 1)]
                scale = weight_scale[:, at(e, 1), :].rearrange("p a j -> p (a j)")
                nc.vector.tensor_scalar(words, words, scale[:, j:j + 1], None, ALU.mult).then_inc(scaled, 1)

            def attention(i):
                products(2 * i, 0)
                divide = sum_squares = lambda: None
                if has(i, 1, PAIRS):
                    divide, sum_squares = after_heads(i - 1)
                if has(i, 3, PAIRS):
                    norm_x1(i - 3)
                divide()
                if has(i, 2, PAIRS):
                    stats_x1(i - 2)
                dve.wait_ge(logits_done, i + 1)
                if has(i, 5, PAIRS):
                    take_logits(i - 5)
                nc.vector.tensor_copy(square_sums[:, at(i, 1), :].rearrange("p a j -> p (a j)"),
                                      logit_ps[:, SUMS:SUMS + 2])
                nc.vector.tensor_scalar(exponent[:], logit_ps[:, SUMS:SUMS + 2].bitcast(I32), 24, None,
                                        ALU.logical_shift_right).then_inc(logits_read, 1)
                dve.wait_ge(logits_read, i + 1)
                scale = weight_scale[:, at(i, 1), :].rearrange("p a j -> p (a j)")
                nc.vector.tensor_scalar(scale.bitcast(I32), exponent[:], -float(1 << 23), float(204 << 23),
                                        ALU.mult, ALU.add).then_inc(scale_ready, 1)
                products(2 * i + 1, 1)
                sum_squares()
                dve.wait_ge(scale_ready, i + 1)
                scale_weights(i, 0)
                if has(i, 0, E - 1):
                    scale_weights(i, 1)

            def scales():
                dve.wait_ge(b1_sums_ready, 1)
                bound, bits, inverse = scale_tmp[:, 0, :], scale_tmp[:, 1, :].bitcast(I32), scale_tmp[:, 2, :]
                link(vec4, nc.vector.tensor_scalar(bound, square_sums[:, :, 0], 256.0, None, ALU.mult))
                link(vec4, nc.vector.tensor_tensor(bound, b1_sums[:], bound, ALU.add))
                link(vec4, nc.vector.tensor_scalar(bound, bound, 2.0, None, ALU.mult))
                link(vec4, nc.vector.tensor_scalar(bits, bound.bitcast(I32), 24, None, ALU.logical_shift_right))
                link(vec4, nc.vector.tensor_scalar(hidden_scale[:].bitcast(I32), bits, -float(1 << 23), float(204 << 23),
                                                   ALU.mult, ALU.add))
                link(vec4, nc.vector.reciprocal(inverse, weight_scale[:, :, 0]))
                link(vec4, nc.vector.tensor_scalar(gelu_scale[:], inverse, 1.0 / TOKEN_SCALE, None, ALU.mult))
                link(vec4, nc.vector.reciprocal(inverse, hidden_scale[:]))
                link(vec4, nc.vector.reciprocal(bound, weight_scale[:, :, 1]))
                nc.vector.tensor_tensor(y_scale[:], inverse, bound, ALU.mult).then_inc(scales_ready, 1)
            peeled(dve, attention, 0, 5, PAIRS - 1, PAIRS)

            divide, sum_squares = after_heads(PAIRS - 1)
            late_logits(PAIRS - 5)
            norm_x1(PAIRS - 3)
            divide()
            sum_squares()
            late_logits(PAIRS - 4)
            stats_x1(PAIRS - 2)
            scale_weights(E - 1, 1)
            norm_x1(PAIRS - 2)
            late_logits(PAIRS - 3)
            stats_x1(PAIRS - 1)
            norm_x1(PAIRS - 1)
            late_logits(PAIRS - 2)
            scales()
            late_logits(PAIRS - 1)

            dve.wait_ge(logits_read, PAIRS + 5)
            by_tile = lambda v: v.rearrange("p (b e) -> p b e", e=E)
            wide = lambda v: v.unsqueeze(2).broadcast_to([P, B, E])
            link(vec4, nc.vector.tensor_reduce(top, logits[:], AX_X, ALU.max))
            nc.vector.tensor_tensor(by_tile(diff), logits[:], wide(top), ALU.subtract).then_inc(diff_ready, 1)
            dve.wait_ge(diff_ready, 1)
            dve.wait_ge(numbers_ready, 1)
            link(vec4, nc.vector.tensor_scalar(key, diff, 0.0, float(E), ALU.is_lt, ALU.mult))
            link(vec4, nc.vector.tensor_tensor(key, key, expert_no, ALU.add))
            link(vec4, nc.vector.tensor_reduce(smallest, by_tile(key), AX_X, ALU.min))
            link(vec4, nc.vector.tensor_tensor(by_tile(onehot), by_tile(expert_no), wide(smallest), ALU.is_equal))
            nc.vector.tensor_copy(onehot_b, onehot).then_inc(onehot_ready, 1)
            dve.wait_ge(chance_ready, 1)
            link(vec4, nc.vector.tensor_reduce(total, by_tile(chance), AX_X, ALU.add))
            link(vec4, nc.vector.reciprocal(prob, total))
            link(vec4, nc.vector.tensor_copy(values[:, :, 1], prob))
            link(vec4, nc.vector.tensor_tensor(prob, prob, values[:, :, 1], ALU.subtract))
            link(vec4, nc.vector.tensor_copy(values[:, :, 2], prob))
            nc.vector.tensor_tensor(values[:, :, 3], prob, values[:, :, 2], ALU.subtract)
            by_expert = lambda v: v.rearrange("p (e b) -> p e b", e=E)
            wide_e = lambda v: v.unsqueeze(2).broadcast_to([P, E, B])
            dve.wait_ge(ranks_done, 1)
            nc.vector.memset(zeros128, 0.0)
            link(vec4, nc.vector.tensor_copy(by_expert(totals_et), by_tile(total_ps).rearrange("p b e -> p e b")))
            link(vec4, nc.vector.tensor_tensor_scan(scan, totals_et, zeros128, 0.0, ALU.add, ALU.add))
            link(vec4, nc.vector.tensor_tensor(inside, scan, totals_et, ALU.subtract))
            link(vec4, nc.vector.tensor_tensor(counts, by_expert(scan)[:, :, B - 1], by_expert(inside)[:, :, 0],
                                               ALU.subtract))
            link(vec4, nc.vector.tensor_tensor(by_expert(spare), by_expert(tile_edge), wide_e(counts), ALU.is_lt))
            link(vec4, nc.vector.tensor_reduce(run_tiles, by_expert(spare), AX_X, ALU.add))
            link(vec4, nc.vector.tensor_tensor_scan(run_end, run_tiles, zeros128[:, 0:E], 0.0, ALU.add, ALU.add))
            link(vec4, nc.vector.tensor_tensor(run_start, run_end, run_tiles, ALU.subtract))
            link(vec4, nc.vector.tensor_scalar(run_start, run_start, float(P), None, ALU.mult))
            link(vec4, nc.vector.tensor_tensor(run_start, run_start, by_expert(inside)[:, :, 0], ALU.subtract))
            link(vec4, nc.vector.tensor_tensor(by_expert(base_et), by_expert(inside), wide_e(run_start), ALU.add))
            link(vec4, nc.vector.tensor_tensor(by_tile(place), by_tile(rank_ps),
                                               by_expert(base_et).rearrange("p e b -> p b e"), ALU.add))
            link(vec4, nc.vector.tensor_tensor(place, place, onehot, ALU.mult))
            link(vec4, nc.vector.tensor_reduce(position, by_tile(place), AX_X, ALU.add))
            link(vec4, nc.vector.tensor_copy(position_i, position))
            link(vec4, nc.vector.tensor_scalar(position_i, position_i, P.bit_length() - 1, None,
                                               ALU.logical_shift_right))
            nc.vector.tensor_copy(tile16, position_i)
            link(vec4, nc.vector.tensor_copy(tile_f, position_i))
            nc.vector.tensor_tensor(in_tile, slot_no.unsqueeze(1).broadcast_to([P, B, TP]),
                                    tile16.unsqueeze(2).broadcast_to([P, B, TP]),
                                    ALU.is_equal).then_inc(in_tile_ready, 1)
            link(vec4, nc.vector.scalar_tensor_tensor(place16, tile_f, -float(P), position, ALU.mult, ALU.add))
            for h in range(2):
                half = slice(B // 2 * h, B // 2 * (h + 1))
                nc.vector.tensor_tensor(at_place[:, half, :], place_no.unsqueeze(1).broadcast_to([P, B // 2, P]),
                                        place16[:, half].unsqueeze(2).broadcast_to([P, B // 2, P]),
                                        ALU.is_equal).then_inc(at_place_ready, 1)
            link(vec4, nc.vector.tensor_tensor(slot_cmp, run_end.unsqueeze(1).broadcast_to([P, 32, E]), tile_no,
                                               ALU.is_le))
            link(vec4, nc.vector.tensor_reduce(tile_expert_f, slot_cmp, AX_X, ALU.add))
            nc.vector.tensor_scalar(tile_expert[:], tile_expert_f, float(E - 1), None, ALU.min)
            dve.wait_ge(chosen_done, 1)
            link(vec4, nc.vector.tensor_copy(chosen, chosen_ps))
            number = chosen[:, 0:TP]
            nc.vector.tensor_scalar(gather_u[:], number, -1.0, 0.0, ALU.add, ALU.max).then_inc(route_ready, 1)
            link(vec4, nc.vector.tensor_scalar(target_f, number, 0.5, float(NOWHERE), ALU.is_lt, ALU.mult))
            link(vec4, nc.vector.scalar_tensor_tensor(target_f, number, -1.0, target_f, ALU.add, ALU.add))
            nc.vector.tensor_copy(scatter_u[:], target_f)
            link(vec4, nc.vector.tensor_reduce(probs[:], chosen[:, TP:].rearrange("p (v s) -> p s v", v=3), AX_X,
                                               ALU.add))
            dve.wait_ge(route_ready, 1)
            dve.wait_ge(scales_ready, 1)

            def tokens(s, u):
                q = u % 2
                dve.wait_ge(row_in[u], 4 * (s - u) + 16)
                if not (isinstance(s, int) and s < 2):
                    dve.wait_ge(tokc_done, s - 1)
                nc.vector.tensor_scalar(tok16[:, q, 0:D], row_ring[:, u, :], TOKEN_SCALE, None,
                                        ALU.mult).then_inc(tok_step, 1)
                if has(s, 0, TILES - 4):
                    nc.vector.tensor_copy(gather_now[:, u:u + 1], gather_u[:, at(s + 4, 1)])
                dve.wait_ge(tok_step, s + 1)
                nc.vector.scalar_tensor_tensor(tok16[:, q, D:2 * D], row_ring[:, u, :], TOKEN_SCALE,
                                               tok16[:, q, 0:D], ALU.mult, ALU.subtract).then_inc(tok_ready, 1)

            def token_cols(s, q):
                dve.wait_ge(tokc_done, s + 1)
                if not (isinstance(s, int) and s < 2):
                    dve.wait_ge(hidden_done[1], s - 1)
                nc.vector.tensor_copy(tok_cols[:, q, :], tokc_ps[q]).then_inc(tokc_ready, 1)

            def split_hidden(s, q, e, h):
                dve.wait_ge(gelu_ready[h], s + 1)
                if not (isinstance(s, int) and s < 2):
                    dve.wait_ge(down_done[h], s - 1)
                a, b = FC * P // 2 * h, FC * P // 2 * (h + 1)
                nc.vector.tensor_scalar(hid16[:, q, a:b], hidden[:, q, a:b], hidden_scale[:, ds(e, 1)], None,
                                        ALU.mult).then_inc(hid_step[h], 1)
                dve.wait_ge(hid_step[h], s + 1)
                nc.vector.scalar_tensor_tensor(hid16[:, q, FC * P + a:FC * P + b], hidden[:, q, a:b],
                                               hidden_scale[:, ds(e, 1)], hid16[:, q, a:b],
                                               ALU.mult, ALU.subtract).then_inc(hid_ready[h], 1)

            def finish(s, u, e):
                q = u % 2
                if isinstance(s, int) and s == 0:
                    dve.wait_ge(b2_in, 16)
                dve.wait_ge(down_done[1], s + 1)
                if not (isinstance(s, int) and s < 2):
                    dve.wait_ge(y_stored[q], 16 * (s // 2))
                nc.vector.scalar_tensor_tensor(y_tile[:, q, :], y_ps[q][:, D:], y_scale[:, ds(e, 1)],
                                               b2_rows[:, ds(e, 1), :].rearrange("p a d -> p (a d)"),
                                               ALU.mult, ALU.add).then_inc(y_step[0], 1)
                nc.vector.tensor_copy(scatter_now[:, u:u + 1], scatter_u[:, at(s, 1)])
                dve.wait_ge(y_step[0], s + 1)
                nc.vector.scalar_tensor_tensor(y_tile[:, q, :], y_ps[q][:, 0:D], y_scale[:, ds(e, 1)],
                                               y_tile[:, q, :], ALU.mult, ALU.add).then_inc(y_step[1], 1)
                dve.wait_ge(y_step[1], s + 1)
                nc.vector.tensor_scalar(y_tile[:, q, :], y_tile[:, q, :], probs[:, at(s, 1)], None,
                                        ALU.mult).then_inc(y_ready, 1)

            experts = TileExperts(dve)

            def ffn(s, u):
                q = u % 2
                if has(s, 3, TILES + 3):
                    finish(s - 3, (u - 3) % 4, experts.of(u - 3))
                if has(s, 1, TILES + 1):
                    split_hidden(s - 1, 1 - q, experts.of(u - 1), 1)
                if has(s, 0, TILES - 2):
                    tokens(s + 2, (u + 2) % 4)
                if has(s, 0, TILES - 1):
                    token_cols(s + 1, 1 - q)
                if has(s, 0, TILES):
                    split_hidden(s, q, experts.load(s, u), 0)

            tokens(0, 0)
            tokens(1, 1)
            token_cols(0, 0)
            in_fours(dve, ffn, 4, TILES - 6, TILES + 3)


_INS = ['x', 'ctx_1024', 'L0_xattn_igate_kernel', 'L0_xattn_igate_bias', 'L0_xattn_fgate_kernel',
        'L0_xattn_fgate_bias', 'L0_ffn_switch_w', 'L0_ffn_switch_b', 'L0_ffn_w1', 'L0_ffn_b1', 'L0_ffn_w2',
        'L0_ffn_b2']
_OUTS = [((16, 128, 256), 'float32')]


def kernel(**inputs):
    import numpy as _np
    import concourse.bacc as _bacc
    from concourse import mybir as _mybir
    from concourse.bass_utils import run_bass_kernel_spmd as _run

    nc = _bacc.Bacc("TRN2", target_bir_lowering=False, num_devices=1)
    arrays, args = {}, []
    for name in _INS:
        a = _np.ascontiguousarray(inputs[name])
        arrays[f"in_{name}_dram"] = a
        args.append(nc.dram_tensor(f"in_{name}_dram", a.shape, _mybir.dt.from_np(a.dtype), kind="ExternalInput").ap())
    for i, (shape, dtype) in enumerate(_OUTS):
        dt = _mybir.dt.from_np(_np.dtype(dtype))
        args.append(nc.dram_tensor(f"out_{i}_dram", shape, dt, kind="ExternalOutput").ap())
    xattn_ffn_kernel(nc, *args)
    r = _run(nc, [arrays], core_ids=[0])
    got = tuple(r.results[0][f"out_{i}_dram"] for i in range(len(_OUTS)))
    return got[0]
```
